# Optimizing a Trainium2 kernel written in Bass

```python
import numpy as np
import jax
import jax.numpy as jnp

def _softmax(x, axis=-1):
    return jax.nn.softmax(x, axis=axis)

def _gelu(x):
    return jax.nn.gelu(x, approximate=True)

def _silu(x):
    return jax.nn.silu(x)

def _sigmoid(x):
    return jax.nn.sigmoid(x)

def _layernorm(x, axis=-1, eps=1e-05):
    m = jnp.mean(x, axis=axis, keepdims=True)
    v = jnp.var(x, axis=axis, keepdims=True)
    return (x - m) / jnp.sqrt(v + eps)

def _scatter_add(tgt, idx, src, axis=0):
    return tgt.at[idx].add(src)

def _segment_sum(src, seg, n):
    return jax.ops.segment_sum(src, seg, n)
kernel_name = 'mk_xattn_ffn_d1_seqx_r8_fe54a2'

def setup_inputs(seed: int=0):
    np.random.seed(seed)
    _w = jnp.asarray

    def _rec_inputs():
        import jax
        import jax.numpy as jnp
        _rk = jax.random.key(seed)
        x = -7.109e-05 + 0.9999 * jax.random.normal(jax.random.fold_in(_rk, 1), (32, 128, 128), jnp.float32)
        _lenS = 128 - jax.random.randint(jax.random.fold_in(_rk, 7), (32,), 0, max(1, 128 // 4) + 1, jnp.int32)
        _lenS2 = 128 - jax.random.randint(jax.random.fold_in(_rk, 8), (32,), 0, max(1, 128 // 4) + 1, jnp.int32)
        _ctx_768P = jax.random.normal(jax.random.fold_in(_rk, 11), (32, 16, 96), jnp.float32)
        _ctx_768c = jax.random.dirichlet(jax.random.fold_in(_rk, 511), 0.3 * jnp.ones((16,), jnp.float32), (32, 128))
        _ctx_768t = jnp.einsum('bsk,bkd->bsd', _ctx_768c, _ctx_768P)
        _ctx_768t = _ctx_768t * jax.lax.rsqrt(jnp.mean(jnp.square(_ctx_768t)) + 1e-12) * 0.953939
        ctx_768 = 0.000486113 + 1.00014 * (_ctx_768t + 0.3 * jax.random.normal(jax.random.fold_in(_rk, 611), (32, 128, 96), jnp.float32))
        return (x, ctx_768)
    x, ctx_768 = _rec_inputs()

    def _L0_xattn_setup():
        import jax, jax.numpy as jnp
        import numpy as np
        HEADS = 16
        DIM_HEAD = 64
        key = jax.random.key(seed)
        ks = jax.random.split(key, 8)
        B, S, D = (16, 512, 128)
        K, DE = (77, 96)
        inner = HEADS * DIM_HEAD
        hidden_states = jax.random.normal(ks[0], (B, S, D), dtype=jnp.float32)
        encoder_hidden_states = jax.random.normal(ks[1], (B, K, DE), dtype=jnp.float32)
        sc_q = 1.0 / np.sqrt(D)
        sc_kv = 1.0 / np.sqrt(DE)
        sc_o = 1.0 / np.sqrt(inner)
        Wq = jax.random.normal(ks[2], (D, inner), dtype=jnp.float32) * sc_q
        Wk = jax.random.normal(ks[3], (DE, inner), dtype=jnp.float32) * sc_kv
        Wv = jax.random.normal(ks[4], (DE, inner), dtype=jnp.float32) * sc_kv
        Wo = jax.random.normal(ks[5], (inner, D), dtype=jnp.float32) * sc_o
        bo = jax.random.normal(ks[6], (D,), dtype=jnp.float32) * 0.01
        return {'hidden_states': hidden_states, 'encoder_hidden_states': encoder_hidden_states, 'Wq': Wq, 'Wk': Wk, 'Wv': Wv, 'Wo': Wo, 'bo': bo}
    _L0_xattn_all = _L0_xattn_setup()
    _L0_xattn_in = {k: v for k, v in _L0_xattn_all.items() if k in ('Wq', 'Wk', 'Wv', 'Wo', 'bo')}
    del _L0_xattn_all

    def _L0_ffn_setup():
        import jax, jax.numpy as jnp
        import numpy as np
        EMB = 128
        HID = 256
        HEADS = 16
        HEAD_DIM = EMB // HEADS
        EXPERTS = 8
        TOPK = 2
        EPS = 1e-05

        def layernorm(x, scale, shift):
            mean = jnp.mean(x, axis=-1, keepdims=True)
            var = jnp.mean((x - mean) ** 2, axis=-1, keepdims=True)
            return scale * (x - mean) / jnp.sqrt(var + EPS) + shift

        def attention(x, wq, wk, wv, wo, bo):
            b, t, _ = x.shape
            q = (x @ wq).reshape(b, t, HEADS, HEAD_DIM)
            k = (x @ wk).reshape(b, t, HEADS, HEAD_DIM)
            v = (x @ wv).reshape(b, t, HEADS, HEAD_DIM)
            scores = jnp.einsum('bqhd,bkhd->bhqk', q, k)
            mask = jnp.arange(t)[:, None] < jnp.arange(t)[None, :]
            scores = jnp.where(mask, -jnp.inf, scores)
            attn = jax.nn.softmax(scores / np.sqrt(HEAD_DIM), axis=-1)
            ctx = jnp.einsum('bhqk,bkhd->bqhd', attn, v).reshape(b, t, EMB)
            return ctx @ wo + bo

        def moe_ff(x, gate_w, w1, w2, w3):
            b, t, d = x.shape
            xf = x.reshape(b * t, d)
            scores = xf @ gate_w
            topk_scores, topk_idx = jax.lax.top_k(scores, TOPK)
            topk_probs = jax.nn.softmax(topk_scores, axis=-1)
            weight = jnp.sum(jax.nn.one_hot(topk_idx, EXPERTS, dtype=xf.dtype) * topk_probs[..., None], axis=1)
            h = jax.nn.silu(jnp.einsum('td,edh->eth', xf, w1)) * jnp.einsum('td,edh->eth', xf, w2)
            out_e = jnp.einsum('eth,ehd->etd', h, w3)
            out = jnp.einsum('etd,te->td', out_e, weight)
            return out.reshape(b, t, d)
        key = jax.random.key(seed)
        ks = jax.random.split(key, 12)
        s = lambda k, shape, fan: jax.random.normal(k, shape, jnp.float32) / np.sqrt(fan)
        return {'x': jax.random.normal(ks[0], (2, 256, EMB), jnp.float32), 'ln1_scale': jnp.ones((EMB,), jnp.float32), 'ln1_shift': jnp.zeros((EMB,), jnp.float32), 'wq': s(ks[1], (EMB, EMB), EMB), 'wk': s(ks[2], (EMB, EMB), EMB), 'wv': s(ks[3], (EMB, EMB), EMB), 'wo': s(ks[4], (EMB, EMB), EMB), 'bo': jnp.zeros((EMB,), jnp.float32), 'ln2_scale': jnp.ones((EMB,), jnp.float32), 'ln2_shift': jnp.zeros((EMB,), jnp.float32), 'gate_w': s(ks[5], (EMB, EXPERTS), EMB), 'w1': s(ks[6], (EXPERTS, EMB, HID), EMB), 'w2': s(ks[7], (EXPERTS, EMB, HID), EMB), 'w3': s(ks[8], (EXPERTS, HID, EMB), HID)}
    _L0_ffn_all = _L0_ffn_setup()
    _L0_ffn_in = {k: v for k, v in _L0_ffn_all.items() if k in ('ln1_scale', 'ln1_shift', 'wq', 'wk', 'wv', 'wo', 'bo', 'ln2_scale', 'ln2_shift', 'gate_w', 'w1', 'w2', 'w3')}
    del _L0_ffn_all
    return {'x': x, 'ctx_768': ctx_768, 'L0_xattn_Wq': _L0_xattn_in['Wq'], 'L0_xattn_Wk': _L0_xattn_in['Wk'], 'L0_xattn_Wv': _L0_xattn_in['Wv'], 'L0_xattn_Wo': _L0_xattn_in['Wo'], 'L0_xattn_bo': _L0_xattn_in['bo'], 'L0_ffn_ln1_scale': _L0_ffn_in['ln1_scale'], 'L0_ffn_ln1_shift': _L0_ffn_in['ln1_shift'], 'L0_ffn_wq': _L0_ffn_in['wq'], 'L0_ffn_wk': _L0_ffn_in['wk'], 'L0_ffn_wv': _L0_ffn_in['wv'], 'L0_ffn_wo': _L0_ffn_in['wo'], 'L0_ffn_bo': _L0_ffn_in['bo'], 'L0_ffn_ln2_scale': _L0_ffn_in['ln2_scale'], 'L0_ffn_ln2_shift': _L0_ffn_in['ln2_shift'], 'L0_ffn_gate_w': _L0_ffn_in['gate_w'], 'L0_ffn_w1': _L0_ffn_in['w1'], 'L0_ffn_w2': _L0_ffn_in['w2'], 'L0_ffn_w3': _L0_ffn_in['w3']}

def reference(x, ctx_768, L0_xattn_Wq, L0_xattn_Wk, L0_xattn_Wv, L0_xattn_Wo, L0_xattn_bo, L0_ffn_ln1_scale, L0_ffn_ln1_shift, L0_ffn_wq, L0_ffn_wk, L0_ffn_wv, L0_ffn_wo, L0_ffn_bo, L0_ffn_ln2_scale, L0_ffn_ln2_shift, L0_ffn_gate_w, L0_ffn_w1, L0_ffn_w2, L0_ffn_w3):
    import jax
    import jax.numpy as jnp

    def _L0_xattn_ref(hidden_states, encoder_hidden_states, Wq, Wk, Wv, Wo, bo):
        import jax, jax.numpy as jnp
        import numpy as np
        HEADS = 16
        DIM_HEAD = 64
        B, S, D = hidden_states.shape
        K = encoder_hidden_states.shape[1]
        H, Dh = (HEADS, DIM_HEAD)
        scale = 1.0 / np.sqrt(Dh)
        q = hidden_states @ Wq
        k = encoder_hidden_states @ Wk
        v = encoder_hidden_states @ Wv
        q = q.reshape(B, S, H, Dh).transpose(0, 2, 1, 3)
        k = k.reshape(B, K, H, Dh).transpose(0, 2, 1, 3)
        v = v.reshape(B, K, H, Dh).transpose(0, 2, 1, 3)
        scores = jnp.einsum('bhsd,bhkd->bhsk', q, k) * scale
        probs = jax.nn.softmax(scores, axis=-1)
        out = jnp.einsum('bhsk,bhkd->bhsd', probs, v)
        out = out.transpose(0, 2, 1, 3).reshape(B, S, H * Dh)
        out = out @ Wo + bo
        return out

    def _L0_ffn_ref(x, ln1_scale, ln1_shift, wq, wk, wv, wo, bo, ln2_scale, ln2_shift, gate_w, w1, w2, w3):
        import jax, jax.numpy as jnp
        import numpy as np
        EMB = 128
        HID = 256
        HEADS = 16
        HEAD_DIM = EMB // HEADS
        EXPERTS = 8
        TOPK = 2
        EPS = 1e-05

        def layernorm(x, scale, shift):
            mean = jnp.mean(x, axis=-1, keepdims=True)
            var = jnp.mean((x - mean) ** 2, axis=-1, keepdims=True)
            return scale * (x - mean) / jnp.sqrt(var + EPS) + shift

        def attention(x, wq, wk, wv, wo, bo):
            b, t, _ = x.shape
            q = (x @ wq).reshape(b, t, HEADS, HEAD_DIM)
            k = (x @ wk).reshape(b, t, HEADS, HEAD_DIM)
            v = (x @ wv).reshape(b, t, HEADS, HEAD_DIM)
            scores = jnp.einsum('bqhd,bkhd->bhqk', q, k)
            mask = jnp.arange(t)[:, None] < jnp.arange(t)[None, :]
            scores = jnp.where(mask, -jnp.inf, scores)
            attn = jax.nn.softmax(scores / np.sqrt(HEAD_DIM), axis=-1)
            ctx = jnp.einsum('bhqk,bkhd->bqhd', attn, v).reshape(b, t, EMB)
            return ctx @ wo + bo

        def moe_ff(x, gate_w, w1, w2, w3):
            b, t, d = x.shape
            xf = x.reshape(b * t, d)
            scores = xf @ gate_w
            topk_scores, topk_idx = jax.lax.top_k(scores, TOPK)
            topk_probs = jax.nn.softmax(topk_scores, axis=-1)
            weight = jnp.sum(jax.nn.one_hot(topk_idx, EXPERTS, dtype=xf.dtype) * topk_probs[..., None], axis=1)
            h = jax.nn.silu(jnp.einsum('td,edh->eth', xf, w1)) * jnp.einsum('td,edh->eth', xf, w2)
            out_e = jnp.einsum('eth,ehd->etd', h, w3)
            out = jnp.einsum('etd,te->td', out_e, weight)
            return out.reshape(b, t, d)
        h = layernorm(x, ln1_scale, ln1_shift)
        x = x + attention(h, wq, wk, wv, wo, bo)
        h = layernorm(x, ln2_scale, ln2_shift)
        x = x + moe_ff(h, gate_w, w1, w2, w3)
        return x
    x = x + _L0_xattn_ref(_layernorm(x, axis=-1), ctx_768, L0_xattn_Wq, L0_xattn_Wk, L0_xattn_Wv, L0_xattn_Wo, L0_xattn_bo)
    x = x + _L0_ffn_ref(_layernorm(x, axis=-1), L0_ffn_ln1_scale, L0_ffn_ln1_shift, L0_ffn_wq, L0_ffn_wk, L0_ffn_wv, L0_ffn_wo, L0_ffn_bo, L0_ffn_ln2_scale, L0_ffn_ln2_shift, L0_ffn_gate_w, L0_ffn_w1, L0_ffn_w2, L0_ffn_w3)
    return x

_drawn_inputs = setup_inputs


def setup_inputs(seed=0):
    import zlib

    import numpy as np

    out = dict(_drawn_inputs(seed))
    spreads = {'L0_ffn_ln1_scale': (1.0, 0.2),
     'L0_ffn_ln1_shift': (0.0, 0.1),
     'L0_ffn_bo': (0.0, 0.1),
     'L0_ffn_ln2_scale': (1.0, 0.2),
     'L0_ffn_ln2_shift': (0.0, 0.1)}
    factors = {'L0_xattn_bo': 2.912}
    for name, (base, spread) in spreads.items():
        noise = np.random.default_rng([zlib.crc32(name.encode()), seed]).standard_normal(out[name].shape)
        drawn = base * np.exp(spread * noise) if base else spread * noise
        out[name] = jnp.asarray(drawn.astype(out[name].dtype))
    for name, factor in factors.items():
        out[name] = (out[name] * factor).astype(out[name].dtype)
    return out
```

```python
from contextlib import ExitStack

import concourse.bass as bass
import concourse.mybir as mybir
from concourse.alu_op_type import AluOpType as ALU

ACT = mybir.ActivationFunctionType
F32 = mybir.dt.float32
F32R = mybir.dt.float32r
F16 = mybir.dt.float16
BF16 = mybir.dt.bfloat16
U32 = mybir.dt.uint32
AX = mybir.AxisListType.X

P = 128
NB = 4
T = NB * P
STEPS = 16
HEADS = 16
Q4 = 4
DE = 96
DH = 64
EB = 8
EXPERTS = 8
CHUNKS = 16
EPS = 1e-5
P_SCALE = 16384.0
MASKED = -1.0e30

B_SLOTS = {6: (0, 2), 7: (2, 2), 8: (4, 2), 9: (6, 2), 10: (8, 2), 11: (10, 3), 12: (13, 3), 13: (16, 2)}
SLOT_GAPS = {2: ((0, 1), (3, 4)), 3: ((0, 1), (2, 3), (4, 5))}
B_OUT_T = {9: (0,), 11: (1,), 13: (2, 3)}
B_OUT_W = {10: (0,), 12: (1,), 14: (2, 3)}
FIRST_LOOP, LAST_LOOP = 2, 6


def b_scores(s, k):
    if s in B_SLOTS:
        w0, n = B_SLOTS[s]
        for i, (g, _) in enumerate(SLOT_GAPS[n]):
            if g == k and w0 + i < STEPS:
                return w0 + i
    return None


def b_values(s, k):
    if s in B_SLOTS:
        w0, n = B_SLOTS[s]
        for i, (_, g) in enumerate(SLOT_GAPS[n]):
            if g == k:
                return w0 + i
    return None


def m_chunk(s, k):
    gaps = {0: 0, 1: 1, 3: 2, 5: 3}
    return 4 * s + gaps[k] if s < 4 and k in gaps else None


def m_down(s, k):
    if s < 4 and k == 2 and s > 0:
        return 2 * s - 1
    if s < 4 and k == 4:
        return 2 * s
    return EXPERTS - 1 if (s, k) == (4, 0) else None


def build(nc, n_groups, x, ctx, Wq, Wk, Wv, Wo, bo_a, ln1_s, ln1_b, wq, wk, wv, wo, bo_b,
          ln2_s, ln2_b, gate_w, w1, w2, w3, out):
    NG = n_groups
    x_v = x.rearrange("(g b) s d -> g s b d", b=NB)
    ctx_v = ctx.rearrange("(g b) s d -> g s b d", b=NB)
    out_v = out.rearrange("(g b) s d -> g s b d", b=NB)

    def live(it, d=0):
        return not isinstance(it, int) or 0 <= it + d < NG

    def wait(eng, sem, it, per, n):
        v = it * per + n
        if not isinstance(it, int) or v > 0:
            eng.wait_ge(sem, v)

    def use1(it, s):
        v = live(it) if s + 1 < STEPS else live(it, 1)
        o = live(it) if s >= 2 else live(it, -1)
        return v or o

    def wo_a(it, s):
        return live(it) if s >= 2 else live(it, -1)

    def act_use2(it, s):
        return (s >= 8 and live(it, 1)) or (s in B_OUT_T and live(it, -1))

    def dve_use2(it, s):
        return (s >= 8 and live(it, 1)) or wo_a(it, s) or (s in B_OUT_W and live(it, -1))

    def use2(it, s):
        return act_use2(it, s) or dve_use2(it, s)

    def through(present, it, s):
        back = 0
        if s < 0:
            s, back = s + STEPS, 1
        if isinstance(it, int):
            it -= back
            return sum(bool(present(i, t)) for i in range(-1, it + 1) for t in range(STEPS) if i < it or t <= s)
        mid = FIRST_LOOP + 1
        per = sum(bool(present(mid, t)) for t in range(STEPS))
        before = through(present, FIRST_LOOP - 1, STEPS - 1)
        here = sum(bool(present(mid, t)) for t in range(s + 1))
        return it * per + (before - (FIRST_LOOP + back) * per + here)

    def wait_use(eng, sem, present, it, s):
        v = through(present, it, s)
        if not isinstance(it, int) or v > 0:
            eng.wait_ge(sem, v)

    def iterations(eng, body):
        for it in range(-1, FIRST_LOOP):
            body(it)
        with eng.Fori(FIRST_LOOP, LAST_LOOP + 1) as it:
            body(it)
        for it in range(LAST_LOOP + 1, NG + 2):
            body(it)

    es = ExitStack()
    with es:
        def sb(name, shape, dt=F32):
            return es.enter_context(nc.sbuf_tensor(name, shape, dt))

        def at(name, shape, dt, offset):
            return nc.alloc_sbuf_tensor_at(name, shape, dt, offset=offset)

        def sem(name):
            return es.enter_context(nc.semaphore(name))

        ident = sb("ident", [P, P])
        ident_b = sb("ident_b", [P, P], BF16)
        mask = sb("mask", [P, Q4, P], BF16)
        half = sb("half", [P, 1])
        eps = sb("eps", [P, 1])
        iota8 = sb("iota8", [P, EXPERTS])
        mt_hi = sb("mt_hi", [DE, HEADS, P], F32R)
        mt_lo = sb("mt_lo", [DE, HEADS, P], F32R)
        wv_hi = sb("wv_hi", [DE, HEADS * DH], F32R)
        wv_lo = sb("wv_lo", [DE, HEADS * DH], F32R)
        wo_sb = sb("wo_sb", [P, 8, P])
        bo_a_sb = sb("bo_a_sb", [P, P])
        bo_b_sb = sb("bo_b_sb", [P, P])
        ln_sb = sb("ln_sb", [P, 4])
        qkw_hi = sb("qkw_hi", [P, 2, P], F32R)
        qkw_lo = sb("qkw_lo", [P, 2, P], F32R)
        vw_sb = sb("vw_sb", [P, P])
        ow_sb = sb("ow_sb", [P, P])
        gate_sb = sb("gate_sb", [P, EXPERTS])
        sel_q = sb("sel_q", [P, 16 + HEADS * 32], F32R)
        sel_k = sb("sel_k", [P, 16 + HEADS * 32], F32R)
        w1_hi = sb("w1_hi", [P, CHUNKS * P], F32R)
        w1_lo = sb("w1_lo", [P, CHUNKS * P], F32R)
        w2_hi = sb("w2_hi", [P, CHUNKS * P], F32R)
        w2_lo = sb("w2_lo", [P, CHUNKS * P], F32R)
        w3_sb = sb("w3_sb", [P, CHUNKS, P])

        x_in = sb("x_in", [P, NB, P])
        x_res = sb("x_res", [P, NB, P])
        ctx_in = sb("ctx_in", [P, NB, DE])
        ctxn_hi = sb("ctxn_hi", [DE, T], F32R)
        ctxn_lo = sb("ctxn_lo", [DE, T], F32R)
        ctxc_hi = sb("ctxc_hi", [DE, T], F32R)
        ctxc_lo = sb("ctxc_lo", [DE, T], F32R)
        ha = sb("ha", [P, 2, P])
        hat_hi = sb("hat_hi", [P, NB, P], F32R)
        hat_lo = sb("hat_lo", [P, NB, P], F32R)
        g_hi = sb("g_hi", [P, 2, Q4, T], F32R)
        g_lo = sb("g_lo", [P, 2, Q4, T], F32R)
        v_a = sb("v_a", [P, 4, Q4, DH + 1])
        nmax_a = sb("nmax_a", [P, 2, Q4])
        p_a = sb("p_a", [P, 2, Q4, P])
        pt_a = sb("pt_a", [P, Q4, P])
        rden_a = sb("rden_a", [P, 2, Q4])
        o_a = sb("o_a", [P, 2, Q4 * DH])
        ot_a = sb("ot_a", [P, 2, 2, P])
        mv_a = sb("mv_a", [P, NB, 2])
        st_a = sb("st_a", [P, NB, 6])
        ve_a = sb("ve_a", [P, NB])
        rs_a = sb("rs_a", [P, NB])

        y_b = sb("y_b", [P, 2, P])
        yb_res = sb("yb_res", [P, NB, P])
        xy_sum = sb("xy_sum", [P, NB, P])
        acc = sb("acc", [P, NB, P])
        nrm = sb("nrm", [P, NB, P])
        st_b = sb("st_b", [P, NB, 6])
        mv_b = sb("mv_b", [P, 3, NB, 2])
        ve_b = sb("ve_b", [P, 3, NB])
        rs_b = sb("rs_b", [P, 3, NB])
        k_diag = sb("k_diag", [P, 2, Q4, Q4, P], F32R)
        moe_in = at("moe_in", [P, 2, CHUNKS * P], F32, nc.sbuf_base - 16 * 1024)
        v_b = sb("v_b", [P, NB, HEADS, 26], BF16)
        nmax_b = sb("nmax_b", [P, 2, Q4])
        p_b = sb("p_b", [P, 2, Q4, P])
        pt_hi = sb("pt_hi", [P, Q4, P], F16)
        pt_lo = sb("pt_lo", [P, Q4, P], F16)
        red_b = sb("red_b", [P, P])
        rden_b = sb("rden_b", [P, HEADS])
        o_b = sb("o_b", [P, 2, P])
        ot_b = sb("ot_b", [P, 2, P])
        sc_m = sb("sc_m", [P, NB, EXPERTS])
        m8 = sb("m8", [P, NB, 8])
        i8 = sb("i8", [P, NB, 8], U32)
        if_m = sb("if_m", [P, NB, 2])
        dd = sb("dd", [P, NB])
        ee = sb("ee", [P, NB])
        zz = sb("zz", [P, NB])
        rr = sb("rr", [P, NB])
        pp = sb("pp", [P, 2, NB])
        eq = sb("eq", [P, 2, NB, EXPERTS])
        wts = sb("wts", [P, NB, EXPERTS])

        KB = 1024
        arena = sb("arena", [P, 24 * KB // 4])
        a0 = nc.sbuf_base - 24 * KB
        q_stk = at("q_stk", [P, Q4, T], F32R, a0)
        g_t = at("g_t", [P, 4, T], F32, a0)
        k_stk = at("k_stk", [P, Q4, T], F32R, a0 + 8 * KB)
        hb_f = at("hb_f", [P, T], F32, a0 + 8 * KB)
        hb_hi = at("hb_hi", [P, T], F32R, a0 + 10 * KB)
        hb_lo = at("hb_lo", [P, T], F32R, a0 + 12 * KB)
        hm_f = at("hm_f", [P, T], F32, a0 + 8 * KB)
        th_m = at("th_m", [P, 2, T], F32, a0 + 10 * KB)
        v_rest = at("v_rest", [P, T], F32, a0 + 14 * KB)
        u_m = at("u_m", [P, T], F32, a0 + 14 * KB)
        qk_hi = at("qk_hi", [P, 2, T], F32R, a0 + 16 * KB)
        qk_lo = at("qk_lo", [P, 2, T], F32R, a0 + 20 * KB)
        hm_hi = at("hm_hi", [P, T], F32R, a0 + 16 * KB)
        hm_lo = at("hm_lo", [P, T], F32R, a0 + 18 * KB)
        wq_in = at("wq_in", [P, HEADS * DH], F32, a0)
        wk_in = at("wk_in", [DE, HEADS * DH], F32, a0 + 4 * KB)
        wv_in = at("wv_in", [DE, HEADS * DH], F32, a0 + 8 * KB)
        wqt = at("wqt", [P, 8, P], F32, a0 + 12 * KB)
        wkt = at("wkt", [P, 8, DE], F32, a0 + 16 * KB)
        qkw_in = at("qkw_in", [P, 2, P], F32, a0 + 19 * KB)
        sel_tmp = at("sel_tmp", [P, 16 + HEADS * 32], F32, a0 + 20 * KB)

        ps = {n: es.enter_context(nc.psum_tensor(f"ps_{n}", [P, 512], F32))
              for n in ("sa", "ta", "ga", "oa", "x", "sb", "tb", "ob")}
        sa, ta, ga, oa, px, psb, tb, ob = (ps[n] for n in ("sa", "ta", "ga", "oa", "x", "sb", "tb", "ob"))

        w_attn_in = sem("w_attn_in")
        w_small_in = sem("w_small_in")
        w_moe_in = sem("w_moe_in")
        w3_in = sem("w3_in")
        x_landed = sem("x_landed")
        ctx_landed = sem("ctx_landed")
        k_placed = [sem(f"k_placed{i}") for i in range(2)]
        out_stored = sem("out_stored")
        const_made = sem("const_made")
        sel_made = sem("sel_made")
        wt_done = sem("wt_done")
        wqt_done = sem("wqt_done")
        wkt_done = sem("wkt_done")
        m_done = sem("m_done")
        mth_done = sem("mth_done")
        mtl_done = sem("mtl_done")
        wvh_done = sem("wvh_done")
        wvl_done = sem("wvl_done")
        qkwh_done = sem("qkwh_done")
        qkwl_done = sem("qkwl_done")
        moew_done = sem("moew_done")
        ones_done = sem("ones_done")

        sa_done = sem("sa_done")
        ta_done = sem("ta_done")
        ga_done = sem("ga_done")
        oa_done = sem("oa_done")
        x1_done = sem("x1_done")
        x2_done = sem("x2_done")
        maxa_done = sem("maxa_done")
        expa_done = sem("expa_done")
        pta_done = sem("pta_done")
        gh_done = sem("gh_done")
        gl_done = sem("gl_done")
        va_done = sem("va_done")
        ota_done = sem("ota_done")
        rdena_done = sem("rdena_done")
        oa_norm = sem("oa_norm")
        x2_act = sem("x2_act")
        x2_free = sem("x2_free")
        sta_done = sem("sta_done")
        mva_done = sem("mva_done")
        vea_done = sem("vea_done")
        rsa_done = sem("rsa_done")
        ha_done = sem("ha_done")
        xres_set = sem("xres_set")
        ctxc_done = sem("ctxc_done")

        st_done = [sem(f"st{i}_done") for i in range(3)]
        mv_done = [sem(f"mv{i}_done") for i in range(3)]
        ve_done = [sem(f"ve{i}_done") for i in range(3)]
        rs_done = [sem(f"rs{i}_done") for i in range(3)]
        y_done = sem("y_done")
        ybo_done = sem("ybo_done")
        sum_done = sem("sum_done")
        nb_done = sem("nb_done")
        nm_done = sem("nm_done")
        hbt_done = sem("hbt_done")
        hbf_done = sem("hbf_done")
        hbh_done = sem("hbh_done")
        hbl_done = sem("hbl_done")
        qk_done = sem("qk_done")
        qkh_done = sem("qkh_done")
        qkl_done = sem("qkl_done")
        vb_done = sem("vb_done")
        v1_done = sem("v1_done")
        vr_done = sem("vr_done")
        v2_done = sem("v2_done")
        v3_done = sem("v3_done")
        stk_done = sem("stk_done")
        qs_done = sem("qs_done")
        ks_done = sem("ks_done")
        sb_done = sem("sb_done")
        tb_done = sem("tb_done")
        ob_done = sem("ob_done")
        maxb_done = sem("maxb_done")
        expb_done = sem("expb_done")
        ph_done = sem("ph_done")
        pl_done = sem("pl_done")
        redb_done = sem("redb_done")
        ob_free = sem("ob_free")
        ob_norm = sem("ob_norm")
        y1_done = sem("y1_done")
        acc_set = sem("acc_set")

        hmt_done = sem("hmt_done")
        hmf_done = sem("hmf_done")
        hmh_done = sem("hmh_done")
        hml_done = sem("hml_done")
        gate_done = sem("gate_done")
        sc_done = sem("sc_done")
        route = sem("route")
        dd_done = sem("dd_done")
        ee_done = sem("ee_done")
        ma_done = sem("ma_done")
        mb_done = sem("mb_done")
        th_done = sem("th_done")
        u_done = sem("u_done")
        g_done = sem("g_done")
        dn_done = sem("dn_done")
        comb_done = sem("comb_done")
        ROUTE = 10

        block = es.enter_context(nc.Block())

        def f32(ap):
            return ap.bitcast(F32)

        def tok(b):
            return slice(b * P, (b + 1) * P)

        @block.sync
        def _(sp):
            sp.dma_start(wq_in[:], Wq).then_inc(w_attn_in, 16)
            sp.dma_start(wk_in[:], Wk).then_inc(w_attn_in, 16)
            sp.dma_start(ctx_in[:], ctx_v[0]).then_inc(ctx_landed, 16)
            sp.dma_start(x_in[:], x_v[0]).then_inc(x_landed, 16)
            sp.dma_start(wv_in[:], Wv).then_inc(w_attn_in, 16)
            sp.dma_start(wo_sb[:], Wo.rearrange("(t p) d -> p t d", p=P)).then_inc(w_small_in, 16)
            for dst, src in ((bo_a_sb, bo_a), (bo_b_sb, bo_b)):
                sp.dma_start(dst[:], src.rearrange("(a d) -> a d", a=1).to_broadcast([P, P])).then_inc(w_small_in, 16)
            for i, src in enumerate((ln1_s, ln1_b, ln2_s, ln2_b)):
                sp.dma_start(ln_sb[:, i:i + 1], src.rearrange("(d a) -> d a", a=1)).then_inc(w_small_in, 16)
            for dst, src in ((qkw_in[:, 0, :], wq), (qkw_in[:, 1, :], wk), (vw_sb[:], wv), (ow_sb[:], wo),
                             (gate_sb[:], gate_w)):
                sp.dma_start(dst, src).then_inc(w_small_in, 16)
            for i, src in enumerate((w1, w2)):
                sp.dma_start(moe_in[:, i, :].rearrange("d (e h) -> d e h", e=EXPERTS),
                             src.rearrange("e d h -> d e h")).then_inc(w_moe_in, 16)
            sp.dma_start(w3_sb[:], w3.rearrange("e (c p) d -> p (e c) d", p=P)).then_inc(w3_in, 16)

            def body(it):
                if live(it, 1) and not (isinstance(it, int) and it < 0):
                    wait_use(sp, x2_done, use2, it, -5)
                    sp.dma_start(ctx_in[:], ctx_v[it + 1]).then_inc(ctx_landed, 16)
                    wait(sp, xres_set, it, NB, NB)
                    wait(sp, ha_done, it, NB, NB)
                    sp.dma_start(x_in[:], x_v[it + 1]).then_inc(x_landed, 16)
                if live(it, -2):
                    wait(sp, comb_done, it - 2, EXPERTS, EXPERTS)
                    sp.dma_start(out_v[it - 2], acc[:]).then_inc(out_stored, 16)
                if live(it, -1):
                    wait(sp, ks_done, it - 1, Q4, Q4)
                    for b in range(NB):
                        wait(sp, sb_done, it - 1, STEPS, Q4 * (b - 1))
                        for hh in range(Q4):
                            r = slice(32 * hh, 32 * hh + 32)
                            sp.dma_start(f32(k_diag[r, b % 2, :, hh, :]), f32(k_stk[r, :, tok(b)])).then_inc(k_placed[b % 2], 16)

            iterations(sp, body)
            sp.wait_ge(out_stored, 16 * NG)

        @block.tensor
        def _(pe):
            def split3(dst, l_hi, l_lo, r_hi, r_lo):
                pe.matmul(dst, l_hi, r_hi, start=True, stop=False)
                pe.matmul(dst, l_hi, r_lo, start=False, stop=False)
                return pe.matmul(dst, l_lo, r_hi, start=False, stop=True)

            pe.wait_ge(const_made, 2)
            pe.wait_ge(w_attn_in, 48)
            for t in range(8):
                pe.transpose((sa if t < 4 else ta)[:, tok(t % 4)], wq_in[:, tok(t)], ident[:])
            for t in range(8):
                mm = pe.transpose((ga if t < 4 else oa)[:, (t % 4) * DE:(t % 4 + 1) * DE], wk_in[:, tok(t)],
                                  ident[0:DE, 0:DE])
            mm.then_inc(wt_done, 1)
            pe.wait_ge(wqt_done, 2)
            pe.wait_ge(wkt_done, 2)
            for h in range(HEADS):
                r = slice(64 * (h % 2), 64 * (h % 2) + 64)
                bank = (psb, tb, ob, px)[2 * (h // 8) + h % 2]
                mm = pe.matmul(bank[0:DE, tok(h % 8 // 2)], wkt[r, h // 2, :], wqt[r, h // 2, :], start=True, stop=True)
            mm.then_inc(m_done, 1)

            def scores_a(it, u):
                hq, b = divmod(u, NB)
                if b == 0:
                    wait(pe, gl_done, it, HEADS, Q4 * hq + Q4)
                if hq == 0:
                    wait_use(pe, x2_free, use2, it, b - 4)
                wait(pe, expa_done, it, STEPS, u)
                g = [t[:, hq % 2, :, tok(b)] for t in (g_hi, g_lo)]
                split3(sa[:].rearrange("q (h k) -> q h k", h=Q4), hat_hi[:, b, :], hat_lo[:, b, :], *g).then_inc(sa_done, 1)

            def transposes_a(it, u):
                wait(pe, expa_done, it, STEPS, u + 1)
                wait(pe, pta_done, it, STEPS, u)
                for h in range(Q4):
                    mm = pe.transpose(ta[:, tok(h)], p_a[:, u % 2, h, :], ident[:])
                mm.then_inc(ta_done, 1)

            def keys_a(it, s):
                j = (s + Q4) % HEADS
                if s == 12:
                    wait_use(pe, x2_free, use2, it, 11)
                if s == 4:
                    wait(pe, ctxc_done, it, 2, 2)
                wait(pe, gl_done, it, HEADS, s + Q4)
                c = (ctxc_hi, ctxc_lo) if 4 <= s < 12 else (ctxn_hi, ctxn_lo)
                split3(ga[:], mt_hi[:, j, :], mt_lo[:, j, :], c[0][:], c[1][:]).then_inc(ga_done, 1)

            def values_and_output_t_a(it, s):
                if not use1(it, s):
                    return
                wait_use(pe, x2_free, use2, it, s - 1)
                if isinstance(it, int) and it == 0 and s in (1, 2):
                    pe.wait_ge(va_done, s + 1)
                mm = None
                if live(it) if s + 1 < STEPS else live(it, 1):
                    hq, b = divmod((s + 1) % STEPS, NB)
                    c = (ctxc_hi, ctxc_lo) if 4 <= s < 15 else (ctxn_hi, ctxn_lo)
                    w = slice(hq * Q4 * DH, (hq + 1) * Q4 * DH)
                    mm = split3(px[:, 0:Q4 * DH], c[0][:, tok(b)], c[1][:, tok(b)], wv_hi[:, w], wv_lo[:, w])
                if wo_a(it, s):
                    wait(pe, oa_norm, it, STEPS, s - 1)
                    for i in range(2):
                        mm = pe.transpose(px[:, tok(2 + i)], o_a[:, s % 2, tok(i)], ident[:])
                mm.then_inc(x1_done, 1)

            def context_a(it, u):
                wait(pe, pta_done, it, STEPS, u + 1)
                wait(pe, va_done, it, STEPS, u + 1)
                wait(pe, oa_norm, it, STEPS, u)
                for h in range(Q4):
                    mm = pe.matmul(oa[:, h * (DH + 1):(h + 1) * (DH + 1)], pt_a[:, h, :], v_a[:, u % 4, h, :],
                                   start=True, stop=True)
                mm.then_inc(oa_done, 1)

            def second_use(it, s):
                if not use2(it, s):
                    return
                if use1(it, s):
                    wait(pe, va_done, it, STEPS, min(s + 2, NG * STEPS if not isinstance(it, int) else NG * STEPS - it * STEPS))
                    if wo_a(it, s):
                        wait(pe, ota_done, it, STEPS, s - 1)
                else:
                    wait_use(pe, x2_free, use2, it, s - 1)
                mm = None
                if 8 <= s < 12 and live(it, 1):
                    if s == 8:
                        wait(pe, ctx_landed, it + 1, 16, 16)
                    mm = pe.transpose(px[0:DE, tok(1)], ctx_in[:, s - 8, :], ident[:])
                if s >= 12 and live(it, 1):
                    wait(pe, ha_done, it + 1, NB, s - 12 + 1)
                    mm = pe.transpose(px[:, tok(1)], ha[:, s % 2, :], ident[:])
                if live(it, -1):
                    for i, b in enumerate(B_OUT_T.get(s, ())):
                        wait(pe, ob_norm, it - 1, NB, b + 1)
                        mm = pe.transpose(px[:, tok(2 + i)], o_b[:, b % 2, :], ident[:])
                    for i, b in enumerate(B_OUT_W.get(s, ())):
                        mm = pe.matmul(px[:, tok(2 + i)], ot_b[:, b % 2, :], ow_sb[:], start=True, stop=True)
                if wo_a(it, s):
                    hq = (s - 2) % STEPS // NB
                    for i in range(2):
                        mm = pe.matmul(px[:, tok(0)], ot_a[:, s % 2, i, :], wo_sb[:, 2 * hq + i, :],
                                       start=(i == 0), stop=(i == 1))
                mm.then_inc(x2_done, 1)

            def project_b(it, s, k):
                if (s, k) == (4, 1):
                    wait(pe, nb_done, it - 1, NB, NB)
                    wait(pe, g_done, it - 1, CHUNKS, 0)
                    for b in range(NB):
                        mm = pe.transpose(tb[:, tok(b)], nrm[:, b, :], ident[:])
                    mm.then_inc(hbt_done, 1)
                if (s, k) == (4, 3):
                    wait(pe, hbl_done, it - 1, 1, 1)
                    wait(pe, u_done, it - 1, CHUNKS, 0)
                    wait(pe, comb_done, it - 1, EXPERTS, 0)
                    for i, bank in enumerate((psb, ob)):
                        split3(bank[:], qkw_hi[:, i, :], qkw_lo[:, i, :], hb_hi[:], hb_lo[:]).then_inc(qk_done, 1)
                if (s, k) == (4, 4):
                    for b in range(NB):
                        mm = pe.matmul(tb[:, tok(b)], hb_f[:, tok(b)], vw_sb[:], start=True, stop=True)
                    mm.then_inc(vb_done, 1)
                if s == 5 and k < 4:
                    for i in (2 * k, 2 * k + 1):
                        side, sel = i % 2, (sel_q, sel_k)[i % 2]
                        bank = (psb, ob, tb)[i % 3]
                        if i < 2:
                            wait(pe, qkl_done, it - 1, 2, i + 1)
                        elif i == 2:
                            wait(pe, vr_done, it - 1, 1, 1)
                        elif i % 2:
                            wait(pe, qs_done, it - 1, Q4, (i - 3) // 2 + 1)
                        else:
                            wait(pe, ks_done, it - 1, Q4, (i - 3) // 2 + 1)
                        c0, shift = 16 + P * k, (16, 8)[side]
                        pe.matmul(bank[:], sel[:, c0:c0 + P], qk_hi[:, side, :], start=True, stop=False)
                        pe.matmul(bank[:], sel[:, c0 - shift:c0 - shift + P], qk_lo[:, side, :],
                                  start=False, stop=True).then_inc(stk_done, 1)

            def unit_b(it, s, k):
                w = b_scores(s, k)
                if w is not None:
                    b, t = divmod(w, Q4)
                    if w == 0:
                        wait(pe, qs_done, it - 1, Q4, Q4)
                    if t == 0:
                        wait(pe, k_placed[b % 2], it - 1, 128, 64 * (b // 2 + 1))
                    wait(pe, expb_done, it - 1, STEPS, w)
                    pe.matmul(psb[:], ident_b[:], mask[:], start=True, stop=False)
                    pe.matmul(psb[:].rearrange("q (h k) -> q h k", h=Q4), q_stk[:, t, tok(b)],
                              k_diag[:, b % 2, t, :, :], start=False, stop=True).then_inc(sb_done, 1)
                v = b_values(s, k)
                if v is None:
                    return
                if 1 <= v <= STEPS:
                    wait(pe, expb_done, it - 1, STEPS, v)
                    if v == 1:
                        wait(pe, ks_done, it - 1, Q4, Q4)
                    wait(pe, pl_done, it - 1, STEPS, v - 1)
                    for h in range(Q4):
                        mm = pe.transpose(tb[:, tok(h)], p_b[:, (v - 1) % 2, h, :], ident[:])
                    mm.then_inc(tb_done, 1)
                if 2 <= v <= STEPS + 1:
                    b, t = divmod(v - 2, Q4)
                    if v - 2 == 0:
                        wait(pe, v3_done, it - 1, 1, 1)
                    if t == 0:
                        wait(pe, ob_free, it - 1, NB, b)
                    wait(pe, pl_done, it - 1, STEPS, v - 1)
                    for h in range(Q4):
                        c = 25 * (Q4 * t + h)
                        vals = v_b[:, b, Q4 * t + h, 0:25]
                        pe.matmul(ob[:, c:c + 25], pt_hi[:, h, :], vals, start=True, stop=False)
                        mm = pe.matmul(ob[:, c:c + 25], pt_lo[:, h, :], vals, start=False, stop=True)
                    mm.then_inc(ob_done, 1)

            def start_m(it, s, k):
                if (s, k) == (15, 2):
                    wait(pe, nm_done, it - 1, NB, NB)
                    wait(pe, pl_done, it - 1, STEPS, STEPS)
                    for b in range(NB):
                        mm = pe.transpose(tb[:, tok(b)], nrm[:, b, :], ident[:])
                    mm.then_inc(hmt_done, 1)
                if (s, k) == (15, 4):
                    wait(pe, hmf_done, it - 1, 1, 1)
                    wait(pe, ob_free, it - 1, NB, NB)
                    for b in range(NB):
                        mm = pe.matmul(ob[:, b * EXPERTS:(b + 1) * EXPERTS], hm_f[:, tok(b)], gate_sb[:],
                                       start=True, stop=True)
                    mm.then_inc(gate_done, 1)

            def expert_m(it, s, k):
                j = m_chunk(s, k)
                if j is not None:
                    if j == 0:
                        wait(pe, hml_done, it - 2, 1, 1)
                        wait(pe, expb_done, it - 2, STEPS, STEPS)
                    else:
                        wait(pe, u_done, it - 2, CHUNKS, j)
                    w = slice(j * P, (j + 1) * P)
                    split3(psb[:], w1_hi[:, w], w1_lo[:, w], hm_hi[:], hm_lo[:]).then_inc(ma_done, 1)
                    if j:
                        wait(pe, g_done, it - 2, CHUNKS, j)
                    split3(tb[:], w2_hi[:, w], w2_lo[:, w], hm_hi[:], hm_lo[:]).then_inc(mb_done, 1)
                e = m_down(s, k)
                if e is not None:
                    if e == 0:
                        wait(pe, sc_done, it - 2, 1, 1)
                    else:
                        wait(pe, comb_done, it - 2, EXPERTS, e)
                    wait(pe, g_done, it - 2, CHUNKS, 2 * e + 2)
                    for b in range(NB):
                        for i in range(2):
                            mm = pe.matmul(ob[:, tok(b)], g_t[:, (2 * e + i) % 4, tok(b)], w3_sb[:, 2 * e + i, :],
                                           start=(i == 0), stop=(i == 1))
                    mm.then_inc(dn_done, 1)

            def gap(it, s, k):
                if live(it, -2):
                    expert_m(it, s, k)
                if live(it, -1):
                    project_b(it, s, k)
                    unit_b(it, s, k)
                    start_m(it, s, k)

            def body(it):
                if isinstance(it, int) and it == -1:
                    pe.wait_ge(mtl_done, 4)
                    pe.wait_ge(wvl_done, 1)
                    pe.wait_ge(w_small_in, 16 * 12)
                if isinstance(it, int) and it == 1:
                    pe.wait_ge(qkwl_done, 1)
                    pe.wait_ge(sel_made, 2)
                    pe.wait_ge(moew_done, 5)
                    pe.wait_ge(w3_in, 16)
                for s in range(STEPS):
                    if live(it):
                        scores_a(it, s)
                    gap(it, s, 0)
                    if live(it, 0 if s else -1):
                        transposes_a(it if s else it - 1, (s - 1) % STEPS)
                    gap(it, s, 1)
                    if live(it, 0 if s < 12 else 1):
                        keys_a(it, s)
                    gap(it, s, 2)
                    values_and_output_t_a(it, s)
                    gap(it, s, 3)
                    if live(it, 0 if s else -1):
                        context_a(it if s else it - 1, (s - 1) % STEPS)
                    gap(it, s, 4)
                    second_use(it, s)
                    gap(it, s, 5)

            iterations(pe, body)

        @block.scalar
        def _(act):
            act.wait_ge(wt_done, 1)
            for i, bank in enumerate((sa, ta)):
                act.activation(wqt[:, 4 * i:4 * i + 4, :], bank[:].rearrange("p (t c) -> p t c", t=4),
                               ACT.Copy).then_inc(wqt_done, 1)
            act.activation(wv_hi[:], wv_in[:], ACT.Copy).then_inc(wvh_done, 1)
            act.wait_ge(m_done, 1)
            for i, bank in enumerate((psb, tb, ob, px)):
                h0 = 8 * (i // 2) + i % 2
                act.activation(mt_hi[:, h0:h0 + 7:2, :], bank[0:DE, :].rearrange("p (t c) -> p t c", t=4),
                               ACT.Copy, scale=DH ** -0.5).then_inc(mth_done, 1)
            act.wait_ge(w_small_in, 16 * 12)
            act.activation(qkw_hi[:], qkw_in[:], ACT.Copy).then_inc(qkwh_done, 1)

            def exp_a(it, u):
                wait(act, maxa_done, it, STEPS, u + 1)
                wait(act, ta_done, it, STEPS, u - 1)
                for h in range(Q4):
                    a = act.activation(p_a[:, u % 2, h, :], sa[:, tok(h)], ACT.Exp, bias=nmax_a[:, u % 2, h:h + 1])
                a.then_inc(expa_done, 1)

            def pt_copy_a(it, u):
                wait(act, ta_done, it, STEPS, u + 1)
                wait(act, oa_done, it, STEPS, u)
                act.activation(pt_a[:], ta[:].rearrange("p (h q) -> p h q", h=Q4), ACT.Copy).then_inc(pta_done, 1)

            def keys_hi_a(it, s):
                j = (s + Q4) % HEADS
                wait(act, ga_done, it, HEADS, s + Q4 + 1)
                act.activation(g_hi[:, j // Q4 % 2, j % Q4, :], ga[:], ACT.Copy).then_inc(gh_done, 1)

            def first_use(it, s):
                if not use1(it, s):
                    return
                wait_use(act, x1_done, use1, it, s)
                if live(it) if s + 1 < STEPS else live(it, 1):
                    act.activation(v_a[:, (s + 1) % 4, :, 0:DH], px[:, 0:Q4 * DH].rearrange("p (h d) -> p h d", h=Q4),
                                   ACT.Copy).then_inc(va_done, 1)
                if wo_a(it, s):
                    act.activation(ot_a[:, s % 2, :, :], px[:, 2 * P:4 * P].rearrange("p (i q) -> p i q", i=2),
                                   ACT.Copy).then_inc(ota_done, 1)

            def second_use(it, s):
                if not act_use2(it, s):
                    return
                wait_use(act, x2_done, use2, it, s)
                a = None
                if 8 <= s < 12 and live(it, 1):
                    if s == 8:
                        wait(act, ctxc_done, it, 2, 2)
                    a = act.activation(ctxn_hi[:, tok(s - 8)], px[0:DE, tok(1)], ACT.Copy)
                if s >= 12 and live(it, 1):
                    a = act.activation(hat_hi[:, s - 12, :], px[:, tok(1)], ACT.Copy)
                if live(it, -1):
                    for i, b in enumerate(B_OUT_T.get(s, ())):
                        a = act.activation(ot_b[:, b % 2, :], px[:, tok(2 + i)], ACT.Copy)
                a.then_inc(x2_act if dve_use2(it, s) else x2_free, 1)

            def project_b(it, s, k):
                if (s, k) == (4, 1):
                    wait(act, hbt_done, it - 1, 1, 1)
                    act.activation(hb_f[:], tb[:], ACT.Identity, bias=ln_sb[:, 1:2], scale=ln_sb[:, 0:1]).then_inc(hbf_done, 1)
                    wait(act, hbf_done, it - 1, 1, 1)
                    act.activation(hb_hi[:], hb_f[:], ACT.Copy).then_inc(hbh_done, 1)
                if (s, k) == (4, 3):
                    for i, bank in enumerate((psb, ob)):
                        wait(act, qk_done, it - 1, 2, i + 1)
                        act.activation(qk_hi[:, i, :], bank[:], ACT.Copy, scale=(EB ** -0.5, 1.0)[i]).then_inc(qkh_done, 1)
                if (s, k) == (4, 4):
                    wait(act, vb_done, it - 1, 1, 1)
                    act.activation(v_b[:, :, :, 0:EB], tb[:].rearrange("p (b h d) -> p b h d", b=NB, h=HEADS),
                                   ACT.Copy).then_inc(v1_done, 1)
                if s == 5 and k < 4:
                    wait(act, stk_done, it - 1, 8, 2 * k + 1)
                    act.activation(q_stk[:, k, :], (psb, ob, tb)[2 * k % 3][:], ACT.Copy).then_inc(qs_done, 1)

            def unit_b(it, s, k):
                w = b_scores(s, k)
                if w is not None:
                    wait(act, maxb_done, it - 1, STEPS, w + 1)
                    wait(act, tb_done, it - 1, STEPS, w - 1)
                    for h in range(Q4):
                        a = act.activation(p_b[:, w % 2, h, :], psb[:, tok(h)], ACT.Exp, bias=nmax_b[:, w % 2, h:h + 1])
                    a.then_inc(expb_done, 1)
                v = b_values(s, k)
                if v is not None and 1 <= v <= STEPS:
                    wait(act, tb_done, it - 1, STEPS, v)
                    wait(act, ob_done, it - 1, STEPS, v - 1)
                    act.activation(pt_hi[:], tb[:].rearrange("p (h q) -> p h q", h=Q4), ACT.Copy,
                                   scale=P_SCALE).then_inc(ph_done, 1)

            def start_m(it, s, k):
                if (s, k) == (15, 2):
                    wait(act, hmt_done, it - 1, 1, 1)
                    act.activation(hm_f[:], tb[:], ACT.Identity, bias=ln_sb[:, 3:4], scale=ln_sb[:, 2:3]).then_inc(hmf_done, 1)
                    wait(act, hmf_done, it - 1, 1, 1)
                    act.activation(hm_hi[:], hm_f[:], ACT.Copy).then_inc(hmh_done, 1)
                if (s, k) == (15, 5):
                    wait(act, dd_done, it - 1, 1, 1)
                    act.activation(ee[:], dd[:], ACT.Exp).then_inc(ee_done, 1)

            def expert_m(it, s, k):
                j = m_chunk(s, k)
                if j is not None:
                    wait(act, ma_done, it - 2, CHUNKS, j + 1)
                    if j >= 2:
                        wait(act, u_done, it - 2, CHUNKS, j - 1)
                    act.activation(th_m[:, j % 2, :], psb[:], ACT.Tanh, scale=0.5).then_inc(th_done, 1)

            def gap(it, s, k):
                if live(it, -2):
                    expert_m(it, s, k)
                if live(it, -1):
                    project_b(it, s, k)
                    unit_b(it, s, k)
                    start_m(it, s, k)

            def body(it):
                for s in range(STEPS):
                    if live(it):
                        exp_a(it, s)
                    if live(it, 0 if s else -1):
                        pt_copy_a(it if s else it - 1, (s - 1) % STEPS)
                    gap(it, s, 0)
                    gap(it, s, 1)
                    if live(it, 0 if s < 12 else 1):
                        keys_hi_a(it, s)
                    gap(it, s, 2)
                    first_use(it, s)
                    gap(it, s, 3)
                    gap(it, s, 4)
                    second_use(it, s)
                    gap(it, s, 5)

            iterations(act, body)

        @block.vector
        def _(dve):
            dve.memset(v_a[:, :, :, DH:DH + 1], 1.0).then_inc(ones_done, 1)
            dve.memset(v_b[:, :, :, 24:25], 1.0).then_inc(ones_done, 1)
            dve.wait_ge(wt_done, 1)
            for i, bank in enumerate((ga, oa)):
                dve.tensor_copy(wkt[:, 4 * i:4 * i + 4, :],
                                bank[:, 0:4 * DE].rearrange("p (t c) -> p t c", t=4)).then_inc(wkt_done, 1)
            dve.wait_ge(wvh_done, 1)
            dve.tensor_tensor(wv_lo[:], wv_in[:], f32(wv_hi[:]), ALU.subtract).then_inc(wvl_done, 1)
            for i, bank in enumerate((psb, tb, ob, px)):
                h0 = 8 * (i // 2) + i % 2
                dve.wait_ge(mth_done, i + 1)
                dve.scalar_tensor_tensor(out=mt_lo[:, h0:h0 + 7:2, :], in0=bank[0:DE, :].rearrange("p (t c) -> p t c", t=4),
                                         scalar=DH ** -0.5, in1=f32(mt_hi[:, h0:h0 + 7:2, :]),
                                         op0=ALU.mult, op1=ALU.subtract).then_inc(mtl_done, 1)
            dve.wait_ge(qkwh_done, 1)
            dve.tensor_tensor(qkw_lo[:], qkw_in[:], f32(qkw_hi[:]), ALU.subtract).then_inc(qkwl_done, 1)

            def max_a(it, u):
                wait(dve, sa_done, it, STEPS, u + 1)
                dve.tensor_reduce(nmax_a[:, u % 2, :], sa[:].rearrange("q (h k) -> q h k", h=Q4), AX, ALU.max,
                                  negate=True).then_inc(maxa_done, 1)

            def keys_lo_a(it, s):
                j = (s + Q4) % HEADS
                wait(dve, gh_done, it, HEADS, s + Q4 + 1)
                dve.tensor_tensor(g_lo[:, j // Q4 % 2, j % Q4, :], ga[:], f32(g_hi[:, j // Q4 % 2, j % Q4, :]),
                                  ALU.subtract).then_inc(gl_done, 1)

            def normalise_a(it, u):
                wait(dve, oa_done, it, STEPS, u + 1)
                o = oa[:, 0:Q4 * (DH + 1)].rearrange("q (h d) -> q h d", h=Q4)
                dve.reciprocal(rden_a[:, u % 2, :], o[:, :, DH]).then_inc(rdena_done, 1)
                wait(dve, rdena_done, it, STEPS, u + 1)
                dve.tensor_tensor(o_a[:, u % 2, :].rearrange("q (h d) -> q h d", h=Q4), o[:, :, 0:DH],
                                  rden_a[:, u % 2, :].unsqueeze(2).to_broadcast([P, Q4, DH]),
                                  ALU.mult).then_inc(oa_norm, 1)

            def norm_stats(it, i, b, src):
                dve.bn_stats(st_b[:, b, :], src).then_inc(st_done[i], 1)
                wait(dve, st_done[i], it, NB, b + 1)
                dve.nop(nofuse=True)
                dve.bn_aggr(mv_b[:, i, b, :], st_b[:, b, :]).then_inc(mv_done[i], 1)

            def norm_apply(it, i, b, dst, src):
                wait(dve, rs_done[i], it, NB, b + 1)
                return dve.tensor_scalar(dst, src, mv_b[:, i, b, 0:1], rs_b[:, i, b:b + 1], ALU.subtract, ALU.mult)

            def second_use(it, s):
                if dve_use2(it, s):
                    wait_use(dve, x2_done, use2, it, s)
                    if act_use2(it, s):
                        wait_use(dve, x2_act, lambda i, t: act_use2(i, t) and dve_use2(i, t), it, s)
                    d = None
                    if 8 <= s < 12 and live(it, 1):
                        d = dve.tensor_tensor(ctxn_lo[:, tok(s - 8)], px[0:DE, tok(1)], f32(ctxn_hi[:, tok(s - 8)]),
                                              ALU.subtract)
                    if s >= 12 and live(it, 1):
                        d = dve.tensor_tensor(hat_lo[:, s - 12, :], px[:, tok(1)], f32(hat_hi[:, s - 12, :]), ALU.subtract)
                    if live(it, -1):
                        for i, b in enumerate(B_OUT_W.get(s, ())):
                            wait(dve, sum_done, it - 1, NB, b + 1)
                            wait(dve, out_stored, it - 1, 16, 0)
                            dve.tensor_tensor(yb_res[:, b, :], px[:, tok(2 + i)], yb_res[:, b, :], ALU.add).then_inc(y1_done, 1)
                            d = dve.tensor_tensor(acc[:, b, :], px[:, tok(2 + i)], xy_sum[:, b, :], ALU.add)
                            if wo_a(it, s) or i + 1 < len(B_OUT_W[s]):
                                d.then_inc(acc_set, 1)
                                d = None
                    if wo_a(it, s):
                        g, u = (it, s - 2) if s >= 2 else (it - 1, s + 14)
                        b = u % NB
                        wait(dve, xres_set, g, NB, b + 1)
                        d = dve.tensor_tensor(x_res[:, b, :], px[:, tok(0)], x_res[:, b, :], ALU.add)
                    d.then_inc(x2_free, 1)
                if live(it, -1):
                    for b in B_OUT_W.get(s, ()):
                        wait(dve, y1_done, it - 1, NB, b + 1)
                        norm_stats(it - 1, 2, b, yb_res[:, b, :])
                g, b = (it, s - 14) if s >= 14 else (it - 1, s + 2)
                if (s >= 14 or s < 2) and live(g):
                    wait_use(dve, x2_free, use2, it, s)
                    norm_stats(g, 0, b, x_res[:, b, :])

            def norms_b(it, s):
                g, b = (it, 0) if s == 15 else (it - 1, s + 1)
                if (s == 15 or s < 3) and live(g):
                    wait(dve, nb_done, g, NB, b - 1)
                    wait(dve, ybo_done, g, NB, b - 1)
                    norm_apply(g, 0, b, y_b[:, b % 2, :], x_res[:, b, :]).then_inc(y_done, 1)
                    wait(dve, y_done, g, NB, b + 1)
                    norm_stats(g, 1, b, y_b[:, b % 2, :])
                if s < 4 and live(it, -1):
                    norm_apply(it - 1, 1, s, nrm[:, s, :], y_b[:, s % 2, :]).then_inc(nb_done, 1)

            def norms_m(it, s):
                if live(it, -1):
                    for b in B_OUT_W.get(s - 1, ()):
                        norm_apply(it - 1, 2, b, nrm[:, b, :], yb_res[:, b, :]).then_inc(nm_done, 1)

            def norm_next_a(it, s):
                if not live(it, 1):
                    return
                if s == 9:
                    wait(dve, x_landed, it + 1, 16, 16)
                    for b in range(NB):
                        dve.bn_stats(st_a[:, b, :], x_in[:, b, :]).then_inc(sta_done, 1)
                    wait(dve, sta_done, it + 1, NB, NB)
                    dve.nop(nofuse=True)
                    for b in range(NB):
                        dve.bn_aggr(mv_a[:, b, :], st_a[:, b, :]).then_inc(mva_done, 1)
                if 11 <= s < 15:
                    b = s - 11
                    wait(dve, rsa_done, it + 1, 1, 1)
                    dve.tensor_scalar(ha[:, b % 2, :], x_in[:, b, :], mv_a[:, b, 0:1], rs_a[:, b:b + 1],
                                      ALU.subtract, ALU.mult).then_inc(ha_done, 1)

            def project_b(it, s, k):
                if (s, k) == (4, 1):
                    wait(dve, hbh_done, it - 1, 1, 1)
                    dve.tensor_tensor(hb_lo[:], hb_f[:], f32(hb_hi[:]), ALU.subtract).then_inc(hbl_done, 1)
                if (s, k) == (4, 3):
                    for i, bank in enumerate((psb, ob)):
                        wait(dve, qkh_done, it - 1, 2, i + 1)
                        dve.scalar_tensor_tensor(out=qk_lo[:, i, :], in0=bank[:], scalar=(EB ** -0.5, 1.0)[i],
                                                 in1=f32(qk_hi[:, i, :]), op0=ALU.mult, op1=ALU.subtract).then_inc(qkl_done, 1)
                if (s, k) == (4, 4):
                    def heads(t):
                        return t.rearrange("p (b h d) -> p b h d", b=NB, h=HEADS)
                    wait(dve, v1_done, it - 1, 1, 1)
                    dve.tensor_tensor(heads(v_rest[:]), heads(tb[:]), v_b[:, :, :, 0:8], ALU.subtract).then_inc(vr_done, 1)
                    wait(dve, vr_done, it - 1, 1, 1)
                    dve.tensor_copy(v_b[:, :, :, 8:16], heads(v_rest[:])).then_inc(v2_done, 1)
                    wait(dve, v2_done, it - 1, 1, 1)
                    dve.tensor_tensor(v_b[:, :, :, 16:24], heads(v_rest[:]), v_b[:, :, :, 8:16], ALU.subtract).then_inc(v3_done, 1)
                if s == 5 and k < 4:
                    wait(dve, stk_done, it - 1, 8, 2 * k + 2)
                    if k == 0:
                        for i in range(2):
                            wait(dve, k_placed[i], it - 1, 128, 0)
                    if k == 3:
                        wait(dve, v3_done, it - 1, 1, 1)
                    dve.tensor_copy(k_stk[:, k, :], (psb, ob, tb)[(2 * k + 1) % 3][:]).then_inc(ks_done, 1)

            def unit_b(it, s, k):
                w = b_scores(s, k)
                if w is not None:
                    wait(dve, sb_done, it - 1, STEPS, w + 1)
                    dve.tensor_reduce(nmax_b[:, w % 2, :], psb[:].rearrange("q (h k) -> q h k", h=Q4), AX, ALU.max,
                                      negate=True).then_inc(maxb_done, 1)
                v = b_values(s, k)
                if v is None:
                    return
                if 1 <= v <= STEPS:
                    wait(dve, ph_done, it - 1, STEPS, v)
                    dve.scalar_tensor_tensor(out=pt_lo[:], in0=tb[:].rearrange("p (h q) -> p h q", h=Q4), scalar=P_SCALE,
                                             in1=pt_hi[:], op0=ALU.mult, op1=ALU.subtract).then_inc(pl_done, 1)
                if v >= 2 and (v - 2) % Q4 == Q4 - 1:
                    b = (v - 2) // Q4
                    wait(dve, ob_done, it - 1, STEPS, v - 1)
                    o = ob[:, 0:25 * HEADS].rearrange("q (h c) -> q h c", h=HEADS)
                    dve.tensor_reduce(red_b[:].rearrange("q (h d) -> q h d", h=HEADS),
                                      o[:, :, 0:24].rearrange("q h (c d) -> q h d c", c=3), AX, ALU.add).then_inc(redb_done, 1)
                    dve.reciprocal(rden_b[:], o[:, :, 24]).then_inc(ob_free, 1)
                    wait(dve, redb_done, it - 1, NB, b + 1)
                    wait(dve, ob_free, it - 1, NB, b + 1)
                    dve.tensor_tensor(o_b[:, b % 2, :].rearrange("q (h d) -> q h d", h=HEADS),
                                      red_b[:].rearrange("q (h d) -> q h d", h=HEADS),
                                      rden_b[:].unsqueeze(2).to_broadcast([P, HEADS, EB]), ALU.mult).then_inc(ob_norm, 1)

            def start_m(it, s, k):
                if (s, k) == (15, 2):
                    wait(dve, hmh_done, it - 1, 1, 1)
                    dve.tensor_tensor(hm_lo[:], hm_f[:], f32(hm_hi[:]), ALU.subtract).then_inc(hml_done, 1)
                if (s, k) == (15, 4):
                    wait(dve, gate_done, it - 1, 1, 1)
                    dve.tensor_copy(sc_m[:], ob[:, 0:NB * EXPERTS].rearrange("q (b e) -> q b e", b=NB)).then_inc(sc_done, 1)
                    wait(dve, sc_done, it - 1, 1, 1)
                    dve.nop(nofuse=True)
                    for b in range(NB):
                        d = dve.max(m8[:, b, :], sc_m[:, b, :])
                    d.then_inc(route, 1)
                    wait(dve, route, it - 1, ROUTE, 1)
                    dve.tensor_tensor(dd[:], m8[:, :, 1], m8[:, :, 0], ALU.subtract).then_inc(dd_done, 1)
                    for b in range(NB):
                        d = dve.max_index(i8[:, b, :], m8[:, b, :], sc_m[:, b, :])
                    d.then_inc(route, 1)
                    wait(dve, route, it - 1, ROUTE, 2)
                    dve.tensor_copy(if_m[:], i8[:, :, 0:2]).then_inc(route, 1)
                    wait(dve, route, it - 1, ROUTE, 3)
                    for i in range(2):
                        dve.tensor_tensor(eq[:, i], iota8[:].unsqueeze(1).to_broadcast([P, NB, EXPERTS]),
                                          if_m[:, :, i:i + 1].to_broadcast([P, NB, EXPERTS]), ALU.is_equal).then_inc(route, 1)
                if (s, k) == (15, 5):
                    wait(dve, ee_done, it - 1, 1, 1)
                    dve.tensor_scalar(zz[:], ee[:], 1.0, None, ALU.add).then_inc(route, 1)
                    wait(dve, route, it - 1, ROUTE, 6)
                    dve.reciprocal(rr[:], zz[:]).then_inc(route, 1)
                    wait(dve, route, it - 1, ROUTE, 7)
                    dve.tensor_scalar(pp[:, 0, :], rr[:], 0.5, None, ALU.mult)
                    dve.scalar_tensor_tensor(out=pp[:, 1, :], in0=rr[:], scalar=0.5, in1=ee[:], op0=ALU.mult,
                                             op1=ALU.mult).then_inc(route, 1)
                    wait(dve, route, it - 1, ROUTE, 8)
                    for i in range(2):
                        d = dve.tensor_tensor(eq[:, i], eq[:, i], pp[:, i, :].unsqueeze(2).to_broadcast([P, NB, EXPERTS]), ALU.mult)
                    d.then_inc(route, 1)
                    wait(dve, route, it - 1, ROUTE, 9)
                    dve.tensor_tensor(wts[:], eq[:, 0], eq[:, 1], ALU.add).then_inc(route, 1)

            def expert_m(it, s, k):
                j = m_chunk(s, k)
                if j is not None:
                    wait(dve, th_done, it - 2, CHUNKS, j + 1)
                    if j:
                        wait(dve, g_done, it - 2, CHUNKS, j)
                    dve.scalar_tensor_tensor(out=u_m[:], in0=th_m[:, j % 2, :], scalar=1.0, in1=psb[:], op0=ALU.add,
                                             op1=ALU.mult).then_inc(u_done, 1)
                    wait(dve, u_done, it - 2, CHUNKS, j + 1)
                    wait(dve, mb_done, it - 2, CHUNKS, j + 1)
                    if j >= 4:
                        wait(dve, dn_done, it - 2, EXPERTS, j // 2 - 1)
                    dve.tensor_tensor(g_t[:, j % 4, :], tb[:], u_m[:], ALU.mult).then_inc(g_done, 1)
                e = m_down(s, k)
                if e is not None:
                    wait(dve, dn_done, it - 2, EXPERTS, e + 1)
                    if e == 0:
                        wait(dve, route, it - 2, ROUTE, ROUTE)
                    if e:
                        wait(dve, comb_done, it - 2, EXPERTS, e)
                    for b in range(NB):
                        d = dve.scalar_tensor_tensor(out=acc[:, b, :], in0=ob[:, tok(b)], scalar=wts[:, b, e:e + 1],
                                                     in1=acc[:, b, :], op0=ALU.mult, op1=ALU.add)
                    d.then_inc(comb_done, 1)

            def gap(it, s, k):
                if live(it, -2):
                    expert_m(it, s, k)
                if live(it, -1):
                    project_b(it, s, k)
                    unit_b(it, s, k)
                    start_m(it, s, k)

            def body(it):
                for s in range(STEPS):
                    if live(it):
                        max_a(it, s)
                    norms_b(it, s)
                    gap(it, s, 0)
                    norms_m(it, s)
                    gap(it, s, 1)
                    if live(it, 0 if s < 12 else 1):
                        keys_lo_a(it, s)
                    gap(it, s, 2)
                    norm_next_a(it, s)
                    gap(it, s, 3)
                    if live(it, 0 if s else -1):
                        normalise_a(it if s else it - 1, (s - 1) % STEPS)
                    gap(it, s, 4)
                    second_use(it, s)
                    gap(it, s, 5)

            iterations(dve, body)

        @block.gpsimd
        def _(pool):
            pool.memset(ident[:], 0.0)
            pool.memset(ident_b[:], 0.0)
            pool.memset(mask[:], 0.0)
            pool.memset(half[:], -0.5)
            pool.memset(eps[:], EPS)
            pool.memset(sel_tmp[:], 0.0).then_inc(const_made, 1)
            pool.wait_ge(const_made, 1)
            pool.affine_select(out=ident[:], in_=ident[:], compare_op=ALU.not_equal, fill=1.0, base=0,
                               pattern=[[-1, P]], channel_multiplier=1).then_inc(const_made, 1)
            pool.affine_select(out=ident_b[:], in_=ident_b[:], compare_op=ALU.not_equal, fill=1.0, base=0,
                               pattern=[[-1, P]], channel_multiplier=1)
            pool.affine_select(out=mask[:], in_=mask[:], compare_op=ALU.is_ge, fill=MASKED, base=0,
                               pattern=[[0, Q4], [-1, P]], channel_multiplier=1)
            pool.iota(iota8[:], pattern=[[1, EXPERTS]], base=0, channel_multiplier=0,
                      allow_small_or_imprecise_dtypes=True)
            body_cols = sel_tmp[:, 16:].rearrange("p (h c d) -> p h c d", h=HEADS, c=4)
            for sel, n, picks in ((sel_q, 0, (0, 1)), (sel_k, 1, (0, 2))):
                if n:
                    pool.wait_ge(sel_made, 1)
                    pool.memset(sel_tmp[:], 0.0).then_inc(const_made, 1)
                    pool.wait_ge(const_made, 5)
                for c in picks:
                    d = pool.affine_select(out=body_cols[:, :, c, :], in_=body_cols[:, :, c, :], compare_op=ALU.not_equal,
                                           fill=1.0, base=0, pattern=[[-8, HEADS], [-1, 8]], channel_multiplier=1)
                    d.then_inc(const_made, 1)
                pool.wait_ge(const_made, (4, 7)[n])
                pool.tensor_copy(sel[:], sel_tmp[:]).then_inc(sel_made, 1)
            pool.wait_ge(w_moe_in, 32)
            for i, hi in enumerate((w1_hi, w2_hi)):
                pool.tensor_copy(hi[:], moe_in[:, i, :]).then_inc(moew_done, 1)
            for i, (hi, lo) in enumerate(((w1_hi, w1_lo), (w2_hi, w2_lo))):
                pool.wait_ge(moew_done, i + 1)
                pool.tensor_tensor(lo[:], moe_in[:, i, :], f32(hi[:]), ALU.subtract).then_inc(moew_done, 1)
            pool.wait_ge(moew_done, 4)
            pool.memset(f32(k_diag[:]), 0.0).then_inc(moew_done, 1)

            def root(g, i, b):
                wait(pool, mv_done[i], g, NB, b + 1)
                pool.tensor_tensor(ve_b[:, i, b:b + 1], mv_b[:, i, b, 1:2], eps[:], ALU.add).then_inc(ve_done[i], 1)
                wait(pool, ve_done[i], g, NB, b + 1)
                pool.tensor_tensor(rs_b[:, i, b:b + 1], ve_b[:, i, b:b + 1], half[:], ALU.pow).then_inc(rs_done[i], 1)

            def body(it):
                for s in range(STEPS):
                    g, b = (it, 0) if s == 15 else (it - 1, s + 1)
                    if (s == 15 or s < 3) and live(g):
                        root(g, 1, b)
                        wait(pool, nm_done, g - 1, NB, b + 1)
                        pool.tensor_tensor(yb_res[:, b, :], y_b[:, b % 2, :], bo_b_sb[:], ALU.add).then_inc(ybo_done, 1)
                        wait(pool, ybo_done, g, NB, b + 1)
                        pool.tensor_tensor(xy_sum[:, b, :], yb_res[:, b, :], x_res[:, b, :], ALU.add).then_inc(sum_done, 1)
                    if s < 4 and live(it):
                        if s == 0 and isinstance(it, int) and it == 0:
                            pool.wait_ge(w_small_in, 16 * 12)
                        wait(pool, x_landed, it, 16, 16)
                        if live(it, -1):
                            wait(pool, sum_done, it - 1, NB, s + 1)
                        pool.tensor_tensor(x_res[:, s, :], x_in[:, s, :], bo_a_sb[:], ALU.add).then_inc(xres_set, 1)
                    if s == 9 and live(it, 1):
                        wait(pool, mva_done, it + 1, NB, NB)
                        pool.tensor_tensor(ve_a[:], mv_a[:, :, 1], eps[:].to_broadcast([P, NB]), ALU.add).then_inc(vea_done, 1)
                        wait(pool, vea_done, it + 1, 1, 1)
                        pool.tensor_tensor(rs_a[:], ve_a[:], half[:].to_broadcast([P, NB]), ALU.pow).then_inc(rsa_done, 1)
                    if live(it, -1):
                        for bb in B_OUT_W.get(s, ()):
                            root(it - 1, 2, bb)
                    g, b = (it, s - 14) if s >= 14 else (it - 1, s + 2)
                    if (s >= 14 or s < 2) and live(g):
                        root(g, 0, b)
                    if s == 15 and live(it, 1):
                        wait_use(pool, x1_done, use1, it, 14)
                        wait_use(pool, x2_free, use2, it, 11)
                        pool.nop(nofuse=True)
                        for dst, src in ((ctxc_hi, ctxn_hi), (ctxc_lo, ctxn_lo)):
                            pool.tensor_copy(dst[:], src[:]).then_inc(ctxc_done, 1)

            iterations(pool, body)


_INS = ("x", "ctx_768", "L0_xattn_Wq", "L0_xattn_Wk", "L0_xattn_Wv", "L0_xattn_Wo", "L0_xattn_bo", "L0_ffn_ln1_scale",
        "L0_ffn_ln1_shift", "L0_ffn_wq", "L0_ffn_wk", "L0_ffn_wv", "L0_ffn_wo", "L0_ffn_bo", "L0_ffn_ln2_scale",
        "L0_ffn_ln2_shift", "L0_ffn_gate_w", "L0_ffn_w1", "L0_ffn_w2", "L0_ffn_w3")


def kernel(**inputs):
    import numpy as np
    import concourse.bacc as bacc
    from concourse.bass_utils import run_bass_kernel_spmd

    nc = bacc.Bacc("TRN2", target_bir_lowering=False, num_devices=1)
    arrays, args = {}, []
    for name in _INS:
        a = np.ascontiguousarray(inputs[name])
        arrays[f"in_{name}"] = a
        args.append(nc.dram_tensor(f"in_{name}", a.shape, mybir.dt.from_np(a.dtype), kind="ExternalInput").ap())
    shape = inputs["x"].shape
    out = nc.dram_tensor("out_0", shape, F32, kind="ExternalOutput").ap()
    build(nc, shape[0] // NB, *args, out)
    r = run_bass_kernel_spmd(nc, [arrays], core_ids=[0])
    return r.results[0]["out_0"]
```

```python
from contextlib import ExitStack

import concourse.bass as bass
import concourse.mybir as mybir
from concourse.alu_op_type import AluOpType as ALU

ACT = mybir.ActivationFunctionType
F32 = mybir.dt.float32
F32R = mybir.dt.float32r
F16 = mybir.dt.float16
BF16 = mybir.dt.bfloat16
U32 = mybir.dt.uint32
AX = mybir.AxisListType.X

P = 128
NB = 4
T = NB * P
STEPS = 16
HEADS = 16
Q4 = 4
DE = 96
DH = 64
EB = 8
EXPERTS = 8
CHUNKS = 16
EPS = 1e-5
P_SCALE = 16384.0
MASKED = -1.0e30

B_SLOTS = {6: (1, 4), 7: (0, 2, 4), 8: (1, 2, 4), 9: (1, 3), 10: (1, 3), 11: (1, 3), 12: (1, 3), 13: (1, 2, 3)}
M_CHUNKS = (0, 1, 3, 4)
M_DOWNS = ((1, False), (3, True))
HBT_GAP, QK_GAP, V_GAP = (4, 1), (4, 3), (4, 4)
HMT_GAP, GATE_GAP, EE_GAP, PROBS_GAP = (14, 4), (15, 0), (15, 1), (15, 3)
V_PARTS_GAP = (6, 0)
STACK_GAPS = ((4, 5), (5, 1), (5, 2), (5, 4))
B_OUT_T = {9: (0,), 11: (1,)}
B_OUT_W = {10: (0,), 12: (1,)}
LAST_T_GAP, LAST_W_GAP = (13, 5), (14, 0)
B_NORMS = {11: (0,), 13: (1,), 14: (2, 3)}
FIRST_LOOP, LAST_LOOP = 2, 6


def b_slot(s, k):
    if k not in B_SLOTS.get(s, ()):
        return None
    return sum(len(B_SLOTS[t]) for t in B_SLOTS if t < s) + B_SLOTS[s].index(k)


def b_bank(w):
    for s, gaps in B_SLOTS.items():
        if w < len(gaps):
            return w % 2
        w -= len(gaps)


def b_before(w):
    return max([v + 1 for v in range(w) if b_bank(v) == b_bank(w)], default=0)


def b_before_a(s):
    w0 = sum(len(B_SLOTS[t]) for t in B_SLOTS if t < s - 1)
    return max([w + 1 for w in range(w0, min(w0 + len(B_SLOTS.get(s - 1, ())), STEPS)) if b_bank(w)], default=0)


def m_chunk(s, k):
    return 4 * s + M_CHUNKS.index(k) if s < 4 and k in M_CHUNKS else None


def m_down(s, k, after):
    for i, place in enumerate(M_DOWNS):
        e = 2 * s - 1 + i
        if place == (k, after) and 0 <= e < EXPERTS:
            return e
    return None


def build(nc, n_groups, x, ctx, Wq, Wk, Wv, Wo, bo_a, ln1_s, ln1_b, wq, wk, wv, wo, bo_b,
          ln2_s, ln2_b, gate_w, w1, w2, w3, out):
    NG = n_groups
    x_v = x.rearrange("(g b) s d -> g s b d", b=NB)
    ctx_v = ctx.rearrange("(g b) s d -> g s b d", b=NB)
    out_v = out.rearrange("(g b) s d -> g s b d", b=NB)

    def live(it, d=0):
        return not isinstance(it, int) or 0 <= it + d < NG

    def wait(eng, sem, it, per, n):
        v = it * per + n
        if not isinstance(it, int) or v > 0:
            eng.wait_ge(sem, v)

    def use1(it, s):
        v = live(it) if s + 1 < STEPS else live(it, 1)
        o = live(it) if s >= 2 else live(it, -1)
        return v or o

    def wo_a(it, s):
        return live(it) if s >= 2 else live(it, -1)

    def act_use2(it, s):
        return (s >= 8 and live(it, 1)) or (s in B_OUT_T and live(it, -1))

    def dve_use2(it, s):
        return (s >= 8 and live(it, 1)) or wo_a(it, s) or (s in B_OUT_W and live(it, -1))

    def use2(it, s):
        return act_use2(it, s) or dve_use2(it, s)

    def through(present, it, s):
        back = 0
        if s < 0:
            s, back = s + STEPS, 1
        if isinstance(it, int):
            it -= back
            return sum(bool(present(i, t)) for i in range(-1, it + 1) for t in range(STEPS) if i < it or t <= s)
        mid = FIRST_LOOP + 1
        per = sum(bool(present(mid, t)) for t in range(STEPS))
        before = through(present, FIRST_LOOP - 1, STEPS - 1)
        here = sum(bool(present(mid, t)) for t in range(s + 1))
        return it * per + (before - (FIRST_LOOP + back) * per + here)

    def wait_use(eng, sem, present, it, s):
        v = through(present, it, s)
        if not isinstance(it, int) or v > 0:
            eng.wait_ge(sem, v)

    def iterations(eng, body):
        for it in range(-1, FIRST_LOOP):
            body(it)
        with eng.Fori(FIRST_LOOP, LAST_LOOP + 1) as it:
            body(it)
        for it in range(LAST_LOOP + 1, NG + 2):
            body(it)

    es = ExitStack()
    with es:
        def sb(name, shape, dt=F32):
            return es.enter_context(nc.sbuf_tensor(name, shape, dt))

        def at(name, shape, dt, offset):
            return nc.alloc_sbuf_tensor_at(name, shape, dt, offset=offset)

        def sem(name):
            return es.enter_context(nc.semaphore(name))

        ident = sb("ident", [P, P])
        ident_b = sb("ident_b", [P, P], BF16)
        mask = sb("mask", [P, Q4, P], BF16)
        half = sb("half", [P, 1])
        eps = sb("eps", [P, 1])
        iota8 = sb("iota8", [P, EXPERTS])
        mt_hi = sb("mt_hi", [DE, HEADS, P], F32R)
        mt_lo = sb("mt_lo", [DE, HEADS, P], F32R)
        wv_hi = sb("wv_hi", [DE, HEADS * DH], F32R)
        wv_lo = sb("wv_lo", [DE, HEADS * DH], F32R)
        wo_sb = sb("wo_sb", [P, 8, P])
        bo_a_sb = sb("bo_a_sb", [P, P])
        bo_b_sb = sb("bo_b_sb", [P, P])
        ln_sb = sb("ln_sb", [P, 4])
        qkw_hi = sb("qkw_hi", [P, 2, P], F32R)
        qkw_lo = sb("qkw_lo", [P, 2, P], F32R)
        vw_sb = sb("vw_sb", [P, P])
        ow_sb = sb("ow_sb", [P, P])
        gate_sb = sb("gate_sb", [P, EXPERTS])
        sel_q = sb("sel_q", [P, 16 + HEADS * 32], F32R)
        sel_k = sb("sel_k", [P, 16 + HEADS * 32], F32R)
        w1_hi = sb("w1_hi", [P, CHUNKS * P], F32R)
        w1_lo = sb("w1_lo", [P, CHUNKS * P], F32R)
        w2_hi = sb("w2_hi", [P, CHUNKS * P], F32R)
        w2_lo = sb("w2_lo", [P, CHUNKS * P], F32R)
        w3_sb = sb("w3_sb", [P, CHUNKS, P])

        x_in = sb("x_in", [P, NB, P])
        x_res = sb("x_res", [P, NB, P])
        ctx_in = sb("ctx_in", [P, NB, DE])
        ctxn_hi = sb("ctxn_hi", [DE, T], F32R)
        ctxn_lo = sb("ctxn_lo", [DE, T], F32R)
        ctxc_hi = sb("ctxc_hi", [DE, T], F32R)
        ctxc_lo = sb("ctxc_lo", [DE, T], F32R)
        ha = sb("ha", [P, 2, P])
        hat_hi = sb("hat_hi", [P, NB, P], F32R)
        hat_lo = sb("hat_lo", [P, NB, P], F32R)
        g_hi = sb("g_hi", [P, 2, Q4, T], F32R)
        g_lo = sb("g_lo", [P, 2, Q4, T], F32R)
        v_a = sb("v_a", [P, 4, Q4, DH + 1])
        nmax_a = sb("nmax_a", [P, 2, Q4])
        p_a = sb("p_a", [P, 2, Q4, P])
        pt_a = sb("pt_a", [P, Q4, P])
        rden_a = sb("rden_a", [P, 2, Q4])
        o_a = sb("o_a", [P, 2, Q4 * DH])
        ot_a = sb("ot_a", [P, 2, 2, P])
        mv_a = sb("mv_a", [P, NB, 2])
        st_a = sb("st_a", [P, NB, 6])
        ve_a = sb("ve_a", [P, NB])
        rs_a = sb("rs_a", [P, NB])

        y_b = sb("y_b", [P, 2, P])
        yb_res = sb("yb_res", [P, NB, P])
        xy_sum = sb("xy_sum", [P, NB, P])
        acc = sb("acc", [P, NB, P])
        nrm = sb("nrm", [P, NB, P])
        st_b = sb("st_b", [P, NB, 6])
        mv_b = sb("mv_b", [P, 3, NB, 2])
        ve_b = sb("ve_b", [P, 3, NB])
        rs_b = sb("rs_b", [P, 3, NB])
        k_diag = sb("k_diag", [P, 2, Q4, Q4, P], F32R)
        moe_in = at("moe_in", [P, 2, CHUNKS * P], F32, nc.sbuf_base - 16 * 1024)
        v_rest = sb("v_rest", [P, T])
        v_b = sb("v_b", [P, NB, HEADS, 26], BF16)
        nmax_b = sb("nmax_b", [P, 2, Q4])
        p_b = sb("p_b", [P, 2, Q4, P])
        pt_hi = sb("pt_hi", [P, Q4, P], F16)
        pt_lo = sb("pt_lo", [P, Q4, P], F16)
        red_b = sb("red_b", [P, P])
        rden_b = sb("rden_b", [P, HEADS])
        o_b = sb("o_b", [P, 2, P])
        ot_b = sb("ot_b", [P, 2, P])
        sc_m = sb("sc_m", [P, NB, EXPERTS])
        m8 = sb("m8", [P, NB, 8])
        i8 = sb("i8", [P, NB, 8], U32)
        if_m = sb("if_m", [P, NB, 2])
        dd = sb("dd", [P, NB])
        ee = sb("ee", [P, NB])
        zz = sb("zz", [P, NB])
        rr = sb("rr", [P, NB])
        pp = sb("pp", [P, 2, NB])
        eq = sb("eq", [P, 2, NB, EXPERTS])
        wts = sb("wts", [P, NB, EXPERTS])

        KB = 1024
        arena = sb("arena", [P, 24 * KB // 4])
        a0 = nc.sbuf_base - 24 * KB
        q_stk = at("q_stk", [P, Q4, T], F32R, a0)
        g_t = at("g_t", [P, 4, T], F32, a0)
        k_stk = at("k_stk", [P, Q4, T], F32R, a0 + 8 * KB)
        hb_f = at("hb_f", [P, T], F32, a0 + 8 * KB)
        hb_hi = at("hb_hi", [P, T], F32R, a0 + 10 * KB)
        hb_lo = at("hb_lo", [P, T], F32R, a0 + 12 * KB)
        hm_f = at("hm_f", [P, T], F32, a0 + 8 * KB)
        th_m = at("th_m", [P, 2, T], F32, a0 + 10 * KB)
        u_m = at("u_m", [P, T], F32, a0 + 14 * KB)
        qk_hi = at("qk_hi", [P, 2, T], F32R, a0 + 16 * KB)
        qk_lo = at("qk_lo", [P, 2, T], F32R, a0 + 20 * KB)
        hm_hi = at("hm_hi", [P, T], F32R, a0 + 16 * KB)
        hm_lo = at("hm_lo", [P, T], F32R, a0 + 18 * KB)
        wq_in = at("wq_in", [P, HEADS * DH], F32, a0)
        wk_in = at("wk_in", [DE, HEADS * DH], F32, a0 + 4 * KB)
        wv_in = at("wv_in", [DE, HEADS * DH], F32, a0 + 8 * KB)
        wqt = at("wqt", [P, 8, P], F32, a0 + 12 * KB)
        wkt = at("wkt", [P, 8, DE], F32, a0 + 16 * KB)
        qkw_in = at("qkw_in", [P, 2, P], F32, a0 + 19 * KB)
        sel_tmp = at("sel_tmp", [P, 16 + HEADS * 32], F32, a0 + 20 * KB)

        ps = {n: es.enter_context(nc.psum_tensor(f"ps_{n}", [P, 512], F32))
              for n in ("sa", "ta", "ga", "oa", "x", "sb", "tb", "ob")}
        sa, ta, ga, oa, px, psb, tb, ob = (ps[n] for n in ("sa", "ta", "ga", "oa", "x", "sb", "tb", "ob"))

        w_attn_in = sem("w_attn_in")
        w_small_in = sem("w_small_in")
        w_moe_in = sem("w_moe_in")
        w3_in = sem("w3_in")
        x_landed = sem("x_landed")
        ctx_landed = sem("ctx_landed")
        k_placed = [sem(f"k_placed{i}") for i in range(2)]
        out_stored = sem("out_stored")
        const_made = sem("const_made")
        sel_made = sem("sel_made")
        wt_done = sem("wt_done")
        wqt_done = sem("wqt_done")
        wkt_done = sem("wkt_done")
        m_done = sem("m_done")
        mth_done = sem("mth_done")
        mtl_done = sem("mtl_done")
        wvh_done = sem("wvh_done")
        wvl_done = sem("wvl_done")
        qkwh_done = sem("qkwh_done")
        qkwl_done = sem("qkwl_done")
        moew_done = sem("moew_done")
        ones_done = sem("ones_done")

        sa_done = sem("sa_done")
        ta_done = sem("ta_done")
        ga_done = sem("ga_done")
        oa_done = sem("oa_done")
        x1_done = sem("x1_done")
        x2_done = sem("x2_done")
        maxa_done = sem("maxa_done")
        expa_done = sem("expa_done")
        pta_done = sem("pta_done")
        gh_done = sem("gh_done")
        gl_done = sem("gl_done")
        va_done = sem("va_done")
        ota_done = sem("ota_done")
        rdena_done = sem("rdena_done")
        oa_norm = sem("oa_norm")
        x2_act = sem("x2_act")
        x2_free = sem("x2_free")
        sta_done = sem("sta_done")
        mva_done = sem("mva_done")
        vea_done = sem("vea_done")
        rsa_done = sem("rsa_done")
        ha_done = sem("ha_done")
        xres_set = sem("xres_set")
        ctxc_done = sem("ctxc_done")

        st_done = [sem(f"st{i}_done") for i in range(3)]
        mv_done = [sem(f"mv{i}_done") for i in range(3)]
        ve_done = [sem(f"ve{i}_done") for i in range(3)]
        rs_done = [sem(f"rs{i}_done") for i in range(3)]
        y_done = sem("y_done")
        ybo_done = sem("ybo_done")
        sum_done = sem("sum_done")
        nb_done = sem("nb_done")
        nm_done = sem("nm_done")
        hbt_done = sem("hbt_done")
        hbf_done = sem("hbf_done")
        hbh_done = sem("hbh_done")
        hbl_done = sem("hbl_done")
        qk_done = sem("qk_done")
        qkh_done = sem("qkh_done")
        qkl_done = sem("qkl_done")
        vb_done = sem("vb_done")
        v1_done = sem("v1_done")
        vr_done = sem("vr_done")
        v2_done = sem("v2_done")
        v3_done = sem("v3_done")
        stk_done = sem("stk_done")
        stk_act = sem("stk_act")
        stk_dve = sem("stk_dve")
        sb_done = sem("sb_done")
        tb_done = sem("tb_done")
        ob_done = sem("ob_done")
        maxb_done = sem("maxb_done")
        expb_done = sem("expb_done")
        ph_done = sem("ph_done")
        pl_done = sem("pl_done")
        redb_done = sem("redb_done")
        ob_free = sem("ob_free")
        ob_norm = sem("ob_norm")
        last_t_done = sem("last_t_done")
        last_ot = sem("last_ot")
        last_w_done = sem("last_w_done")
        y1_done = sem("y1_done")
        acc_set = sem("acc_set")

        hmt_done = sem("hmt_done")
        hmf_done = sem("hmf_done")
        hmh_done = sem("hmh_done")
        hml_done = sem("hml_done")
        gate_done = sem("gate_done")
        sc_done = sem("sc_done")
        route = sem("route")
        dd_done = sem("dd_done")
        ee_done = sem("ee_done")
        ma_done = sem("ma_done")
        mb_done = sem("mb_done")
        th_done = sem("th_done")
        u_done = sem("u_done")
        g_done = sem("g_done")
        dn_done = sem("dn_done")
        comb_done = sem("comb_done")
        ROUTE = 10

        block = es.enter_context(nc.Block())

        def f32(ap):
            return ap.bitcast(F32)

        def tok(b):
            return slice(b * P, (b + 1) * P)

        @block.sync
        def _(sp):
            sp.dma_start(wq_in[:], Wq).then_inc(w_attn_in, 16)
            sp.dma_start(wk_in[:], Wk).then_inc(w_attn_in, 16)
            sp.dma_start(ctx_in[:], ctx_v[0]).then_inc(ctx_landed, 16)
            sp.dma_start(x_in[:], x_v[0]).then_inc(x_landed, 16)
            sp.dma_start(wv_in[:], Wv).then_inc(w_attn_in, 16)
            sp.dma_start(wo_sb[:], Wo.rearrange("(t p) d -> p t d", p=P)).then_inc(w_small_in, 16)
            for dst, src in ((bo_a_sb, bo_a), (bo_b_sb, bo_b)):
                sp.dma_start(dst[:], src.rearrange("(a d) -> a d", a=1).to_broadcast([P, P])).then_inc(w_small_in, 16)
            for i, src in enumerate((ln1_s, ln1_b, ln2_s, ln2_b)):
                sp.dma_start(ln_sb[:, i:i + 1], src.rearrange("(d a) -> d a", a=1)).then_inc(w_small_in, 16)
            for dst, src in ((qkw_in[:, 0, :], wq), (qkw_in[:, 1, :], wk), (vw_sb[:], wv), (ow_sb[:], wo),
                             (gate_sb[:], gate_w)):
                sp.dma_start(dst, src).then_inc(w_small_in, 16)
            for i, src in enumerate((w1, w2)):
                sp.dma_start(moe_in[:, i, :].rearrange("d (e h) -> d e h", e=EXPERTS),
                             src.rearrange("e d h -> d e h")).then_inc(w_moe_in, 16)
            sp.dma_start(w3_sb[:], w3.rearrange("e (c p) d -> p (e c) d", p=P)).then_inc(w3_in, 16)

            def body(it):
                if live(it, 1) and not (isinstance(it, int) and it < 0):
                    wait_use(sp, x2_done, use2, it, -5)
                    sp.dma_start(ctx_in[:], ctx_v[it + 1]).then_inc(ctx_landed, 16)
                    wait(sp, xres_set, it, NB, NB)
                    wait(sp, ha_done, it, NB, NB)
                    sp.dma_start(x_in[:], x_v[it + 1]).then_inc(x_landed, 16)
                if live(it, -2):
                    wait(sp, comb_done, it - 2, EXPERTS, EXPERTS)
                    sp.dma_start(out_v[it - 2], acc[:]).then_inc(out_stored, 16)
                if live(it, -1):
                    wait(sp, stk_act, it - 1, Q4, 2)
                    wait(sp, stk_dve, it - 1, Q4, 2)
                    for b in range(NB):
                        wait(sp, sb_done, it - 1, STEPS, Q4 * (b - 1))
                        for hh in range(Q4):
                            r = slice(32 * hh, 32 * hh + 32)
                            sp.dma_start(f32(k_diag[r, b % 2, :, hh, :]), f32(k_stk[r, :, tok(b)])).then_inc(k_placed[b % 2], 16)

            iterations(sp, body)
            sp.wait_ge(out_stored, 16 * NG)

        @block.tensor
        def _(pe):
            def split3(dst, l_hi, l_lo, r_hi, r_lo):
                pe.matmul(dst, l_hi, r_hi, start=True, stop=False)
                pe.matmul(dst, l_hi, r_lo, start=False, stop=False)
                return pe.matmul(dst, l_lo, r_hi, start=False, stop=True)

            pe.wait_ge(const_made, 2)
            pe.wait_ge(w_attn_in, 48)
            for t in range(8):
                pe.transpose((sa if t < 4 else ta)[:, tok(t % 4)], wq_in[:, tok(t)], ident[:])
            for t in range(8):
                mm = pe.transpose((ga if t < 4 else oa)[:, (t % 4) * DE:(t % 4 + 1) * DE], wk_in[:, tok(t)],
                                  ident[0:DE, 0:DE])
            mm.then_inc(wt_done, 1)
            pe.wait_ge(wqt_done, 2)
            pe.wait_ge(wkt_done, 2)
            for h in range(HEADS):
                r = slice(64 * (h % 2), 64 * (h % 2) + 64)
                bank = (psb, tb, ob, px)[2 * (h // 8) + h % 2]
                mm = pe.matmul(bank[0:DE, tok(h % 8 // 2)], wkt[r, h // 2, :], wqt[r, h // 2, :], start=True, stop=True)
            mm.then_inc(m_done, 1)

            def scores_a(it, u):
                hq, b = divmod(u, NB)
                if b == 0:
                    wait(pe, gl_done, it, HEADS, Q4 * hq + Q4)
                if hq == 0:
                    wait_use(pe, x2_free, use2, it, b - 4)
                wait(pe, expa_done, it, STEPS, u)
                if b_before_a(u) and live(it, -1):
                    wait(pe, expb_done, it - 1, STEPS, b_before_a(u))
                g = [t[:, hq % 2, :, tok(b)] for t in (g_hi, g_lo)]
                split3(sa[:].rearrange("q (h k) -> q h k", h=Q4), hat_hi[:, b, :], hat_lo[:, b, :], *g).then_inc(sa_done, 1)

            def transposes_a(it, u):
                wait(pe, expa_done, it, STEPS, u + 1)
                wait(pe, pta_done, it, STEPS, u)
                for h in range(Q4):
                    mm = pe.transpose(ta[:, tok(h)], p_a[:, u % 2, h, :], ident[:])
                mm.then_inc(ta_done, 1)

            def keys_a(it, s):
                j = (s + Q4) % HEADS
                if s == 12:
                    wait_use(pe, x2_free, use2, it, 11)
                if s == 4:
                    wait(pe, ctxc_done, it, 2, 2)
                wait(pe, gl_done, it, HEADS, s + Q4)
                c = (ctxc_hi, ctxc_lo) if 4 <= s < 12 else (ctxn_hi, ctxn_lo)
                split3(ga[:], mt_hi[:, j, :], mt_lo[:, j, :], c[0][:], c[1][:]).then_inc(ga_done, 1)

            def values_and_output_t_a(it, s):
                if not use1(it, s):
                    return
                wait_use(pe, x2_free, use2, it, s - 1)
                if isinstance(it, int) and it == 0 and s in (1, 2):
                    pe.wait_ge(va_done, s + 1)
                mm = None
                if live(it) if s + 1 < STEPS else live(it, 1):
                    hq, b = divmod((s + 1) % STEPS, NB)
                    c = (ctxc_hi, ctxc_lo) if 4 <= s < 15 else (ctxn_hi, ctxn_lo)
                    w = slice(hq * Q4 * DH, (hq + 1) * Q4 * DH)
                    mm = split3(px[:, 0:Q4 * DH], c[0][:, tok(b)], c[1][:, tok(b)], wv_hi[:, w], wv_lo[:, w])
                if wo_a(it, s):
                    wait(pe, oa_norm, it, STEPS, s - 1)
                    for i in range(2):
                        mm = pe.transpose(px[:, tok(2 + i)], o_a[:, s % 2, tok(i)], ident[:])
                mm.then_inc(x1_done, 1)

            def context_a(it, u):
                wait(pe, pta_done, it, STEPS, u + 1)
                wait(pe, va_done, it, STEPS, u + 1)
                wait(pe, oa_norm, it, STEPS, u)
                for h in range(Q4):
                    mm = pe.matmul(oa[:, h * (DH + 1):(h + 1) * (DH + 1)], pt_a[:, h, :], v_a[:, u % 4, h, :],
                                   start=True, stop=True)
                mm.then_inc(oa_done, 1)

            def second_use(it, s):
                if not use2(it, s):
                    return
                if use1(it, s):
                    wait(pe, va_done, it, STEPS, min(s + 2, NG * STEPS if not isinstance(it, int) else NG * STEPS - it * STEPS))
                    if wo_a(it, s):
                        wait(pe, ota_done, it, STEPS, s - 1)
                else:
                    wait_use(pe, x2_free, use2, it, s - 1)
                mm = None
                if 8 <= s < 12 and live(it, 1):
                    if s == 8:
                        wait(pe, ctx_landed, it + 1, 16, 16)
                    mm = pe.transpose(px[0:DE, tok(1)], ctx_in[:, s - 8, :], ident[:])
                if s >= 12 and live(it, 1):
                    wait(pe, ha_done, it + 1, NB, s - 12 + 1)
                    mm = pe.transpose(px[:, tok(1)], ha[:, s % 2, :], ident[:])
                if live(it, -1):
                    for i, b in enumerate(B_OUT_T.get(s, ())):
                        wait(pe, ob_norm, it - 1, NB, b + 1)
                        mm = pe.transpose(px[:, tok(2 + i)], o_b[:, b % 2, :], ident[:])
                    for i, b in enumerate(B_OUT_W.get(s, ())):
                        mm = pe.matmul(px[:, tok(2 + i)], ot_b[:, b % 2, :], ow_sb[:], start=True, stop=True)
                if wo_a(it, s):
                    hq = (s - 2) % STEPS // NB
                    for i in range(2):
                        mm = pe.matmul(px[:, tok(0)], ot_a[:, s % 2, i, :], wo_sb[:, 2 * hq + i, :],
                                       start=(i == 0), stop=(i == 1))
                mm.then_inc(x2_done, 1)

            def project_b(it, s, k):
                if (s, k) == HBT_GAP:
                    wait(pe, nb_done, it - 1, NB, NB)
                    wait(pe, g_done, it - 1, CHUNKS, 0)
                    for b in range(NB):
                        mm = pe.transpose(tb[:, tok(b)], nrm[:, b, :], ident[:])
                    mm.then_inc(hbt_done, 1)
                if (s, k) == QK_GAP:
                    wait(pe, hbl_done, it - 1, 1, 1)
                    wait(pe, u_done, it - 1, CHUNKS, 0)
                    wait(pe, comb_done, it - 1, EXPERTS, 0)
                    for i, bank in enumerate((psb, ob)):
                        split3(bank[:], qkw_hi[:, i, :], qkw_lo[:, i, :], hb_hi[:], hb_lo[:]).then_inc(qk_done, 1)
                if (s, k) == V_GAP:
                    for b in range(NB):
                        mm = pe.matmul(tb[:, tok(b)], hb_f[:, tok(b)], vw_sb[:], start=True, stop=True)
                    mm.then_inc(vb_done, 1)
                if (s, k) in STACK_GAPS:
                    n = STACK_GAPS.index((s, k))
                    for i in (2 * n, 2 * n + 1):
                        side, t = (1, 0)[i // 4], i % 4
                        bank, sel = (psb, ob, tb)[i % 3], (sel_q, sel_k)[side]
                        if i < 2:
                            wait(pe, qkl_done, it - 1, 2, 2)
                        elif i == 2:
                            wait(pe, vr_done, it - 1, 1, 1)
                        else:
                            wait(pe, (stk_dve, stk_act)[i % 2], it - 1, Q4, (i - 3) // 2 + 1)
                        c0, shift = 16 + P * t, (16, 8)[side]
                        pe.matmul(bank[:], sel[:, c0:c0 + P], qk_hi[:, side, :], start=True, stop=False)
                        pe.matmul(bank[:], sel[:, c0 - shift:c0 - shift + P], qk_lo[:, side, :],
                                  start=False, stop=True).then_inc(stk_done, 1)

            def unit_b(it, s, k):
                w = b_slot(s, k)
                if w is None:
                    return
                if w < STEPS:
                    b, t = divmod(w, Q4)
                    if w == 0:
                        wait(pe, stk_act, it - 1, Q4, Q4)
                        wait(pe, stk_dve, it - 1, Q4, Q4)
                    if t == 0:
                        wait(pe, k_placed[b % 2], it - 1, 128, 64 * (b // 2 + 1))
                    wait(pe, expb_done, it - 1, STEPS, b_before(w))
                    if b_bank(w) and live(it):
                        wait(pe, expa_done, it, STEPS, s + 1)
                    bank = (psb, sa)[b_bank(w)]
                    pe.matmul(bank[:], ident_b[:], mask[:], start=True, stop=False)
                    pe.matmul(bank[:].rearrange("q (h k) -> q h k", h=Q4), q_stk[:, t, tok(b)],
                              k_diag[:, b % 2, t, :, :], start=False, stop=True).then_inc(sb_done, 1)
                if 2 <= w <= STEPS + 1:
                    wait(pe, expb_done, it - 1, STEPS, w - 1)
                    if w == 2:
                        wait(pe, stk_dve, it - 1, Q4, Q4)
                    wait(pe, pl_done, it - 1, STEPS, w - 2)
                    for h in range(Q4):
                        mm = pe.transpose(tb[:, tok(h)], p_b[:, w % 2, h, :], ident[:])
                    mm.then_inc(tb_done, 1)
                if w >= 3:
                    b, t = divmod(w - 3, Q4)
                    if w == 3:
                        wait(pe, v3_done, it - 1, 1, 1)
                    if t == 0:
                        wait(pe, ob_free, it - 1, NB, b)
                    wait(pe, pl_done, it - 1, STEPS, w - 2)
                    for h in range(Q4):
                        c = 25 * (Q4 * t + h)
                        vals = v_b[:, b, Q4 * t + h, 0:25]
                        pe.matmul(ob[:, c:c + 25], pt_hi[:, h, :], vals, start=True, stop=False)
                        mm = pe.matmul(ob[:, c:c + 25], pt_lo[:, h, :], vals, start=False, stop=True)
                    mm.then_inc(ob_done, 1)

            def last_outputs_b(it, s, k):
                if (s, k) == LAST_T_GAP:
                    wait(pe, ob_norm, it - 1, NB, NB)
                    wait(pe, pl_done, it - 1, STEPS, STEPS)
                    for i in range(2):
                        mm = pe.transpose(tb[:, tok(i)], o_b[:, i, :], ident[:])
                    mm.then_inc(last_t_done, 1)
                if (s, k) == LAST_W_GAP:
                    wait(pe, last_ot, it - 1, 1, 1)
                    wait(pe, expb_done, it - 1, STEPS, STEPS)
                    for i in range(2):
                        mm = pe.matmul(psb[:, tok(i)], ot_b[:, i, :], ow_sb[:], start=True, stop=True)
                    mm.then_inc(last_w_done, 1)

            def start_m(it, s, k):
                if (s, k) == HMT_GAP:
                    wait(pe, nm_done, it - 1, NB, NB)
                    wait(pe, last_ot, it - 1, 1, 1)
                    for b in range(NB):
                        mm = pe.transpose(tb[:, tok(b)], nrm[:, b, :], ident[:])
                    mm.then_inc(hmt_done, 1)
                if (s, k) == GATE_GAP:
                    wait(pe, hmf_done, it - 1, 1, 1)
                    wait(pe, ob_free, it - 1, NB, NB)
                    for b in range(NB):
                        mm = pe.matmul(ob[:, b * EXPERTS:(b + 1) * EXPERTS], hm_f[:, tok(b)], gate_sb[:],
                                       start=True, stop=True)
                    mm.then_inc(gate_done, 1)

            def expert_m(it, s, k):
                j = m_chunk(s, k)
                if j is not None:
                    if j == 0:
                        wait(pe, hml_done, it - 2, 1, 1)
                        wait(pe, expb_done, it - 2, STEPS, STEPS)
                    else:
                        wait(pe, u_done, it - 2, CHUNKS, j)
                    w = slice(j * P, (j + 1) * P)
                    split3(psb[:], w1_hi[:, w], w1_lo[:, w], hm_hi[:], hm_lo[:]).then_inc(ma_done, 1)
                    if j:
                        wait(pe, g_done, it - 2, CHUNKS, j)
                    split3(tb[:], w2_hi[:, w], w2_lo[:, w], hm_hi[:], hm_lo[:]).then_inc(mb_done, 1)

            def down_m(it, s, k, after):
                e = m_down(s, k, after)
                if e is not None:
                    if e == 0:
                        wait(pe, sc_done, it - 2, 1, 1)
                    else:
                        wait(pe, comb_done, it - 2, EXPERTS, e)
                    wait(pe, g_done, it - 2, CHUNKS, 2 * e + 2)
                    for b in range(NB):
                        for i in range(2):
                            mm = pe.matmul(ob[:, tok(b)], g_t[:, (2 * e + i) % 4, tok(b)], w3_sb[:, 2 * e + i, :],
                                           start=(i == 0), stop=(i == 1))
                    mm.then_inc(dn_done, 1)

            def gap(it, s, k):
                if live(it, -2):
                    down_m(it, s, k, False)
                    expert_m(it, s, k)
                    down_m(it, s, k, True)
                if live(it, -1):
                    project_b(it, s, k)
                    unit_b(it, s, k)
                    last_outputs_b(it, s, k)
                    start_m(it, s, k)

            def body(it):
                if isinstance(it, int) and it == -1:
                    pe.wait_ge(mtl_done, 4)
                    pe.wait_ge(wvl_done, 1)
                    pe.wait_ge(w_small_in, 16 * 12)
                if isinstance(it, int) and it == 1:
                    pe.wait_ge(qkwl_done, 1)
                    pe.wait_ge(sel_made, 2)
                    pe.wait_ge(moew_done, 5)
                    pe.wait_ge(w3_in, 16)
                for s in range(STEPS):
                    if live(it):
                        scores_a(it, s)
                    gap(it, s, 0)
                    if live(it, 0 if s else -1):
                        transposes_a(it if s else it - 1, (s - 1) % STEPS)
                    gap(it, s, 1)
                    if live(it, 0 if s < 12 else 1):
                        keys_a(it, s)
                    gap(it, s, 2)
                    values_and_output_t_a(it, s)
                    gap(it, s, 3)
                    if live(it, 0 if s else -1):
                        context_a(it if s else it - 1, (s - 1) % STEPS)
                    gap(it, s, 4)
                    second_use(it, s)
                    gap(it, s, 5)

            iterations(pe, body)

        @block.scalar
        def _(act):
            act.wait_ge(wt_done, 1)
            for i, bank in enumerate((sa, ta)):
                act.activation(wqt[:, 4 * i:4 * i + 4, :], bank[:].rearrange("p (t c) -> p t c", t=4),
                               ACT.Copy).then_inc(wqt_done, 1)
            act.activation(wv_hi[:], wv_in[:], ACT.Copy).then_inc(wvh_done, 1)
            act.wait_ge(m_done, 1)
            for i, bank in enumerate((psb, tb, ob, px)):
                h0 = 8 * (i // 2) + i % 2
                act.activation(mt_hi[:, h0:h0 + 7:2, :], bank[0:DE, :].rearrange("p (t c) -> p t c", t=4),
                               ACT.Copy, scale=DH ** -0.5).then_inc(mth_done, 1)
            act.wait_ge(w_small_in, 16 * 12)
            act.activation(qkw_hi[:], qkw_in[:], ACT.Copy).then_inc(qkwh_done, 1)

            def exp_a(it, u):
                wait(act, maxa_done, it, STEPS, u + 1)
                wait(act, ta_done, it, STEPS, u - 1)
                for h in range(Q4):
                    a = act.activation(p_a[:, u % 2, h, :], sa[:, tok(h)], ACT.Exp, bias=nmax_a[:, u % 2, h:h + 1])
                a.then_inc(expa_done, 1)

            def pt_copy_a(it, u):
                wait(act, ta_done, it, STEPS, u + 1)
                wait(act, oa_done, it, STEPS, u)
                act.activation(pt_a[:], ta[:].rearrange("p (h q) -> p h q", h=Q4), ACT.Copy).then_inc(pta_done, 1)

            def keys_hi_a(it, s):
                j = (s + Q4) % HEADS
                wait(act, ga_done, it, HEADS, s + Q4 + 1)
                act.activation(g_hi[:, j // Q4 % 2, j % Q4, :], ga[:], ACT.Copy).then_inc(gh_done, 1)

            def first_use(it, s):
                if not use1(it, s):
                    return
                wait_use(act, x1_done, use1, it, s)
                if live(it) if s + 1 < STEPS else live(it, 1):
                    act.activation(v_a[:, (s + 1) % 4, :, 0:DH], px[:, 0:Q4 * DH].rearrange("p (h d) -> p h d", h=Q4),
                                   ACT.Copy).then_inc(va_done, 1)
                if wo_a(it, s):
                    act.activation(ot_a[:, s % 2, :, :], px[:, 2 * P:4 * P].rearrange("p (i q) -> p i q", i=2),
                                   ACT.Copy).then_inc(ota_done, 1)

            def second_use(it, s):
                if not act_use2(it, s):
                    return
                wait_use(act, x2_done, use2, it, s)
                a = None
                if 8 <= s < 12 and live(it, 1):
                    if s == 8:
                        wait(act, ctxc_done, it, 2, 2)
                    a = act.activation(ctxn_hi[:, tok(s - 8)], px[0:DE, tok(1)], ACT.Copy)
                if s >= 12 and live(it, 1):
                    a = act.activation(hat_hi[:, s - 12, :], px[:, tok(1)], ACT.Copy)
                if live(it, -1):
                    for i, b in enumerate(B_OUT_T.get(s, ())):
                        a = act.activation(ot_b[:, b % 2, :], px[:, tok(2 + i)], ACT.Copy)
                a.then_inc(x2_act if dve_use2(it, s) else x2_free, 1)

            def project_b(it, s, k):
                if (s, k) == HBT_GAP:
                    wait(act, hbt_done, it - 1, 1, 1)
                    act.activation(hb_f[:], tb[:], ACT.Identity, bias=ln_sb[:, 1:2], scale=ln_sb[:, 0:1]).then_inc(hbf_done, 1)
                    wait(act, hbf_done, it - 1, 1, 1)
                    act.activation(hb_hi[:], hb_f[:], ACT.Copy).then_inc(hbh_done, 1)
                if (s, k) == QK_GAP:
                    for i, bank in enumerate((psb, ob)):
                        wait(act, qk_done, it - 1, 2, i + 1)
                        act.activation(qk_hi[:, i, :], bank[:], ACT.Copy, scale=(EB ** -0.5, 1.0)[i]).then_inc(qkh_done, 1)
                if (s, k) == V_GAP:
                    wait(act, vb_done, it - 1, 1, 1)
                    act.activation(v_b[:, :, :, 0:EB], tb[:].rearrange("p (b h d) -> p b h d", b=NB, h=HEADS),
                                   ACT.Copy).then_inc(v1_done, 1)
                if (s, k) in STACK_GAPS:
                    n = STACK_GAPS.index((s, k))
                    wait(act, stk_done, it - 1, 8, 2 * n + 1)
                    act.activation((k_stk, q_stk)[n // 2][:, 2 * n % 4, :], (psb, ob, tb)[2 * n % 3][:], ACT.Copy).then_inc(stk_act, 1)

            def unit_b(it, s, k):
                w = b_slot(s, k)
                if w is None:
                    return
                if 2 <= w <= STEPS + 1:
                    wait(act, tb_done, it - 1, STEPS, w - 1)
                    wait(act, ob_done, it - 1, STEPS, w - 2)
                    act.activation(pt_hi[:], tb[:].rearrange("p (h q) -> p h q", h=Q4), ACT.Copy,
                                   scale=P_SCALE).then_inc(ph_done, 1)
                if w < STEPS:
                    wait(act, maxb_done, it - 1, STEPS, w + 1)
                    wait(act, tb_done, it - 1, STEPS, w - 1)
                    for h in range(Q4):
                        a = act.activation(p_b[:, w % 2, h, :], (psb, sa)[b_bank(w)][:, tok(h)], ACT.Exp, bias=nmax_b[:, w % 2, h:h + 1])
                    a.then_inc(expb_done, 1)

            def last_outputs_b(it, s, k):
                if (s, k) == LAST_T_GAP:
                    wait(act, last_t_done, it - 1, 1, 1)
                    act.activation(ot_b[:], tb[:, 0:2 * P].rearrange("p (i q) -> p i q", i=2), ACT.Copy).then_inc(last_ot, 1)

            def start_m(it, s, k):
                if (s, k) == HMT_GAP:
                    wait(act, hmt_done, it - 1, 1, 1)
                    act.activation(hm_f[:], tb[:], ACT.Identity, bias=ln_sb[:, 3:4], scale=ln_sb[:, 2:3]).then_inc(hmf_done, 1)
                    wait(act, hmf_done, it - 1, 1, 1)
                    act.activation(hm_hi[:], hm_f[:], ACT.Copy).then_inc(hmh_done, 1)
                if (s, k) == EE_GAP:
                    wait(act, dd_done, it - 1, 1, 1)
                    act.activation(ee[:], dd[:], ACT.Exp).then_inc(ee_done, 1)

            def expert_m(it, s, k):
                j = m_chunk(s, k)
                if j is not None:
                    wait(act, ma_done, it - 2, CHUNKS, j + 1)
                    if j >= 2:
                        wait(act, u_done, it - 2, CHUNKS, j - 1)
                    act.activation(th_m[:, j % 2, :], psb[:], ACT.Tanh, scale=0.5).then_inc(th_done, 1)

            def gap(it, s, k):
                if live(it, -2):
                    expert_m(it, s, k)
                if live(it, -1):
                    project_b(it, s, k)
                    unit_b(it, s, k)
                    last_outputs_b(it, s, k)
                    start_m(it, s, k)

            def body(it):
                for s in range(STEPS):
                    if live(it):
                        exp_a(it, s)
                    if live(it, 0 if s else -1):
                        pt_copy_a(it if s else it - 1, (s - 1) % STEPS)
                    gap(it, s, 0)
                    gap(it, s, 1)
                    if live(it, 0 if s < 12 else 1):
                        keys_hi_a(it, s)
                    gap(it, s, 2)
                    first_use(it, s)
                    gap(it, s, 3)
                    gap(it, s, 4)
                    second_use(it, s)
                    gap(it, s, 5)

            iterations(act, body)

        @block.vector
        def _(dve):
            dve.memset(v_a[:, :, :, DH:DH + 1], 1.0).then_inc(ones_done, 1)
            dve.memset(v_b[:, :, :, 24:25], 1.0).then_inc(ones_done, 1)
            dve.wait_ge(wt_done, 1)
            for i, bank in enumerate((ga, oa)):
                dve.tensor_copy(wkt[:, 4 * i:4 * i + 4, :],
                                bank[:, 0:4 * DE].rearrange("p (t c) -> p t c", t=4)).then_inc(wkt_done, 1)
            dve.wait_ge(wvh_done, 1)
            dve.tensor_tensor(wv_lo[:], wv_in[:], f32(wv_hi[:]), ALU.subtract).then_inc(wvl_done, 1)
            for i, bank in enumerate((psb, tb, ob, px)):
                h0 = 8 * (i // 2) + i % 2
                dve.wait_ge(mth_done, i + 1)
                dve.scalar_tensor_tensor(out=mt_lo[:, h0:h0 + 7:2, :], in0=bank[0:DE, :].rearrange("p (t c) -> p t c", t=4),
                                         scalar=DH ** -0.5, in1=f32(mt_hi[:, h0:h0 + 7:2, :]),
                                         op0=ALU.mult, op1=ALU.subtract).then_inc(mtl_done, 1)
            dve.wait_ge(qkwh_done, 1)
            dve.tensor_tensor(qkw_lo[:], qkw_in[:], f32(qkw_hi[:]), ALU.subtract).then_inc(qkwl_done, 1)

            def max_a(it, u):
                wait(dve, sa_done, it, STEPS, u + 1)
                dve.tensor_reduce(nmax_a[:, u % 2, :], sa[:].rearrange("q (h k) -> q h k", h=Q4), AX, ALU.max,
                                  negate=True).then_inc(maxa_done, 1)

            def keys_lo_a(it, s):
                j = (s + Q4) % HEADS
                wait(dve, gh_done, it, HEADS, s + Q4 + 1)
                dve.tensor_tensor(g_lo[:, j // Q4 % 2, j % Q4, :], ga[:], f32(g_hi[:, j // Q4 % 2, j % Q4, :]),
                                  ALU.subtract).then_inc(gl_done, 1)

            def normalise_a(it, u):
                wait(dve, oa_done, it, STEPS, u + 1)
                o = oa[:, 0:Q4 * (DH + 1)].rearrange("q (h d) -> q h d", h=Q4)
                dve.reciprocal(rden_a[:, u % 2, :], o[:, :, DH]).then_inc(rdena_done, 1)
                wait(dve, rdena_done, it, STEPS, u + 1)
                dve.tensor_tensor(o_a[:, u % 2, :].rearrange("q (h d) -> q h d", h=Q4), o[:, :, 0:DH],
                                  rden_a[:, u % 2, :].unsqueeze(2).to_broadcast([P, Q4, DH]),
                                  ALU.mult).then_inc(oa_norm, 1)

            def norm_stats(it, i, b, src):
                dve.bn_stats(st_b[:, b, :], src).then_inc(st_done[i], 1)
                wait(dve, st_done[i], it, NB, b + 1)
                dve.nop(nofuse=True)
                dve.bn_aggr(mv_b[:, i, b, :], st_b[:, b, :]).then_inc(mv_done[i], 1)

            def norm_apply(it, i, b, dst, src):
                wait(dve, rs_done[i], it, NB, b + 1)
                return dve.tensor_scalar(dst, src, mv_b[:, i, b, 0:1], rs_b[:, i, b:b + 1], ALU.subtract, ALU.mult)

            def add_output(it, b, attn):
                wait(dve, sum_done, it - 1, NB, b + 1)
                wait(dve, out_stored, it - 1, 16, 0)
                dve.tensor_tensor(yb_res[:, b, :], attn, yb_res[:, b, :], ALU.add).then_inc(y1_done, 1)
                return dve.tensor_tensor(acc[:, b, :], attn, xy_sum[:, b, :], ALU.add)

            def last_outputs_b(it, s, k):
                if (s, k) == LAST_W_GAP:
                    wait(dve, last_w_done, it - 1, 1, 1)
                    for i in range(2):
                        add_output(it, 2 + i, psb[:, tok(i)]).then_inc(acc_set, 1)

            def second_use(it, s):
                if dve_use2(it, s):
                    wait_use(dve, x2_done, use2, it, s)
                    if act_use2(it, s):
                        wait_use(dve, x2_act, lambda i, t: act_use2(i, t) and dve_use2(i, t), it, s)
                    d = None
                    if 8 <= s < 12 and live(it, 1):
                        d = dve.tensor_tensor(ctxn_lo[:, tok(s - 8)], px[0:DE, tok(1)], f32(ctxn_hi[:, tok(s - 8)]),
                                              ALU.subtract)
                    if s >= 12 and live(it, 1):
                        d = dve.tensor_tensor(hat_lo[:, s - 12, :], px[:, tok(1)], f32(hat_hi[:, s - 12, :]), ALU.subtract)
                    if live(it, -1):
                        for i, b in enumerate(B_OUT_W.get(s, ())):
                            d = add_output(it, b, px[:, tok(2 + i)])
                            if wo_a(it, s):
                                d.then_inc(acc_set, 1)
                                d = None
                    if wo_a(it, s):
                        g, u = (it, s - 2) if s >= 2 else (it - 1, s + 14)
                        b = u % NB
                        wait(dve, xres_set, g, NB, b + 1)
                        d = dve.tensor_tensor(x_res[:, b, :], px[:, tok(0)], x_res[:, b, :], ALU.add)
                    d.then_inc(x2_free, 1)

            def norms_early(it, s):
                if live(it, -1):
                    for b in B_NORMS.get(s, ()):
                        wait(dve, y1_done, it - 1, NB, b + 1)
                        norm_stats(it - 1, 2, b, yb_res[:, b, :])
                g, b = (it, 0) if s == 15 else (it - 1, s + 1)
                if (s == 15 or s < 3) and live(g):
                    wait_use(dve, x2_free, use2, it, s - 1)
                    norm_stats(g, 0, b, x_res[:, b, :])
                if s < 4 and live(it, -1):
                    norm_apply(it - 1, 1, s, nrm[:, s, :], y_b[:, s % 2, :]).then_inc(nb_done, 1)

            def norms_late(it, s):
                if live(it, -1):
                    for b in B_NORMS.get(s, ()):
                        norm_apply(it - 1, 2, b, nrm[:, b, :], yb_res[:, b, :]).then_inc(nm_done, 1)
                g, b = (it, 0) if s == 15 else (it - 1, s + 1)
                if (s == 15 or s < 3) and live(g):
                    wait(dve, nb_done, g, NB, b - 1)
                    wait(dve, ybo_done, g, NB, b - 1)
                    norm_apply(g, 0, b, y_b[:, b % 2, :], x_res[:, b, :]).then_inc(y_done, 1)
                    wait(dve, y_done, g, NB, b + 1)
                    norm_stats(g, 1, b, y_b[:, b % 2, :])

            def norm_next_a(it, s):
                if not live(it, 1):
                    return
                if s == 9:
                    wait(dve, x_landed, it + 1, 16, 16)
                    for b in range(NB):
                        dve.bn_stats(st_a[:, b, :], x_in[:, b, :]).then_inc(sta_done, 1)
                    wait(dve, sta_done, it + 1, NB, NB)
                    dve.nop(nofuse=True)
                    for b in range(NB):
                        dve.bn_aggr(mv_a[:, b, :], st_a[:, b, :]).then_inc(mva_done, 1)
                if 11 <= s < 15:
                    b = s - 11
                    wait(dve, rsa_done, it + 1, 1, 1)
                    dve.tensor_scalar(ha[:, b % 2, :], x_in[:, b, :], mv_a[:, b, 0:1], rs_a[:, b:b + 1],
                                      ALU.subtract, ALU.mult).then_inc(ha_done, 1)

            def project_b(it, s, k):
                if (s, k) == HBT_GAP:
                    wait(dve, hbh_done, it - 1, 1, 1)
                    dve.tensor_tensor(hb_lo[:], hb_f[:], f32(hb_hi[:]), ALU.subtract).then_inc(hbl_done, 1)
                if (s, k) == QK_GAP:
                    for i, bank in enumerate((psb, ob)):
                        wait(dve, qkh_done, it - 1, 2, i + 1)
                        dve.scalar_tensor_tensor(out=qk_lo[:, i, :], in0=bank[:], scalar=(EB ** -0.5, 1.0)[i],
                                                 in1=f32(qk_hi[:, i, :]), op0=ALU.mult, op1=ALU.subtract).then_inc(qkl_done, 1)
                if (s, k) == V_GAP:
                    wait(dve, v1_done, it - 1, 1, 1)
                    dve.tensor_tensor(heads(v_rest[:]), heads(tb[:]), v_b[:, :, :, 0:8], ALU.subtract).then_inc(vr_done, 1)
                if (s, k) in STACK_GAPS:
                    n = STACK_GAPS.index((s, k))
                    wait(dve, stk_done, it - 1, 8, 2 * n + 2)
                    dve.tensor_copy((k_stk, q_stk)[n // 2][:, 2 * n % 4 + 1, :], (psb, ob, tb)[(2 * n + 1) % 3][:]).then_inc(stk_dve, 1)
                if (s, k) == V_PARTS_GAP:
                    wait(dve, vr_done, it - 1, 1, 1)
                    dve.tensor_copy(v_b[:, :, :, 8:16], heads(v_rest[:])).then_inc(v2_done, 1)
                    wait(dve, v2_done, it - 1, 1, 1)
                    dve.tensor_tensor(v_b[:, :, :, 16:24], heads(v_rest[:]), v_b[:, :, :, 8:16], ALU.subtract).then_inc(v3_done, 1)

            def heads(t):
                return t.rearrange("p (b h d) -> p b h d", b=NB, h=HEADS)

            def unit_b(it, s, k):
                w = b_slot(s, k)
                if w is None:
                    return
                if w < STEPS:
                    wait(dve, sb_done, it - 1, STEPS, w + 1)
                    dve.tensor_reduce(nmax_b[:, w % 2, :], (psb, sa)[b_bank(w)][:].rearrange("q (h k) -> q h k", h=Q4), AX, ALU.max,
                                      negate=True).then_inc(maxb_done, 1)
                if 2 <= w <= STEPS + 1:
                    wait(dve, ph_done, it - 1, STEPS, w - 1)
                    dve.scalar_tensor_tensor(out=pt_lo[:], in0=tb[:].rearrange("p (h q) -> p h q", h=Q4), scalar=P_SCALE,
                                             in1=pt_hi[:], op0=ALU.mult, op1=ALU.subtract).then_inc(pl_done, 1)
                if w >= 3 and (w - 3) % Q4 == Q4 - 1:
                    b = (w - 3) // Q4
                    wait(dve, ob_done, it - 1, STEPS, w - 2)
                    o = ob[:, 0:25 * HEADS].rearrange("q (h c) -> q h c", h=HEADS)
                    dve.tensor_reduce(red_b[:].rearrange("q (h d) -> q h d", h=HEADS),
                                      o[:, :, 0:24].rearrange("q h (c d) -> q h d c", c=3), AX, ALU.add).then_inc(redb_done, 1)
                    dve.reciprocal(rden_b[:], o[:, :, 24]).then_inc(ob_free, 1)
                    wait(dve, redb_done, it - 1, NB, b + 1)
                    wait(dve, ob_free, it - 1, NB, b + 1)
                    dve.tensor_tensor(o_b[:, b % 2, :].rearrange("q (h d) -> q h d", h=HEADS),
                                      red_b[:].rearrange("q (h d) -> q h d", h=HEADS),
                                      rden_b[:].unsqueeze(2).to_broadcast([P, HEADS, EB]), ALU.mult).then_inc(ob_norm, 1)

            def start_m(it, s, k):
                if (s, k) == HMT_GAP:
                    wait(dve, hmh_done, it - 1, 1, 1)
                    dve.tensor_tensor(hm_lo[:], hm_f[:], f32(hm_hi[:]), ALU.subtract).then_inc(hml_done, 1)
                if (s, k) == GATE_GAP:
                    wait(dve, gate_done, it - 1, 1, 1)
                    dve.tensor_copy(sc_m[:], ob[:, 0:NB * EXPERTS].rearrange("q (b e) -> q b e", b=NB)).then_inc(sc_done, 1)
                    wait(dve, sc_done, it - 1, 1, 1)
                    dve.nop(nofuse=True)
                    for b in range(NB):
                        d = dve.max(m8[:, b, :], sc_m[:, b, :])
                    d.then_inc(route, 1)
                    wait(dve, route, it - 1, ROUTE, 1)
                    dve.tensor_tensor(dd[:], m8[:, :, 1], m8[:, :, 0], ALU.subtract).then_inc(dd_done, 1)
                    for b in range(NB):
                        d = dve.max_index(i8[:, b, :], m8[:, b, :], sc_m[:, b, :])
                    d.then_inc(route, 1)
                    wait(dve, route, it - 1, ROUTE, 2)
                    dve.tensor_copy(if_m[:], i8[:, :, 0:2]).then_inc(route, 1)
                    wait(dve, route, it - 1, ROUTE, 3)
                    for i in range(2):
                        dve.tensor_tensor(eq[:, i], iota8[:].unsqueeze(1).to_broadcast([P, NB, EXPERTS]),
                                          if_m[:, :, i:i + 1].to_broadcast([P, NB, EXPERTS]), ALU.is_equal).then_inc(route, 1)

            def probs_m(it, s, k):
                if (s, k) == PROBS_GAP:
                    wait(dve, ee_done, it - 1, 1, 1)
                    dve.tensor_scalar(zz[:], ee[:], 1.0, None, ALU.add).then_inc(route, 1)
                    wait(dve, route, it - 1, ROUTE, 6)
                    dve.reciprocal(rr[:], zz[:]).then_inc(route, 1)
                    wait(dve, route, it - 1, ROUTE, 7)
                    dve.tensor_scalar(pp[:, 0, :], rr[:], 0.5, None, ALU.mult)
                    dve.scalar_tensor_tensor(out=pp[:, 1, :], in0=rr[:], scalar=0.5, in1=ee[:], op0=ALU.mult,
                                             op1=ALU.mult).then_inc(route, 1)
                    wait(dve, route, it - 1, ROUTE, 8)
                    for i in range(2):
                        d = dve.tensor_tensor(eq[:, i], eq[:, i], pp[:, i, :].unsqueeze(2).to_broadcast([P, NB, EXPERTS]), ALU.mult)
                    d.then_inc(route, 1)
                    wait(dve, route, it - 1, ROUTE, 9)
                    dve.tensor_tensor(wts[:], eq[:, 0], eq[:, 1], ALU.add).then_inc(route, 1)

            def expert_m(it, s, k):
                j = m_chunk(s, k)
                if j is not None:
                    wait(dve, th_done, it - 2, CHUNKS, j + 1)
                    if j:
                        wait(dve, g_done, it - 2, CHUNKS, j)
                    dve.scalar_tensor_tensor(out=u_m[:], in0=th_m[:, j % 2, :], scalar=1.0, in1=psb[:], op0=ALU.add,
                                             op1=ALU.mult).then_inc(u_done, 1)
                    wait(dve, u_done, it - 2, CHUNKS, j + 1)
                    wait(dve, mb_done, it - 2, CHUNKS, j + 1)
                    if j >= 4:
                        wait(dve, dn_done, it - 2, EXPERTS, j // 2 - 1)
                    dve.tensor_tensor(g_t[:, j % 4, :], tb[:], u_m[:], ALU.mult).then_inc(g_done, 1)

            def combine_m(it, s, k, after):
                e = m_down(s, k, after)
                if e is not None:
                    wait(dve, dn_done, it - 2, EXPERTS, e + 1)
                    if e == 0:
                        wait(dve, route, it - 2, ROUTE, ROUTE)
                    if e:
                        wait(dve, comb_done, it - 2, EXPERTS, e)
                    for b in range(NB):
                        d = dve.scalar_tensor_tensor(out=acc[:, b, :], in0=ob[:, tok(b)], scalar=wts[:, b, e:e + 1],
                                                     in1=acc[:, b, :], op0=ALU.mult, op1=ALU.add)
                    d.then_inc(comb_done, 1)

            def gap(it, s, k):
                if live(it, -2):
                    combine_m(it, s, k, False)
                    expert_m(it, s, k)
                    combine_m(it, s, k, True)
                if live(it, -1):
                    project_b(it, s, k)
                    unit_b(it, s, k)
                    last_outputs_b(it, s, k)
                    start_m(it, s, k)
                    probs_m(it, s, k)

            def body(it):
                for s in range(STEPS):
                    if live(it):
                        max_a(it, s)
                    gap(it, s, 0)
                    norms_early(it, s)
                    gap(it, s, 1)
                    if live(it, 0 if s < 12 else 1):
                        keys_lo_a(it, s)
                    gap(it, s, 2)
                    norms_late(it, s)
                    norm_next_a(it, s)
                    gap(it, s, 3)
                    if live(it, 0 if s else -1):
                        normalise_a(it if s else it - 1, (s - 1) % STEPS)
                    gap(it, s, 4)
                    second_use(it, s)
                    gap(it, s, 5)

            iterations(dve, body)

        @block.gpsimd
        def _(pool):
            pool.memset(ident[:], 0.0)
            pool.memset(ident_b[:], 0.0)
            pool.memset(mask[:], 0.0)
            pool.memset(half[:], -0.5)
            pool.memset(eps[:], EPS)
            pool.memset(sel_tmp[:], 0.0).then_inc(const_made, 1)
            pool.wait_ge(const_made, 1)
            pool.affine_select(out=ident[:], in_=ident[:], compare_op=ALU.not_equal, fill=1.0, base=0,
                               pattern=[[-1, P]], channel_multiplier=1).then_inc(const_made, 1)
            pool.affine_select(out=ident_b[:], in_=ident_b[:], compare_op=ALU.not_equal, fill=1.0, base=0,
                               pattern=[[-1, P]], channel_multiplier=1)
            pool.affine_select(out=mask[:], in_=mask[:], compare_op=ALU.is_ge, fill=MASKED, base=0,
                               pattern=[[0, Q4], [-1, P]], channel_multiplier=1)
            pool.iota(iota8[:], pattern=[[1, EXPERTS]], base=0, channel_multiplier=0,
                      allow_small_or_imprecise_dtypes=True)
            body_cols = sel_tmp[:, 16:].rearrange("p (h c d) -> p h c d", h=HEADS, c=4)
            for sel, n, picks in ((sel_q, 0, (0, 1)), (sel_k, 1, (0, 2))):
                if n:
                    pool.wait_ge(sel_made, 1)
                    pool.memset(sel_tmp[:], 0.0).then_inc(const_made, 1)
                    pool.wait_ge(const_made, 5)
                for c in picks:
                    d = pool.affine_select(out=body_cols[:, :, c, :], in_=body_cols[:, :, c, :], compare_op=ALU.not_equal,
                                           fill=1.0, base=0, pattern=[[-8, HEADS], [-1, 8]], channel_multiplier=1)
                    d.then_inc(const_made, 1)
                pool.wait_ge(const_made, (4, 7)[n])
                pool.tensor_copy(sel[:], sel_tmp[:]).then_inc(sel_made, 1)
            pool.wait_ge(w_moe_in, 32)
            for i, hi in enumerate((w1_hi, w2_hi)):
                pool.tensor_copy(hi[:], moe_in[:, i, :]).then_inc(moew_done, 1)
            for i, (hi, lo) in enumerate(((w1_hi, w1_lo), (w2_hi, w2_lo))):
                pool.wait_ge(moew_done, i + 1)
                pool.tensor_tensor(lo[:], moe_in[:, i, :], f32(hi[:]), ALU.subtract).then_inc(moew_done, 1)
            pool.wait_ge(moew_done, 4)
            pool.memset(f32(k_diag[:]), 0.0).then_inc(moew_done, 1)

            def root(g, i, b):
                wait(pool, mv_done[i], g, NB, b + 1)
                pool.tensor_tensor(ve_b[:, i, b:b + 1], mv_b[:, i, b, 1:2], eps[:], ALU.add).then_inc(ve_done[i], 1)
                wait(pool, ve_done[i], g, NB, b + 1)
                pool.tensor_tensor(rs_b[:, i, b:b + 1], ve_b[:, i, b:b + 1], half[:], ALU.pow).then_inc(rs_done[i], 1)

            def body(it):
                for s in range(STEPS):
                    if live(it, -1):
                        for bb in B_NORMS.get(s, ()):
                            root(it - 1, 2, bb)
                    g, b = (it, 0) if s == 15 else (it - 1, s + 1)
                    if (s == 15 or s < 3) and live(g):
                        root(g, 0, b)
                        root(g, 1, b)
                        wait(pool, nm_done, g - 1, NB, b + 1)
                        pool.tensor_tensor(yb_res[:, b, :], y_b[:, b % 2, :], bo_b_sb[:], ALU.add).then_inc(ybo_done, 1)
                        wait(pool, ybo_done, g, NB, b + 1)
                        pool.tensor_tensor(xy_sum[:, b, :], yb_res[:, b, :], x_res[:, b, :], ALU.add).then_inc(sum_done, 1)
                    if s < 4 and live(it):
                        if s == 0 and isinstance(it, int) and it == 0:
                            pool.wait_ge(w_small_in, 16 * 12)
                        wait(pool, x_landed, it, 16, 16)
                        if live(it, -1):
                            wait(pool, sum_done, it - 1, NB, s + 1)
                        pool.tensor_tensor(x_res[:, s, :], x_in[:, s, :], bo_a_sb[:], ALU.add).then_inc(xres_set, 1)
                    if s == 9 and live(it, 1):
                        wait(pool, mva_done, it + 1, NB, NB)
                        pool.tensor_tensor(ve_a[:], mv_a[:, :, 1], eps[:].to_broadcast([P, NB]), ALU.add).then_inc(vea_done, 1)
                        wait(pool, vea_done, it + 1, 1, 1)
                        pool.tensor_tensor(rs_a[:], ve_a[:], half[:].to_broadcast([P, NB]), ALU.pow).then_inc(rsa_done, 1)
                    if s == 15 and live(it, 1):
                        wait_use(pool, x1_done, use1, it, 14)
                        wait_use(pool, x2_free, use2, it, 11)
                        pool.nop(nofuse=True)
                        for dst, src in ((ctxc_hi, ctxn_hi), (ctxc_lo, ctxn_lo)):
                            pool.tensor_copy(dst[:], src[:]).then_inc(ctxc_done, 1)

            iterations(pool, body)


_INS = ("x", "ctx_768", "L0_xattn_Wq", "L0_xattn_Wk", "L0_xattn_Wv", "L0_xattn_Wo", "L0_xattn_bo", "L0_ffn_ln1_scale",
        "L0_ffn_ln1_shift", "L0_ffn_wq", "L0_ffn_wk", "L0_ffn_wv", "L0_ffn_wo", "L0_ffn_bo", "L0_ffn_ln2_scale",
        "L0_ffn_ln2_shift", "L0_ffn_gate_w", "L0_ffn_w1", "L0_ffn_w2", "L0_ffn_w3")


def kernel(**inputs):
    import numpy as np
    import concourse.bacc as bacc
    from concourse.bass_utils import run_bass_kernel_spmd

    nc = bacc.Bacc("TRN2", target_bir_lowering=False, num_devices=1)
    arrays, args = {}, []
    for name in _INS:
        a = np.ascontiguousarray(inputs[name])
        arrays[f"in_{name}"] = a
        args.append(nc.dram_tensor(f"in_{name}", a.shape, mybir.dt.from_np(a.dtype), kind="ExternalInput").ap())
    shape = inputs["x"].shape
    out = nc.dram_tensor("out_0", shape, F32, kind="ExternalOutput").ap()
    build(nc, shape[0] // NB, *args, out)
    r = run_bass_kernel_spmd(nc, [arrays], core_ids=[0])
    return r.results[0]["out_0"]
```

```python
from contextlib import ExitStack

import concourse.bass as bass
import concourse.mybir as mybir
from concourse.alu_op_type import AluOpType as ALU

ACT = mybir.ActivationFunctionType
F32 = mybir.dt.float32
F32R = mybir.dt.float32r
BF16 = mybir.dt.bfloat16
U32 = mybir.dt.uint32
AX = mybir.AxisListType.X

P = 128
NB = 4
T = NB * P
STEPS = 16
HEADS = 16
Q4 = 4
DE = 96
DH = 64
EB = 8
EXPERTS = 8
CHUNKS = 16
EPS = 1e-5
MASKED = -1.0e30

B_SLOTS = {6: (4,), 7: (1, 3, 4), 8: (1, 2, 4), 9: (1, 3, 4), 10: (1, 3, 5), 11: (1,), 12: (1, 3), 13: (1, 2, 5)}
PE_TRANSPOSES = (1, 1, 1, 1, 1, 1, 1, 1, 1, 1, 2, 0, 1, 1, 2, 3)
KEYS = (2, 3, 2, 3, 2, 2, 1, 1, 2, 2, 2, 1, 2, 2, 2, 2)
KEYS_LO = (2, 3, 2, 2, 2, 2, 2, 3, 2, 3, 3, 2, 3, 2, 3, 2)
FIRST_USE = (3, 3, 3, 3, 2, 2, 3, 3, 3, 2, 2, 3, 3, 2, 3, 3)
PE_CONTEXT = (4, 4, 4, 4, 4, 4, 4, 4, 4, 4, 4, 4, 4, 5, 5, 3)
NORMALISE = (4, 5, 5, 4, 4, 4, 4, 4, 4, 4, 4, 4, 5, 3, 5, 5)
NORMS_EARLY = (1, 1, 1, 1, 0, 1, 1, 1, 1, 1, 1, 1, 1, 2, 1, 0)
NORMS_LATE = (3, 3, 2, 2, 2, 3, 4, 3, 4, 3, 4, 3, 3, 2, 3, 3)
NORMS_NEXT = (3, 2, 3, 3, 3, 3, 3, 3, 3, 5, 3, 2, 3, 3, 4, 4)
PT_COPY = (1, 0, 1, 0, 0, -1, 0, 0, 0, 0, 1, 0, 1, 0, 0, 1)
M_PLACES = (((0, 0), (0, 1), (0, 3), (0, 3), (0, 4), (1, 0), (1, 1), (1, 1),
            (1, 3), (1, 3), (1, 4), (2, 0), (2, 1), (2, 1), (2, 3), (2, 3),
            (2, 4), (3, 0), (3, 1), (3, 1), (3, 3), (3, 3), (3, 4), (4, 1)),
            ((1, 2), (1, 5), (2, 3), (2, 4), (3, 0), (3, 2), (3, 2), (4, 0),
            (4, 1), (4, 2), (4, 4), (5, 2), (5, 2), (5, 3), (5, 5), (6, 1),
            (6, 5), (7, 2), (7, 2), (7, 5), (8, 2), (8, 2), (8, 3), (9, 0)),
            ((0, 1), (0, 2), (0, 4), (0, 5), (1, 0), (1, 0), (1, 1), (1, 2),
            (1, 3), (1, 3), (1, 5), (2, 1), (2, 1), (2, 1), (2, 3), (2, 4),
            (2, 4), (2, 4), (2, 5), (3, 0), (3, 1), (3, 2), (3, 2), (3, 5)))
M_LAGS = (1, 1, 2)
HBT_GAP, QK_GAP, V_GAP = (4, 0), (4, 2), (4, 2)
HMT_GAP, GATE_GAP, EE_GAP, PROBS_GAP = (14, 5), (15, 1), (15, 3), (15, 3)
STACK_GAPS = ((4, 5), (5, 1), (5, 2), (5, 4))
B_OUT_T = {9: (0,), 11: (1,)}
B_OUT_W = {10: (0,), 12: (1,)}
LAST_T_GAP, LAST_W_GAP = (13, 5), (14, 0)
B_NORMS = {11: (0,), 13: (1,), 14: (2, 3)}
FIRST_LOOP, LAST_LOOP = 2, 6


def b_slot(s, k):
    if k not in B_SLOTS.get(s, ()):
        return None
    return sum(len(B_SLOTS[t]) for t in B_SLOTS if t < s) + B_SLOTS[s].index(k)


def b_bank(w, alone):
    if alone:
        return w % 2
    for s, gaps in B_SLOTS.items():
        if w < len(gaps):
            return w % 2
        w -= len(gaps)


def b_before(w, alone):
    return max([v + 1 for v in range(w) if b_bank(v, alone) == b_bank(w, alone)], default=0)


def b_before_a(s):
    w0 = sum(len(B_SLOTS[t]) for t in B_SLOTS if t < s - 1)
    return max([w + 1 for w in range(w0, min(w0 + len(B_SLOTS.get(s - 1, ())), STEPS)) if b_bank(w, False)], default=0)


def m_order(lag):
    pieces = []
    for j in range(CHUNKS + lag):
        if j < CHUNKS:
            pieces.append(("chunk", j))
        if j > lag and (j - lag) % 2:
            pieces.append(("down", (j - lag) // 2))
    return pieces + ([("down", EXPERTS - 1)] if ("down", EXPERTS - 1) not in pieces else [])


def m_pieces(mode, s, k):
    return [piece for piece, place in zip(m_order(M_LAGS[mode]), M_PLACES[mode]) if place == (s, k)]


def build(nc, n_groups, x, ctx, Wq, Wk, Wv, Wo, bo_a, ln1_s, ln1_b, wq, wk, wv, wo, bo_b,
          ln2_s, ln2_b, gate_w, w1, w2, w3, out):
    NG = n_groups
    x_v = x.rearrange("(g b) s d -> g s b d", b=NB)
    ctx_v = ctx.rearrange("(g b) s d -> g s b d", b=NB)
    out_v = out.rearrange("(g b) s d -> g s b d", b=NB)

    def live(it, d=0):
        return not isinstance(it, int) or 0 <= it + d < NG

    def due(it, per, n):
        v = it * per + n
        return v if not isinstance(it, int) or v > 0 else None

    def use1(it, s):
        v = live(it) if s + 1 < STEPS else live(it, 1)
        o = live(it) if s >= 2 else live(it, -1)
        return v or o

    def wo_a(it, s):
        return live(it) if s >= 2 else live(it, -1)

    def act_use2(it, s):
        return (s >= 8 and live(it, 1)) or (s in B_OUT_T and live(it, -1))

    def dve_use2(it, s):
        return (s >= 8 and live(it, 1)) or wo_a(it, s) or (s in B_OUT_W and live(it, -1))

    def use2(it, s):
        return act_use2(it, s) or dve_use2(it, s)

    def both_use2(it, s):
        return act_use2(it, s) and dve_use2(it, s)

    def through(present, it, s):
        back = 0
        if s < 0:
            s, back = s + STEPS, 1
        if isinstance(it, int):
            it -= back
            return sum(bool(present(i, t)) for i in range(-1, it + 1) for t in range(STEPS) if i < it or t <= s)
        mid = FIRST_LOOP + 1
        per = sum(bool(present(mid, t)) for t in range(STEPS))
        before = through(present, FIRST_LOOP - 1, STEPS - 1)
        here = sum(bool(present(mid, t)) for t in range(s + 1))
        return it * per + (before - (FIRST_LOOP + back) * per + here)

    def uses(present, it, s):
        v = through(present, it, s)
        return v if not isinstance(it, int) or v > 0 else None

    def iterations(eng, body):
        for it in range(-1, FIRST_LOOP):
            body(it)
        with eng.Fori(FIRST_LOOP, LAST_LOOP + 1) as it:
            body(it)
        for it in range(LAST_LOOP + 1, NG + 2):
            body(it)

    es = ExitStack()
    with es:
        def sb(name, shape, dt=F32):
            return es.enter_context(nc.sbuf_tensor(name, shape, dt))

        def at(name, shape, dt, offset):
            return nc.alloc_sbuf_tensor_at(name, shape, dt, offset=offset)

        def sem(name):
            return es.enter_context(nc.semaphore(name))

        ident = sb("ident", [P, P])
        ident_b = sb("ident_b", [P, P], BF16)
        mask = sb("mask", [P, Q4, P], BF16)
        half = sb("half", [P, 1])
        eps = sb("eps", [P, 1])
        iota8 = sb("iota8", [P, EXPERTS])
        mt_hi = sb("mt_hi", [DE, HEADS, P], F32R)
        mt_lo = sb("mt_lo", [DE, HEADS, P], F32R)
        wv_hi = sb("wv_hi", [DE, HEADS * DH], F32R)
        wv_lo = sb("wv_lo", [DE, HEADS * DH], F32R)
        wo_sb = sb("wo_sb", [P, 8, P])
        bo_a_sb = sb("bo_a_sb", [P, P])
        bo_b_sb = sb("bo_b_sb", [P, P])
        ln_sb = sb("ln_sb", [P, 4])
        qkw_hi = sb("qkw_hi", [P, 2, P], F32R)
        qkw_lo = sb("qkw_lo", [P, 2, P], F32R)
        vw_sb = sb("vw_sb", [P, P])
        ow_sb = sb("ow_sb", [P, P])
        gate_sb = sb("gate_sb", [P, EXPERTS])
        sel_q = sb("sel_q", [P, 16 + HEADS * 32], F32R)
        sel_k = sb("sel_k", [P, 16 + HEADS * 32], F32R)
        w1_hi = sb("w1_hi", [P, CHUNKS * P], F32R)
        w1_lo = sb("w1_lo", [P, CHUNKS * P], F32R)
        w2_hi = sb("w2_hi", [P, CHUNKS * P], F32R)
        w2_lo = sb("w2_lo", [P, CHUNKS * P], F32R)
        w3_sb = sb("w3_sb", [P, CHUNKS, P])

        x_in = sb("x_in", [P, NB, P])
        x_res = sb("x_res", [P, NB, P])
        ctx_in = sb("ctx_in", [P, NB, DE])
        ctxn_hi = sb("ctxn_hi", [DE, T], F32R)
        ctxn_lo = sb("ctxn_lo", [DE, T], F32R)
        ctxc_hi = sb("ctxc_hi", [DE, T], F32R)
        ctxc_lo = sb("ctxc_lo", [DE, T], F32R)
        ha = sb("ha", [P, 2, P])
        hat_hi = sb("hat_hi", [P, NB, P], F32R)
        hat_lo = sb("hat_lo", [P, NB, P], F32R)
        g_hi = sb("g_hi", [P, 2, Q4, T], F32R)
        g_hi0 = nc.sbuf_base - 16 * 1024
        g_lo = sb("g_lo", [P, 2, Q4, T], F32R)
        g_lo0 = nc.sbuf_base - 16 * 1024
        v_a = sb("v_a", [P, 4, Q4, DH + 1])
        nmax_a = sb("nmax_a", [P, 2, Q4])
        p_a = sb("p_a", [P, 2, Q4, P])
        pt_a = sb("pt_a", [P, Q4, P])
        rden_a = sb("rden_a", [P, 2, Q4])
        o_a = sb("o_a", [P, 2, Q4 * DH])
        ot_a = sb("ot_a", [P, 2, 2, P])
        mv_a = sb("mv_a", [P, NB, 2])
        st_a = sb("st_a", [P, NB, 6])
        ve_a = sb("ve_a", [P, NB])
        rs_a = sb("rs_a", [P, NB])

        y_b = sb("y_b", [P, 2, P])
        yb_res = sb("yb_res", [P, NB, P])
        xy_sum = sb("xy_sum", [P, NB, P])
        acc = sb("acc", [P, NB, P])
        nrm = sb("nrm", [P, NB, P])
        st_b = sb("st_b", [P, NB, 6])
        mv_b = sb("mv_b", [P, 3, NB, 2])
        ve_b = sb("ve_b", [P, 3, NB])
        rs_b = sb("rs_b", [P, 3, NB])
        k_diag = sb("k_diag", [P, 2, Q4, Q4, P], F32R)
        moe_in = at("moe_in", [P, 2, CHUNKS * P], F32, nc.sbuf_base - 16 * 1024)
        v_b = sb("v_b", [P, NB, HEADS, EB + 1])
        nmax_b = sb("nmax_b", [P, 2, Q4])
        p_b = sb("p_b", [P, 2, Q4, P])
        pt_b = sb("pt_b", [P, Q4, P])
        rden_b = sb("rden_b", [P, HEADS])
        o_b = sb("o_b", [P, 2, P])
        ot_b = sb("ot_b", [P, 2, P])
        sc_m = sb("sc_m", [P, NB, EXPERTS])
        m8 = sb("m8", [P, NB, 8])
        i8 = sb("i8", [P, NB, 8], U32)
        if_m = sb("if_m", [P, NB, 2])
        dd = sb("dd", [P, NB])
        ee = sb("ee", [P, NB])
        zz = sb("zz", [P, NB])
        rr = sb("rr", [P, NB])
        pp = sb("pp", [P, 2, NB])
        eq = sb("eq", [P, 2, NB, EXPERTS])
        wts = sb("wts", [P, NB, EXPERTS])

        KB = 1024
        arena = sb("arena", [P, 24 * KB // 4])
        a0 = nc.sbuf_base - 24 * KB
        q_stk = at("q_stk", [P, Q4, T], F32R, a0)
        g_t = at("g_t", [P, 4, T], F32, a0)
        k_stk = at("k_stk", [P, Q4, T], F32R, a0 + 8 * KB)
        hb_f = at("hb_f", [P, T], F32, a0 + 8 * KB)
        hb_hi = at("hb_hi", [P, T], F32R, a0 + 10 * KB)
        hb_lo = at("hb_lo", [P, T], F32R, a0 + 12 * KB)
        hm_f = at("hm_f", [P, T], F32, a0 + 8 * KB)
        th_m = at("th_m", [P, 2, T], F32, a0 + 10 * KB)
        u_m = at("u_m", [P, T], F32, a0 + 14 * KB)
        qk_hi = at("qk_hi", [P, 2, T], F32R, a0 + 16 * KB)
        qk_lo = at("qk_lo", [P, 2, T], F32R, a0 + 20 * KB)
        hm_hi = at("hm_hi", [P, T], F32R, a0 + 16 * KB)
        hm_lo = at("hm_lo", [P, T], F32R, a0 + 18 * KB)
        eo_m = at("eo_m", [P, 2, NB, P], F32, a0 + 20 * KB)
        arena_m = (hm_f, hm_hi, hm_lo, th_m, u_m, g_t, eo_m)
        spread_m = (at("hm_f2", [P, T], F32, g_hi0), at("hm_hi2", [P, T], F32R, g_hi0 + 2 * KB),
                    at("hm_lo2", [P, T], F32R, g_hi0 + 4 * KB), at("th_m2", [P, 2, T], F32, g_hi0 + 8 * KB),
                    at("u_m2", [P, T], F32, g_hi0 + 6 * KB), at("g_t2", [P, 4, T], F32, g_lo0),
                    at("eo_m2", [P, 2, NB, P], F32, g_lo0 + 8 * KB))
        wq_in = at("wq_in", [P, HEADS * DH], F32, a0)
        wk_in = at("wk_in", [DE, HEADS * DH], F32, a0 + 4 * KB)
        wv_in = at("wv_in", [DE, HEADS * DH], F32, a0 + 8 * KB)
        wqt = at("wqt", [P, 8, P], F32, a0 + 12 * KB)
        wkt = at("wkt", [P, 8, DE], F32, a0 + 16 * KB)
        qkw_in = at("qkw_in", [P, 2, P], F32, a0 + 19 * KB)
        sel_tmp = at("sel_tmp", [P, 16 + HEADS * 32], F32, a0 + 20 * KB)

        ps = {n: es.enter_context(nc.psum_tensor(f"ps_{n}", [P, 512], F32))
              for n in ("sa", "ta", "ga", "oa", "x", "sb", "tb", "ob")}
        sa, ta, ga, oa, px, psb, tb, ob = (ps[n] for n in ("sa", "ta", "ga", "oa", "x", "sb", "tb", "ob"))

        def spread(it):
            return isinstance(it, int) and it == NG

        def next_it(it):
            return it + 1 if isinstance(it, int) else it

        def mode(it):
            return (1 if it == NG else 2 if it == NG + 1 else 0) if isinstance(it, int) else 0

        def m_gap(it, s, k, chunk, down):
            for g_it, t in ((it, s),) + (((it + 1, -1),) if s == STEPS - 1 else ()):
                if live(g_it, -2):
                    for kind, n in m_pieces(mode(g_it), t, k):
                        (chunk if kind == "chunk" else down)(g_it, n)

        def m_tiles(it):
            return spread_m if spread(it) else arena_m

        def m_banks(it, n):
            if spread(it):
                return ga, ta, oa
            return (ga, ta, oa) if m_ring(it) == 2 and n % 2 else (psb, tb, ob)

        def m_ring(it):
            return 2 if isinstance(it, int) and it == NG + 1 else 1

        w_attn_in = sem("w_attn_in")
        w_small_in = sem("w_small_in")
        w_moe_in = sem("w_moe_in")
        w3_in = sem("w3_in")
        x_landed = sem("x_landed")
        ctx_landed = sem("ctx_landed")
        k_placed = [sem(f"k_placed{i}") for i in range(2)]
        out_stored = sem("out_stored")
        const_made = sem("const_made")
        sel_made = sem("sel_made")
        wt_done = sem("wt_done")
        wqt_done = sem("wqt_done")
        wkt_done = sem("wkt_done")
        m_done = sem("m_done")
        mth_done = sem("mth_done")
        mtl_done = sem("mtl_done")
        wvh_done = sem("wvh_done")
        wvl_done = sem("wvl_done")
        qkwh_done = sem("qkwh_done")
        qkwl_done = sem("qkwl_done")
        moew_done = sem("moew_done")
        ones_done = sem("ones_done")

        sa_done = sem("sa_done")
        ta_done = sem("ta_done")
        ga_done = sem("ga_done")
        oa_done = sem("oa_done")
        x1_done = sem("x1_done")
        x2_done = sem("x2_done")
        maxa_done = sem("maxa_done")
        expa_done = sem("expa_done")
        pta_done = sem("pta_done")
        gh_done = sem("gh_done")
        gl_done = sem("gl_done")
        va_done = sem("va_done")
        ota_done = sem("ota_done")
        rdena_done = sem("rdena_done")
        oa_norm = sem("oa_norm")
        x2_act = sem("x2_act")
        x2_free = sem("x2_free")
        sta_done = sem("sta_done")
        mva_done = sem("mva_done")
        vea_done = sem("vea_done")
        rsa_done = sem("rsa_done")
        ha_done = sem("ha_done")
        xres_set = sem("xres_set")
        ctxc_done = sem("ctxc_done")

        st_done = [sem(f"st{i}_done") for i in range(3)]
        mv_done = [sem(f"mv{i}_done") for i in range(3)]
        ve_done = [sem(f"ve{i}_done") for i in range(3)]
        rs_done = [sem(f"rs{i}_done") for i in range(3)]
        y_done = sem("y_done")
        ybo_done = sem("ybo_done")
        sum_done = sem("sum_done")
        nb_done = sem("nb_done")
        nm_done = sem("nm_done")
        hbt_done = sem("hbt_done")
        hbf_done = sem("hbf_done")
        hbh_done = sem("hbh_done")
        hbl_done = sem("hbl_done")
        qk_done = sem("qk_done")
        qkh_done = sem("qkh_done")
        qkl_done = sem("qkl_done")
        vb_done = sem("vb_done")
        vals_done = sem("vals_done")
        stk_done = sem("stk_done")
        stk_act = sem("stk_act")
        stk_dve = sem("stk_dve")
        sb_done = sem("sb_done")
        tb_done = sem("tb_done")
        ob_done = sem("ob_done")
        maxb_done = sem("maxb_done")
        expb_done = sem("expb_done")
        ptb_done = sem("ptb_done")
        rdenb_done = sem("rdenb_done")
        ob_norm = sem("ob_norm")
        last_t_done = sem("last_t_done")
        last_ot = sem("last_ot")
        last_w_done = sem("last_w_done")
        y1_done = sem("y1_done")

        hmt_done = sem("hmt_done")
        hmf_done = sem("hmf_done")
        hmh_done = sem("hmh_done")
        hml_done = sem("hml_done")
        gate_done = sem("gate_done")
        sc_done = sem("sc_done")
        route = sem("route")
        dd_done = sem("dd_done")
        ee_done = sem("ee_done")
        ma_done = sem("ma_done")
        mb_done = sem("mb_done")
        th_done = sem("th_done")
        u_done = sem("u_done")
        g_done = sem("g_done")
        dn_done = sem("dn_done")
        eo_done = sem("eo_done")
        comb_done = sem("comb_done")
        ROUTE = 10

        block = es.enter_context(nc.Block())

        def f32(ap):
            return ap.bitcast(F32)

        def tok(b):
            return slice(b * P, (b + 1) * P)

        @block.sync
        def _(sp):
            sp.dma_start(wq_in[:], Wq).then_inc(w_attn_in, 16)
            sp.dma_start(wk_in[:], Wk).then_inc(w_attn_in, 16)
            sp.dma_start(ctx_in[:], ctx_v[0]).then_inc(ctx_landed, 16)
            sp.dma_start(x_in[:], x_v[0]).then_inc(x_landed, 16)
            sp.dma_start(wv_in[:], Wv).then_inc(w_attn_in, 16)
            sp.dma_start(wo_sb[:], Wo.rearrange("(t p) d -> p t d", p=P)).then_inc(w_small_in, 16)
            for dst, src in ((bo_a_sb, bo_a), (bo_b_sb, bo_b)):
                sp.dma_start(dst[:], src.rearrange("(a d) -> a d", a=1).to_broadcast([P, P])).then_inc(w_small_in, 16)
            for i, src in enumerate((ln1_s, ln1_b, ln2_s, ln2_b)):
                sp.dma_start(ln_sb[:, i:i + 1], src.rearrange("(d a) -> d a", a=1)).then_inc(w_small_in, 16)
            for dst, src in ((qkw_in[:, 0, :], wq), (qkw_in[:, 1, :], wk), (vw_sb[:], wv), (ow_sb[:], wo),
                             (gate_sb[:], gate_w)):
                sp.dma_start(dst, src).then_inc(w_small_in, 16)
            for i, src in enumerate((w1, w2)):
                sp.dma_start(moe_in[:, i, :].rearrange("d (e h) -> d e h", e=EXPERTS),
                             src.rearrange("e d h -> d e h")).then_inc(w_moe_in, 16)
            sp.dma_start(w3_sb[:], w3.rearrange("e (c p) d -> p (e c) d", p=P)).then_inc(w3_in, 16)

            def store(g):
                sp.wait_ge(comb_done, g * EXPERTS + EXPERTS)
                sp.dma_start(out_v[g], acc[:]).then_inc(out_stored, 16)

            def body(it):
                if live(it, 1) and not (isinstance(it, int) and it < 0):
                    if (n_due := uses(use2, it, -5)) is not None:
                        sp.wait_ge(x2_done, n_due)
                    sp.dma_start(ctx_in[:], ctx_v[it + 1]).then_inc(ctx_landed, 16)
                    sp.wait_ge(xres_set, it * NB + NB)
                    sp.wait_ge(ha_done, it * NB + NB)
                    sp.dma_start(x_in[:], x_v[it + 1]).then_inc(x_landed, 16)
                if live(it, -2) and not spread(it):
                    store(it - 2)
                if live(it, -1):
                    sp.wait_ge(stk_act, (it - 1) * Q4 + 2)
                    sp.wait_ge(stk_dve, (it - 1) * Q4 + 2)
                    for b in range(NB):
                        if b == 3 and spread(it):
                            store(it - 2)
                        if (n_due := due(it - 1, STEPS, Q4 * (b - 1))) is not None:
                            sp.wait_ge(sb_done, n_due)
                        for hh in range(Q4):
                            r = slice(32 * hh, 32 * hh + 32)
                            sp.dma_start(f32(k_diag[r, b % 2, :, hh, :]), f32(k_stk[r, :, tok(b)])).then_inc(k_placed[b % 2], 16)

            iterations(sp, body)
            sp.wait_ge(out_stored, 16 * NG)

        @block.tensor
        def _(pe):
            def split3(dst, l_hi, l_lo, r_hi, r_lo):
                pe.matmul(dst, l_hi, r_hi, start=True, stop=False)
                pe.matmul(dst, l_hi, r_lo, start=False, stop=False)
                return pe.matmul(dst, l_lo, r_hi, start=False, stop=True)

            pe.wait_ge(const_made, 2)
            pe.wait_ge(w_attn_in, 48)
            for t in range(8):
                pe.transpose((sa if t < 4 else ta)[:, tok(t % 4)], wq_in[:, tok(t)], ident[:])
            for t in range(8):
                mm = pe.transpose((ga if t < 4 else oa)[:, (t % 4) * DE:(t % 4 + 1) * DE], wk_in[:, tok(t)],
                                  ident[0:DE, 0:DE])
            mm.then_inc(wt_done, 1)

            def products_m(i):
                if i == 0:
                    pe.wait_ge(wqt_done, 2)
                    pe.wait_ge(wkt_done, 2)
                for t in range(4):
                    h = 8 * (i // 2) + i % 2 + 2 * t
                    r = slice(64 * (h % 2), 64 * (h % 2) + 64)
                    mm = pe.matmul((psb, tb, ob, sa)[i][0:DE, tok(t)], wkt[r, h // 2, :], wqt[r, h // 2, :],
                                   start=True, stop=True)
                mm.then_inc(m_done, 1)

            def scores_a(it, u):
                hq, b = divmod(u, NB)
                if b == 0:
                    pe.wait_ge(gl_done, it * HEADS + Q4 * hq + Q4)
                if hq == 0:
                    if (n_due := uses(use2, it, b - 4)) is not None:
                        pe.wait_ge(x2_free, n_due)
                if (n_due := due(it, STEPS, u)) is not None:
                    pe.wait_ge(expa_done, n_due)
                if b_before_a(u) and live(it, -1):
                    pe.wait_ge(expb_done, (it - 1) * STEPS + b_before_a(u))
                g = [t[:, hq % 2, :, tok(b)] for t in (g_hi, g_lo)]
                split3(sa[:].rearrange("q (h k) -> q h k", h=Q4), hat_hi[:, b, :], hat_lo[:, b, :], *g).then_inc(sa_done, 1)

            def transposes_a(it, u):
                pe.wait_ge(expa_done, it * STEPS + u + 1)
                if (n_due := due(it, STEPS, u)) is not None:
                    pe.wait_ge(pta_done, n_due)
                for h in range(Q4):
                    mm = pe.transpose(ta[:, tok(h)], p_a[:, u % 2, h, :], ident[:])
                mm.then_inc(ta_done, 1)

            def keys_a(it, s):
                j = (s + Q4) % HEADS
                if s == 12:
                    if (n_due := uses(use2, it, 11)) is not None:
                        pe.wait_ge(x2_free, n_due)
                    if isinstance(it, int) and it == -1:
                        pe.wait_ge(mtl_done, 4)
                if s == 4:
                    if (n_due := due(it, 2, 2)) is not None:
                        pe.wait_ge(ctxc_done, n_due)
                if (n_due := due(it, HEADS, s + Q4)) is not None:
                    pe.wait_ge(gl_done, n_due)
                c = (ctxc_hi, ctxc_lo) if 4 <= s < 12 else (ctxn_hi, ctxn_lo)
                split3(ga[:], mt_hi[:, j, :], mt_lo[:, j, :], c[0][:], c[1][:]).then_inc(ga_done, 1)

            def values_and_output_t_a(it, s):
                if not use1(it, s):
                    return
                if (n_due := uses(use2, it, s - 1)) is not None:
                    pe.wait_ge(x2_free, n_due)
                if isinstance(it, int) and it == 0 and s in (1, 2):
                    pe.wait_ge(va_done, s + 1)
                mm = None
                if isinstance(it, int) and it == -1:
                    pe.wait_ge(wvl_done, 1)
                if live(it) if s + 1 < STEPS else live(it, 1):
                    hq, b = divmod((s + 1) % STEPS, NB)
                    c = (ctxc_hi, ctxc_lo) if 4 <= s < 15 else (ctxn_hi, ctxn_lo)
                    w = slice(hq * Q4 * DH, (hq + 1) * Q4 * DH)
                    mm = split3(px[:, 0:Q4 * DH], c[0][:, tok(b)], c[1][:, tok(b)], wv_hi[:, w], wv_lo[:, w])
                if wo_a(it, s):
                    if (n_due := due(it, STEPS, s - 1)) is not None:
                        pe.wait_ge(oa_norm, n_due)
                    for i in range(2):
                        mm = pe.transpose(px[:, tok(2 + i)], o_a[:, s % 2, tok(i)], ident[:])
                mm.then_inc(x1_done, 1)

            def context_a(it, u):
                pe.wait_ge(pta_done, it * STEPS + u + 1)
                pe.wait_ge(va_done, it * STEPS + u + 1)
                if (n_due := due(it, STEPS, u)) is not None:
                    pe.wait_ge(oa_norm, n_due)
                for h in range(Q4):
                    mm = pe.matmul(oa[:, h * (DH + 1):(h + 1) * (DH + 1)], pt_a[:, h, :], v_a[:, u % 4, h, :],
                                   start=True, stop=True)
                mm.then_inc(oa_done, 1)

            def second_use(it, s):
                if not use2(it, s):
                    return
                if use1(it, s):
                    last = (NG - it) * STEPS if isinstance(it, int) else s + 2
                    if (n_due := due(it, STEPS, min(s + 2, last))) is not None:
                        pe.wait_ge(va_done, n_due)
                    if wo_a(it, s):
                        if (n_due := due(it, STEPS, s - 1)) is not None:
                            pe.wait_ge(ota_done, n_due)
                else:
                    if (n_due := uses(use2, it, s - 1)) is not None:
                        pe.wait_ge(x2_free, n_due)
                mm = None
                if 8 <= s < 12 and live(it, 1):
                    if s == 8:
                        pe.wait_ge(ctx_landed, (it + 1) * 16 + 16)
                    mm = pe.transpose(px[0:DE, tok(1)], ctx_in[:, s - 8, :], ident[:])
                if s >= 12 and live(it, 1):
                    pe.wait_ge(ha_done, (it + 1) * NB + s - 12 + 1)
                    mm = pe.transpose(px[:, tok(1)], ha[:, s % 2, :], ident[:])
                if live(it, -1):
                    for i, b in enumerate(B_OUT_T.get(s, ())):
                        pe.wait_ge(ob_norm, (it - 1) * NB + b + 1)
                        mm = pe.transpose(px[:, tok(2 + i)], o_b[:, b % 2, :], ident[:])
                    for i, b in enumerate(B_OUT_W.get(s, ())):
                        mm = pe.matmul(px[:, tok(2 + i)], ot_b[:, b % 2, :], ow_sb[:], start=True, stop=True)
                if wo_a(it, s):
                    hq = (s - 2) % STEPS // NB
                    for i in range(2):
                        mm = pe.matmul(px[:, tok(0)], ot_a[:, s % 2, i, :], wo_sb[:, 2 * hq + i, :],
                                       start=(i == 0), stop=(i == 1))
                mm.then_inc(x2_done, 1)

            def project_b(it, s, k):
                if (s, k) == HBT_GAP:
                    pe.wait_ge(nb_done, (it - 1) * NB + NB)
                    if not spread(it):
                        if (n_due := due(it - 1, CHUNKS, 0)) is not None:
                            pe.wait_ge(g_done, n_due)
                    for b in range(NB):
                        mm = pe.transpose(tb[:, tok(b)], nrm[:, b, :], ident[:])
                    mm.then_inc(hbt_done, 1)
                if (s, k) == QK_GAP:
                    pe.wait_ge(hbl_done, it)
                    if not spread(it):
                        if (n_due := due(it - 1, CHUNKS, 0)) is not None:
                            pe.wait_ge(u_done, n_due)
                        if (n_due := due(it - 1, EXPERTS, 0)) is not None:
                            pe.wait_ge(eo_done, n_due)
                    for i, bank in enumerate((psb, ob)):
                        split3(bank[:], qkw_hi[:, i, :], qkw_lo[:, i, :], hb_hi[:], hb_lo[:]).then_inc(qk_done, 1)
                if (s, k) == V_GAP:
                    for b in range(NB):
                        mm = pe.matmul(tb[:, tok(b)], hb_f[:, tok(b)], vw_sb[:], start=True, stop=True)
                    mm.then_inc(vb_done, 1)
                if (s, k) in STACK_GAPS:
                    n = STACK_GAPS.index((s, k))
                    for i in (2 * n, 2 * n + 1):
                        side, t = (1, 0)[i // 4], i % 4
                        bank, sel = (psb, ob, tb)[i % 3], (sel_q, sel_k)[side]
                        if i < 2:
                            pe.wait_ge(qkl_done, (it - 1) * 2 + 2)
                        elif i == 2:
                            pe.wait_ge(vals_done, it)
                        else:
                            pe.wait_ge((stk_dve, stk_act)[i % 2], (it - 1) * Q4 + (i - 3) // 2 + 1)
                        c0, shift = 16 + P * t, (16, 8)[side]
                        pe.matmul(bank[:], sel[:, c0:c0 + P], qk_hi[:, side, :], start=True, stop=False)
                        pe.matmul(bank[:], sel[:, c0 - shift:c0 - shift + P], qk_lo[:, side, :],
                                  start=False, stop=True).then_inc(stk_done, 1)

            def unit_b(it, s, k):
                w = b_slot(s, k)
                if w is None:
                    return
                if w < STEPS:
                    b, t = divmod(w, Q4)
                    if w == 0:
                        pe.wait_ge(stk_act, (it - 1) * Q4 + Q4)
                        pe.wait_ge(stk_dve, (it - 1) * Q4 + Q4)
                    if t == 0:
                        pe.wait_ge(k_placed[b % 2], (it - 1) * 128 + 64 * (b // 2 + 1))
                    if (n_due := due(it - 1, STEPS, b_before(w, not live(it)))) is not None:
                        pe.wait_ge(expb_done, n_due)
                    if b_bank(w, not live(it)) and live(it):
                        pe.wait_ge(expa_done, it * STEPS + s + 1)
                    bank = (psb, sa)[b_bank(w, not live(it))]
                    pe.matmul(bank[:], ident_b[:], mask[:], start=True, stop=False)
                    pe.matmul(bank[:].rearrange("q (h k) -> q h k", h=Q4), q_stk[:, t, tok(b)],
                              k_diag[:, b % 2, t, :, :], start=False, stop=True).then_inc(sb_done, 1)
                if 2 <= w <= STEPS + 1:
                    if (n_due := due(it - 1, STEPS, w - 1)) is not None:
                        pe.wait_ge(expb_done, n_due)
                    if w == 2:
                        pe.wait_ge(stk_dve, (it - 1) * Q4 + Q4)
                    if (n_due := due(it - 1, STEPS, w - 2)) is not None:
                        pe.wait_ge(ptb_done, n_due)
                    for h in range(Q4):
                        mm = pe.transpose(tb[:, tok(h)], p_b[:, w % 2, h, :], ident[:])
                    mm.then_inc(tb_done, 1)
                if w >= 3:
                    b, t = divmod(w - 3, Q4)
                    if w == 3:
                        pe.wait_ge(vals_done, it)
                    if t == 0:
                        if (n_due := due(it - 1, NB, b)) is not None:
                            pe.wait_ge(ob_norm, n_due)
                    if (n_due := due(it - 1, STEPS, w - 2)) is not None:
                        pe.wait_ge(ptb_done, n_due)
                    for h in range(Q4):
                        c = (EB + 1) * (Q4 * t + h)
                        mm = pe.matmul(ob[:, c:c + EB + 1], pt_b[:, h, :], v_b[:, b, Q4 * t + h, :], start=True, stop=True)
                    mm.then_inc(ob_done, 1)

            def last_outputs_b(it, s, k):
                if (s, k) == LAST_T_GAP:
                    pe.wait_ge(ob_norm, (it - 1) * NB + NB)
                    pe.wait_ge(ptb_done, (it - 1) * STEPS + STEPS)
                    for i in range(2):
                        mm = pe.transpose(tb[:, tok(i)], o_b[:, i, :], ident[:])
                    mm.then_inc(last_t_done, 1)
                if (s, k) == LAST_W_GAP:
                    pe.wait_ge(last_ot, it)
                    pe.wait_ge(expb_done, (it - 1) * STEPS + STEPS)
                    for i in range(2):
                        mm = pe.matmul(psb[:, tok(i)], ot_b[:, i, :], ow_sb[:], start=True, stop=True)
                    mm.then_inc(last_w_done, 1)

            def start_m(it, s, k):
                hm_f = m_tiles(next_it(it))[0]
                if (s, k) == HMT_GAP:
                    pe.wait_ge(nm_done, (it - 1) * NB + NB)
                    pe.wait_ge(last_ot, it)
                    for b in range(NB):
                        mm = pe.transpose(tb[:, tok(b)], nrm[:, b, :], ident[:])
                    mm.then_inc(hmt_done, 1)
                if (s, k) == GATE_GAP:
                    pe.wait_ge(hmf_done, it)
                    pe.wait_ge(ob_norm, (it - 1) * NB + NB)
                    for b in range(NB):
                        mm = pe.matmul(ob[:, b * EXPERTS:(b + 1) * EXPERTS], hm_f[:, tok(b)], gate_sb[:],
                                       start=True, stop=True)
                    mm.then_inc(gate_done, 1)

            def expert_m(it, j):
                _, hm_hi, hm_lo = m_tiles(it)[:3]
                w1_bank, w2_bank, _ = m_banks(it, j)
                if j == 0:
                    pe.wait_ge(hml_done, it - 1)
                    pe.wait_ge(expb_done, (it - 2) * STEPS + STEPS)
                    if spread(it):
                        pe.wait_ge(gl_done, NG * HEADS)
                        pe.wait_ge(pta_done, NG * STEPS)
                elif j >= m_ring(it):
                    if (n_due := due(it - 2, CHUNKS, j + 1 - m_ring(it))) is not None:
                        pe.wait_ge(u_done, n_due)
                w = slice(j * P, (j + 1) * P)
                split3(w1_bank[:], w1_hi[:, w], w1_lo[:, w], hm_hi[:], hm_lo[:]).then_inc(ma_done, 1)
                if j >= m_ring(it):
                    if (n_due := due(it - 2, CHUNKS, j + 1 - m_ring(it))) is not None:
                        pe.wait_ge(g_done, n_due)
                split3(w2_bank[:], w2_hi[:, w], w2_lo[:, w], hm_hi[:], hm_lo[:]).then_inc(mb_done, 1)

            def down_m(it, e):
                g_t, out_bank = m_tiles(it)[5], m_banks(it, e)[2]
                if e == 0:
                    pe.wait_ge(sc_done, it - 1)
                    if spread(it):
                        pe.wait_ge(oa_norm, NG * STEPS)
                elif e >= m_ring(it):
                    if (n_due := due(it - 2, EXPERTS, e + 1 - m_ring(it))) is not None:
                        pe.wait_ge(eo_done, n_due)
                pe.wait_ge(g_done, (it - 2) * CHUNKS + 2 * e + 2)
                for b in range(NB):
                    for i in range(2):
                        mm = pe.matmul(out_bank[:, tok(b)], g_t[:, (2 * e + i) % 4, tok(b)], w3_sb[:, 2 * e + i, :],
                                       start=(i == 0), stop=(i == 1))
                mm.then_inc(dn_done, 1)

            def gap(it, s, k):
                m_gap(it, s, k, expert_m, down_m)
                if live(it, -1):
                    project_b(it, s, k)
                    unit_b(it, s, k)
                    last_outputs_b(it, s, k)
                    start_m(it, s, k)

            def body(it):
                if isinstance(it, int) and it == 0:
                    pe.wait_ge(w_small_in, 16 * 12)
                    pe.wait_ge(ones_done, 2)
                if isinstance(it, int) and it == 1:
                    pe.wait_ge(qkwl_done, 1)
                    pe.wait_ge(sel_made, 2)
                    pe.wait_ge(moew_done, 5)
                    pe.wait_ge(w3_in, 16)
                for s in range(STEPS):
                    if live(it):
                        scores_a(it, s)
                    for k in range(6):
                        if k == PE_TRANSPOSES[s] and live(it, 0 if s else -1):
                            transposes_a(it if s else it - 1, (s - 1) % STEPS)
                        if k == KEYS[s] and live(it, 0 if s < 12 else 1):
                            keys_a(it, s)
                        if k == FIRST_USE[s]:
                            values_and_output_t_a(it, s)
                        if k == PE_CONTEXT[s] and live(it, 0 if s else -1):
                            context_a(it if s else it - 1, (s - 1) % STEPS)
                        if k == 5:
                            second_use(it, s)
                        gap(it, s, k)
                    if isinstance(it, int) and it == -1 and 8 <= s < 12:
                        products_m(s - 8)

            iterations(pe, body)

        @block.scalar
        def _(act):
            act.wait_ge(wt_done, 1)
            for i, bank in enumerate((sa, ta)):
                act.activation(wqt[:, 4 * i:4 * i + 4, :], bank[:].rearrange("p (t c) -> p t c", t=4),
                               ACT.Copy).then_inc(wqt_done, 1)

            def products_hi(i):
                h0 = 8 * (i // 2) + i % 2
                act.wait_ge(m_done, i + 1)
                act.activation(mt_hi[:, h0:h0 + 7:2, :], (psb, tb, ob, sa)[i][0:DE, :].rearrange("p (t c) -> p t c", t=4),
                               ACT.Copy, scale=DH ** -0.5).then_inc(mth_done, 1)

            def exp_a(it, u):
                act.wait_ge(maxa_done, it * STEPS + u + 1)
                if (n_due := due(it, STEPS, u - 1)) is not None:
                    act.wait_ge(ta_done, n_due)
                for h in range(Q4):
                    a = act.activation(p_a[:, u % 2, h, :], sa[:, tok(h)], ACT.Exp, bias=nmax_a[:, u % 2, h:h + 1])
                a.then_inc(expa_done, 1)

            def pt_copy_a(it, u):
                act.wait_ge(ta_done, it * STEPS + u + 1)
                if (n_due := due(it, STEPS, u)) is not None:
                    act.wait_ge(oa_done, n_due)
                act.activation(pt_a[:], ta[:].rearrange("p (h q) -> p h q", h=Q4), ACT.Copy).then_inc(pta_done, 1)

            def keys_hi_a(it, s):
                j = (s + Q4) % HEADS
                act.wait_ge(ga_done, it * HEADS + s + Q4 + 1)
                act.activation(g_hi[:, j // Q4 % 2, j % Q4, :], ga[:], ACT.Copy).then_inc(gh_done, 1)

            def first_use(it, s):
                if not use1(it, s):
                    return
                if (n_due := uses(use1, it, s)) is not None:
                    act.wait_ge(x1_done, n_due)
                if live(it) if s + 1 < STEPS else live(it, 1):
                    act.activation(v_a[:, (s + 1) % 4, :, 0:DH], px[:, 0:Q4 * DH].rearrange("p (h d) -> p h d", h=Q4),
                                   ACT.Copy).then_inc(va_done, 1)
                if wo_a(it, s):
                    act.activation(ot_a[:, s % 2, :, :], px[:, 2 * P:4 * P].rearrange("p (i q) -> p i q", i=2),
                                   ACT.Copy).then_inc(ota_done, 1)

            def second_use(it, s):
                if not act_use2(it, s):
                    return
                if (n_due := uses(use2, it, s)) is not None:
                    act.wait_ge(x2_done, n_due)
                a = None
                if 8 <= s < 12 and live(it, 1):
                    if s == 8:
                        if (n_due := due(it, 2, 2)) is not None:
                            act.wait_ge(ctxc_done, n_due)
                    a = act.activation(ctxn_hi[:, tok(s - 8)], px[0:DE, tok(1)], ACT.Copy)
                if s >= 12 and live(it, 1):
                    a = act.activation(hat_hi[:, s - 12, :], px[:, tok(1)], ACT.Copy)
                if live(it, -1):
                    for i, b in enumerate(B_OUT_T.get(s, ())):
                        a = act.activation(ot_b[:, b % 2, :], px[:, tok(2 + i)], ACT.Copy)
                a.then_inc(x2_act if dve_use2(it, s) else x2_free, 1)

            def project_b(it, s, k):
                if (s, k) == HBT_GAP:
                    act.wait_ge(hbt_done, it)
                    act.activation(hb_f[:], tb[:], ACT.Identity, bias=ln_sb[:, 1:2], scale=ln_sb[:, 0:1]).then_inc(hbf_done, 1)
                    act.wait_ge(hbf_done, it)
                    act.activation(hb_hi[:], hb_f[:], ACT.Copy).then_inc(hbh_done, 1)
                if (s, k) == QK_GAP:
                    for i, bank in enumerate((psb, ob)):
                        act.wait_ge(qk_done, (it - 1) * 2 + i + 1)
                        act.activation(qk_hi[:, i, :], bank[:], ACT.Copy, scale=(EB ** -0.5, 1.0)[i]).then_inc(qkh_done, 1)
                if (s, k) == V_GAP:
                    act.wait_ge(vb_done, it)
                    act.activation(v_b[:, :, :, 0:EB], tb[:].rearrange("p (b h d) -> p b h d", b=NB, h=HEADS),
                                   ACT.Copy).then_inc(vals_done, 1)
                if (s, k) in STACK_GAPS:
                    n = STACK_GAPS.index((s, k))
                    act.wait_ge(stk_done, (it - 1) * 8 + 2 * n + 1)
                    act.activation((k_stk, q_stk)[n // 2][:, 2 * n % 4, :], (psb, ob, tb)[2 * n % 3][:], ACT.Copy).then_inc(stk_act, 1)

            def unit_b(it, s, k):
                w = b_slot(s, k)
                if w is None:
                    return
                if w < STEPS:
                    act.wait_ge(maxb_done, (it - 1) * STEPS + w + 1)
                    if (n_due := due(it - 1, STEPS, w - 1)) is not None:
                        act.wait_ge(tb_done, n_due)
                    for h in range(Q4):
                        a = act.activation(p_b[:, w % 2, h, :], (psb, sa)[b_bank(w, not live(it))][:, tok(h)], ACT.Exp, bias=nmax_b[:, w % 2, h:h + 1])
                    a.then_inc(expb_done, 1)

            def last_outputs_b(it, s, k):
                if (s, k) == LAST_T_GAP:
                    act.wait_ge(last_t_done, it)
                    act.activation(ot_b[:], tb[:, 0:2 * P].rearrange("p (i q) -> p i q", i=2), ACT.Copy).then_inc(last_ot, 1)

            def start_m(it, s, k):
                hm_f, hm_hi = m_tiles(next_it(it))[:2]
                if (s, k) == HMT_GAP:
                    act.wait_ge(hmt_done, it)
                    act.activation(hm_f[:], tb[:], ACT.Identity, bias=ln_sb[:, 3:4], scale=ln_sb[:, 2:3]).then_inc(hmf_done, 1)
                    act.wait_ge(hmf_done, it)
                    act.activation(hm_hi[:], hm_f[:], ACT.Copy).then_inc(hmh_done, 1)
                if (s, k) == EE_GAP:
                    act.wait_ge(dd_done, it)
                    act.activation(ee[:], dd[:], ACT.Exp).then_inc(ee_done, 1)

            def expert_m(it, j):
                th_m = m_tiles(it)[3]
                act.wait_ge(ma_done, (it - 2) * CHUNKS + j + 1)
                if j >= 2:
                    if (n_due := due(it - 2, CHUNKS, j - 1)) is not None:
                        act.wait_ge(u_done, n_due)
                act.activation(th_m[:, j % 2, :], m_banks(it, j)[0][:], ACT.Tanh, scale=0.5).then_inc(th_done, 1)

            def weigh_m(it, e):
                act.wait_ge(dn_done, (it - 2) * EXPERTS + e + 1)
                if e == 0:
                    act.wait_ge(route, (it - 2) * ROUTE + ROUTE)
                elif e > 1:
                    if (n_due := due(it - 2, EXPERTS, e - 1)) is not None:
                        act.wait_ge(comb_done, n_due)
                for b in range(NB):
                    a = act.activation(m_tiles(it)[6][:, e % 2, b, :], m_banks(it, e)[2][:, tok(b)], ACT.Copy,
                                       scale=wts[:, b, e:e + 1])
                a.then_inc(eo_done, 1)

            def gap(it, s, k):
                if k:
                    m_gap(it, s, k, expert_m, weigh_m)
                if live(it, -1):
                    project_b(it, s, k)
                    unit_b(it, s, k)
                    last_outputs_b(it, s, k)
                    start_m(it, s, k)

            def body(it):
                for s in range(STEPS):
                    m_gap(it, s, 0, expert_m, weigh_m)
                    copy_at = PT_COPY[s] if live(it, -1) else -1
                    if copy_at == -1 and live(it, 0 if s else -1):
                        pt_copy_a(it if s else it - 1, (s - 1) % STEPS)
                    if live(it):
                        exp_a(it, s)
                    for k in range(6):
                        if k == copy_at and live(it, 0 if s else -1):
                            pt_copy_a(it if s else it - 1, (s - 1) % STEPS)
                        if k == KEYS[s] and live(it, 0 if s < 12 else 1):
                            keys_hi_a(it, s)
                        if k == FIRST_USE[s]:
                            first_use(it, s)
                        if k == 5:
                            second_use(it, s)
                        gap(it, s, k)
                    if isinstance(it, int) and it == -1 and 8 <= s < 12:
                        products_hi(s - 8)
                    if isinstance(it, int) and it == -1 and s == 13:
                        act.activation(wv_hi[:], wv_in[:], ACT.Copy).then_inc(wvh_done, 1)
                    if isinstance(it, int) and it == 0 and s == 8:
                        act.wait_ge(w_small_in, 16 * 12)
                        act.activation(qkw_hi[:], qkw_in[:], ACT.Copy).then_inc(qkwh_done, 1)

            iterations(act, body)

        @block.vector
        def _(dve):
            dve.memset(v_a[:, :, :, DH:DH + 1], 1.0).then_inc(ones_done, 1)
            dve.memset(v_b[:, :, :, EB:EB + 1], 1.0).then_inc(ones_done, 1)
            dve.wait_ge(wt_done, 1)
            for i, bank in enumerate((ga, oa)):
                dve.tensor_copy(wkt[:, 4 * i:4 * i + 4, :],
                                bank[:, 0:4 * DE].rearrange("p (t c) -> p t c", t=4)).then_inc(wkt_done, 1)

            def products_lo(i):
                h0 = 8 * (i // 2) + i % 2
                dve.wait_ge(mth_done, i + 1)
                dve.scalar_tensor_tensor(out=mt_lo[:, h0:h0 + 7:2, :],
                                         in0=(psb, tb, ob, sa)[i][0:DE, :].rearrange("p (t c) -> p t c", t=4),
                                         scalar=DH ** -0.5, in1=f32(mt_hi[:, h0:h0 + 7:2, :]),
                                         op0=ALU.mult, op1=ALU.subtract).then_inc(mtl_done, 1)

            def max_a(it, u):
                dve.wait_ge(sa_done, it * STEPS + u + 1)
                dve.tensor_reduce(nmax_a[:, u % 2, :], sa[:].rearrange("q (h k) -> q h k", h=Q4), AX, ALU.max,
                                  negate=True).then_inc(maxa_done, 1)

            def keys_lo_a(it, s):
                j = (s + Q4) % HEADS
                dve.wait_ge(gh_done, it * HEADS + s + Q4 + 1)
                dve.tensor_tensor(g_lo[:, j // Q4 % 2, j % Q4, :], ga[:], f32(g_hi[:, j // Q4 % 2, j % Q4, :]),
                                  ALU.subtract).then_inc(gl_done, 1)

            def normalise_a(it, u):
                dve.wait_ge(oa_done, it * STEPS + u + 1)
                o = oa[:, 0:Q4 * (DH + 1)].rearrange("q (h d) -> q h d", h=Q4)
                dve.reciprocal(rden_a[:, u % 2, :], o[:, :, DH]).then_inc(rdena_done, 1)
                dve.wait_ge(rdena_done, it * STEPS + u + 1)
                dve.tensor_tensor(o_a[:, u % 2, :].rearrange("q (h d) -> q h d", h=Q4), o[:, :, 0:DH],
                                  rden_a[:, u % 2, :].unsqueeze(2).to_broadcast([P, Q4, DH]),
                                  ALU.mult).then_inc(oa_norm, 1)

            def norm_stats(it, i, b, src):
                dve.bn_stats(st_b[:, b, :], src).then_inc(st_done[i], 1)
                dve.wait_ge(st_done[i], it * NB + b + 1)
                dve.nop(nofuse=True)
                dve.bn_aggr(mv_b[:, i, b, :], st_b[:, b, :]).then_inc(mv_done[i], 1)

            def norm_apply(it, i, b, dst, src):
                dve.wait_ge(rs_done[i], it * NB + b + 1)
                return dve.tensor_scalar(dst, src, mv_b[:, i, b, 0:1], rs_b[:, i, b:b + 1], ALU.subtract, ALU.mult)

            def add_output(it, b, attn):
                dve.wait_ge(sum_done, (it - 1) * NB + b + 1)
                if (n_due := due(it - 1, 16, 0)) is not None:
                    dve.wait_ge(out_stored, n_due)
                dve.tensor_tensor(yb_res[:, b, :], attn, yb_res[:, b, :], ALU.add).then_inc(y1_done, 1)
                return dve.tensor_tensor(acc[:, b, :], attn, xy_sum[:, b, :], ALU.add)

            def last_outputs_b(it, s, k):
                if (s, k) == LAST_W_GAP:
                    dve.wait_ge(last_w_done, it)
                    for i in range(2):
                        add_output(it, 2 + i, psb[:, tok(i)])

            def second_use(it, s):
                if dve_use2(it, s):
                    if (n_due := uses(use2, it, s)) is not None:
                        dve.wait_ge(x2_done, n_due)
                    if act_use2(it, s):
                        if (n_due := uses(both_use2, it, s)) is not None:
                            dve.wait_ge(x2_act, n_due)
                    d = None
                    if 8 <= s < 12 and live(it, 1):
                        d = dve.tensor_tensor(ctxn_lo[:, tok(s - 8)], px[0:DE, tok(1)], f32(ctxn_hi[:, tok(s - 8)]),
                                              ALU.subtract)
                    if s >= 12 and live(it, 1):
                        d = dve.tensor_tensor(hat_lo[:, s - 12, :], px[:, tok(1)], f32(hat_hi[:, s - 12, :]), ALU.subtract)
                    if live(it, -1):
                        for i, b in enumerate(B_OUT_W.get(s, ())):
                            d = add_output(it, b, px[:, tok(2 + i)])
                    if wo_a(it, s):
                        g, u = (it, s - 2) if s >= 2 else (it - 1, s + 14)
                        b = u % NB
                        dve.wait_ge(xres_set, g * NB + b + 1)
                        d = dve.tensor_tensor(x_res[:, b, :], px[:, tok(0)], x_res[:, b, :], ALU.add)
                    d.then_inc(x2_free, 1)

            def norms_early(it, s):
                if live(it, -1):
                    for b in B_NORMS.get(s, ()):
                        dve.wait_ge(y1_done, (it - 1) * NB + b + 1)
                        norm_stats(it - 1, 2, b, yb_res[:, b, :])
                g, b = (it, 0) if s == 15 else (it - 1, s + 1)
                if (s == 15 or s < 3) and live(g):
                    if (n_due := uses(use2, it, s - 1)) is not None:
                        dve.wait_ge(x2_free, n_due)
                    norm_stats(g, 0, b, x_res[:, b, :])
                if s < 4 and live(it, -1):
                    norm_apply(it - 1, 1, s, nrm[:, s, :], y_b[:, s % 2, :]).then_inc(nb_done, 1)

            def norms_late(it, s):
                if live(it, -1):
                    for b in B_NORMS.get(s, ()):
                        norm_apply(it - 1, 2, b, nrm[:, b, :], yb_res[:, b, :]).then_inc(nm_done, 1)
                g, b = (it, 0) if s == 15 else (it - 1, s + 1)
                if (s == 15 or s < 3) and live(g):
                    if (n_due := due(g, NB, b - 1)) is not None:
                        dve.wait_ge(nb_done, n_due)
                    if (n_due := due(g, NB, b - 1)) is not None:
                        dve.wait_ge(ybo_done, n_due)
                    norm_apply(g, 0, b, y_b[:, b % 2, :], x_res[:, b, :]).then_inc(y_done, 1)
                    dve.wait_ge(y_done, g * NB + b + 1)
                    norm_stats(g, 1, b, y_b[:, b % 2, :])

            def norm_next_a(it, s):
                if not live(it, 1):
                    return
                if s == 9:
                    dve.wait_ge(x_landed, (it + 1) * 16 + 16)
                    for b in range(NB):
                        dve.bn_stats(st_a[:, b, :], x_in[:, b, :]).then_inc(sta_done, 1)
                    dve.wait_ge(sta_done, (it + 1) * NB + NB)
                    dve.nop(nofuse=True)
                    for b in range(NB):
                        dve.bn_aggr(mv_a[:, b, :], st_a[:, b, :]).then_inc(mva_done, 1)
                if 11 <= s < 15:
                    b = s - 11
                    dve.wait_ge(rsa_done, it + 2)
                    dve.tensor_scalar(ha[:, b % 2, :], x_in[:, b, :], mv_a[:, b, 0:1], rs_a[:, b:b + 1],
                                      ALU.subtract, ALU.mult).then_inc(ha_done, 1)

            def project_b(it, s, k):
                if (s, k) == HBT_GAP:
                    dve.wait_ge(hbh_done, it)
                    dve.tensor_tensor(hb_lo[:], hb_f[:], f32(hb_hi[:]), ALU.subtract).then_inc(hbl_done, 1)
                if (s, k) == QK_GAP:
                    for i, bank in enumerate((psb, ob)):
                        if not spread(it):
                            if (n_due := due(it - 1, EXPERTS, i - 1)) is not None:
                                dve.wait_ge(comb_done, n_due)
                        dve.wait_ge(qkh_done, (it - 1) * 2 + i + 1)
                        dve.scalar_tensor_tensor(out=qk_lo[:, i, :], in0=bank[:], scalar=(EB ** -0.5, 1.0)[i],
                                                 in1=f32(qk_hi[:, i, :]), op0=ALU.mult, op1=ALU.subtract).then_inc(qkl_done, 1)
                if (s, k) in STACK_GAPS:
                    n = STACK_GAPS.index((s, k))
                    dve.wait_ge(stk_done, (it - 1) * 8 + 2 * n + 2)
                    dve.tensor_copy((k_stk, q_stk)[n // 2][:, 2 * n % 4 + 1, :], (psb, ob, tb)[(2 * n + 1) % 3][:]).then_inc(stk_dve, 1)
            def unit_b(it, s, k):
                w = b_slot(s, k)
                if w is None:
                    return
                if w < STEPS:
                    dve.wait_ge(sb_done, (it - 1) * STEPS + w + 1)
                    dve.tensor_reduce(nmax_b[:, w % 2, :], (psb, sa)[b_bank(w, not live(it))][:].rearrange("q (h k) -> q h k", h=Q4), AX, ALU.max,
                                      negate=True).then_inc(maxb_done, 1)
                if 2 <= w <= STEPS + 1:
                    if (n_due := due(it - 1, STEPS, w - 1)) is not None:
                        dve.wait_ge(tb_done, n_due)
                    if (n_due := due(it - 1, STEPS, w - 2)) is not None:
                        dve.wait_ge(ob_done, n_due)
                    dve.tensor_copy(pt_b[:], tb[:].rearrange("p (h q) -> p h q", h=Q4)).then_inc(ptb_done, 1)
                if w >= 3 and (w - 3) % Q4 == Q4 - 1:
                    b = (w - 3) // Q4
                    if (n_due := due(it - 1, STEPS, w - 2)) is not None:
                        dve.wait_ge(ob_done, n_due)
                    o = ob[:, 0:(EB + 1) * HEADS].rearrange("q (h c) -> q h c", h=HEADS)
                    dve.reciprocal(rden_b[:], o[:, :, EB]).then_inc(rdenb_done, 1)
                    dve.wait_ge(rdenb_done, (it - 1) * NB + b + 1)
                    dve.tensor_tensor(o_b[:, b % 2, :].rearrange("q (h d) -> q h d", h=HEADS), o[:, :, 0:EB],
                                      rden_b[:].unsqueeze(2).to_broadcast([P, HEADS, EB]), ALU.mult).then_inc(ob_norm, 1)

            def start_m(it, s, k):
                hm_f, hm_hi, hm_lo = m_tiles(next_it(it))[:3]
                if (s, k) == HMT_GAP:
                    dve.wait_ge(hmh_done, it)
                    dve.tensor_tensor(hm_lo[:], hm_f[:], f32(hm_hi[:]), ALU.subtract).then_inc(hml_done, 1)
                if (s, k) == GATE_GAP:
                    dve.wait_ge(gate_done, it)
                    dve.tensor_copy(sc_m[:], ob[:, 0:NB * EXPERTS].rearrange("q (b e) -> q b e", b=NB)).then_inc(sc_done, 1)
                    dve.wait_ge(sc_done, it)
                    dve.nop(nofuse=True)
                    for b in range(NB):
                        d = dve.max(m8[:, b, :], sc_m[:, b, :])
                    d.then_inc(route, 1)
                    dve.wait_ge(route, (it - 1) * ROUTE + 1)
                    dve.tensor_tensor(dd[:], m8[:, :, 1], m8[:, :, 0], ALU.subtract).then_inc(dd_done, 1)
                    for b in range(NB):
                        d = dve.max_index(i8[:, b, :], m8[:, b, :], sc_m[:, b, :])
                    d.then_inc(route, 1)
                    dve.wait_ge(route, (it - 1) * ROUTE + 2)
                    dve.tensor_copy(if_m[:], i8[:, :, 0:2]).then_inc(route, 1)
                    dve.wait_ge(route, (it - 1) * ROUTE + 3)
                    for i in range(2):
                        dve.tensor_tensor(eq[:, i], iota8[:].unsqueeze(1).to_broadcast([P, NB, EXPERTS]),
                                          if_m[:, :, i:i + 1].to_broadcast([P, NB, EXPERTS]), ALU.is_equal).then_inc(route, 1)

            def probs_m(it, s, k):
                if (s, k) == PROBS_GAP:
                    dve.wait_ge(ee_done, it)
                    dve.tensor_scalar(zz[:], ee[:], 1.0, None, ALU.add).then_inc(route, 1)
                    dve.wait_ge(route, (it - 1) * ROUTE + 6)
                    dve.reciprocal(rr[:], zz[:]).then_inc(route, 1)
                    dve.wait_ge(route, (it - 1) * ROUTE + 7)
                    dve.tensor_scalar(pp[:, 0, :], rr[:], 0.5, None, ALU.mult)
                    dve.scalar_tensor_tensor(out=pp[:, 1, :], in0=rr[:], scalar=0.5, in1=ee[:], op0=ALU.mult,
                                             op1=ALU.mult).then_inc(route, 1)
                    dve.wait_ge(route, (it - 1) * ROUTE + 8)
                    for i in range(2):
                        d = dve.tensor_tensor(eq[:, i], eq[:, i], pp[:, i, :].unsqueeze(2).to_broadcast([P, NB, EXPERTS]), ALU.mult)
                    d.then_inc(route, 1)
                    dve.wait_ge(route, (it - 1) * ROUTE + 9)
                    dve.tensor_tensor(wts[:], eq[:, 0], eq[:, 1], ALU.add).then_inc(route, 1)

            def expert_m(it, j):
                th_m, u_m, g_t = m_tiles(it)[3:6]
                w1_bank, w2_bank, _ = m_banks(it, j)
                dve.wait_ge(th_done, (it - 2) * CHUNKS + j + 1)
                if j:
                    if (n_due := due(it - 2, CHUNKS, j)) is not None:
                        dve.wait_ge(g_done, n_due)
                dve.scalar_tensor_tensor(out=u_m[:], in0=th_m[:, j % 2, :], scalar=1.0, in1=w1_bank[:], op0=ALU.add,
                                         op1=ALU.mult).then_inc(u_done, 1)
                dve.wait_ge(u_done, (it - 2) * CHUNKS + j + 1)
                dve.wait_ge(mb_done, (it - 2) * CHUNKS + j + 1)
                if j >= 4:
                    if (n_due := due(it - 2, EXPERTS, j // 2 - 1)) is not None:
                        dve.wait_ge(dn_done, n_due)
                dve.tensor_tensor(g_t[:, j % 4, :], w2_bank[:], u_m[:], ALU.mult).then_inc(g_done, 1)

            def gap(it, s, k):
                m_gap(it, s, k, expert_m, lambda it, e: None)
                if live(it, -1):
                    project_b(it, s, k)
                    unit_b(it, s, k)
                    last_outputs_b(it, s, k)
                    start_m(it, s, k)
                    probs_m(it, s, k)

            def body(it):
                for s in range(STEPS):
                    if live(it):
                        max_a(it, s)
                    for k in range(6):
                        if k == NORMS_EARLY[s]:
                            norms_early(it, s)
                        if k == KEYS_LO[s] and live(it, 0 if s < 12 else 1):
                            keys_lo_a(it, s)
                        if k == NORMS_LATE[s]:
                            norms_late(it, s)
                        if k == NORMS_NEXT[s]:
                            norm_next_a(it, s)
                        if k == NORMALISE[s] and live(it, 0 if s else -1):
                            normalise_a(it if s else it - 1, (s - 1) % STEPS)
                        if k == 5:
                            second_use(it, s)
                        gap(it, s, k)
                    if isinstance(it, int) and it == -1 and 8 <= s < 12:
                        products_lo(s - 8)
                    if isinstance(it, int) and it == -1 and s == 13:
                        dve.wait_ge(wvh_done, 1)
                        dve.tensor_tensor(wv_lo[:], wv_in[:], f32(wv_hi[:]), ALU.subtract).then_inc(wvl_done, 1)
                    if isinstance(it, int) and it == 0 and s == 8:
                        dve.wait_ge(qkwh_done, 1)
                        dve.tensor_tensor(qkw_lo[:], qkw_in[:], f32(qkw_hi[:]), ALU.subtract).then_inc(qkwl_done, 1)

            iterations(dve, body)

        @block.gpsimd
        def _(pool):
            pool.memset(ident[:], 0.0)
            pool.memset(ident_b[:], 0.0)
            pool.memset(mask[:], 0.0)
            pool.memset(half[:], -0.5)
            pool.memset(eps[:], EPS)
            pool.memset(sel_tmp[:], 0.0).then_inc(const_made, 1)
            pool.wait_ge(const_made, 1)
            pool.affine_select(out=ident[:], in_=ident[:], compare_op=ALU.not_equal, fill=1.0, base=0,
                               pattern=[[-1, P]], channel_multiplier=1).then_inc(const_made, 1)
            pool.affine_select(out=ident_b[:], in_=ident_b[:], compare_op=ALU.not_equal, fill=1.0, base=0,
                               pattern=[[-1, P]], channel_multiplier=1)
            pool.affine_select(out=mask[:], in_=mask[:], compare_op=ALU.is_ge, fill=MASKED, base=0,
                               pattern=[[0, Q4], [-1, P]], channel_multiplier=1)
            pool.iota(iota8[:], pattern=[[1, EXPERTS]], base=0, channel_multiplier=0,
                      allow_small_or_imprecise_dtypes=True)
            body_cols = sel_tmp[:, 16:].rearrange("p (h c d) -> p h c d", h=HEADS, c=4)
            for sel, n, picks in ((sel_q, 0, (0, 1)), (sel_k, 1, (0, 2))):
                if n:
                    pool.wait_ge(sel_made, 1)
                    pool.memset(sel_tmp[:], 0.0).then_inc(const_made, 1)
                    pool.wait_ge(const_made, 5)
                for c in picks:
                    d = pool.affine_select(out=body_cols[:, :, c, :], in_=body_cols[:, :, c, :], compare_op=ALU.not_equal,
                                           fill=1.0, base=0, pattern=[[-8, HEADS], [-1, 8]], channel_multiplier=1)
                    d.then_inc(const_made, 1)
                pool.wait_ge(const_made, (4, 7)[n])
                pool.tensor_copy(sel[:], sel_tmp[:]).then_inc(sel_made, 1)
            def split_moe():
                pool.wait_ge(w_moe_in, 32)
                for i, hi in enumerate((w1_hi, w2_hi)):
                    pool.tensor_copy(hi[:], moe_in[:, i, :]).then_inc(moew_done, 1)
                for i, (hi, lo) in enumerate(((w1_hi, w1_lo), (w2_hi, w2_lo))):
                    pool.wait_ge(moew_done, i + 1)
                    pool.tensor_tensor(lo[:], moe_in[:, i, :], f32(hi[:]), ALU.subtract).then_inc(moew_done, 1)
                pool.wait_ge(moew_done, 4)
                pool.memset(f32(k_diag[:]), 0.0).then_inc(moew_done, 1)

            def root(g, i, b):
                pool.wait_ge(mv_done[i], g * NB + b + 1)
                pool.tensor_tensor(ve_b[:, i, b:b + 1], mv_b[:, i, b, 1:2], eps[:], ALU.add).then_inc(ve_done[i], 1)
                pool.wait_ge(ve_done[i], g * NB + b + 1)
                pool.tensor_tensor(rs_b[:, i, b:b + 1], ve_b[:, i, b:b + 1], half[:], ALU.pow).then_inc(rs_done[i], 1)

            def combine_m(it, e):
                if e == 0:
                    pool.wait_ge(route, (it - 2) * ROUTE + ROUTE)
                else:
                    pool.wait_ge(comb_done, (it - 2) * EXPERTS + e)
                pool.wait_ge(eo_done, (it - 2) * EXPERTS + e + 1)
                pool.tensor_tensor(acc[:], acc[:], m_tiles(it)[6][:, e % 2], ALU.add).then_inc(comb_done, 1)

            def body(it):
                for s in range(STEPS):
                    if live(it, -1):
                        for bb in B_NORMS.get(s, ()):
                            root(it - 1, 2, bb)
                    g, b = (it, 0) if s == 15 else (it - 1, s + 1)
                    if (s == 15 or s < 3) and live(g):
                        root(g, 0, b)
                        root(g, 1, b)
                        if (n_due := due(g - 1, NB, b + 1)) is not None:
                            pool.wait_ge(nm_done, n_due)
                        pool.tensor_tensor(yb_res[:, b, :], y_b[:, b % 2, :], bo_b_sb[:], ALU.add).then_inc(ybo_done, 1)
                        pool.wait_ge(ybo_done, g * NB + b + 1)
                        pool.tensor_tensor(xy_sum[:, b, :], yb_res[:, b, :], x_res[:, b, :], ALU.add).then_inc(sum_done, 1)
                    if s < 4 and live(it):
                        if s == 0 and isinstance(it, int) and it == 0:
                            pool.wait_ge(w_small_in, 16 * 12)
                        pool.wait_ge(x_landed, it * 16 + 16)
                        if live(it, -1):
                            pool.wait_ge(sum_done, (it - 1) * NB + s + 1)
                        pool.tensor_tensor(x_res[:, s, :], x_in[:, s, :], bo_a_sb[:], ALU.add).then_inc(xres_set, 1)
                    if s == 4 and isinstance(it, int) and it == 0:
                        split_moe()
                    if s == 9 and live(it, 1):
                        pool.wait_ge(mva_done, (it + 1) * NB + NB)
                        pool.tensor_tensor(ve_a[:], mv_a[:, :, 1], eps[:].to_broadcast([P, NB]), ALU.add).then_inc(vea_done, 1)
                        pool.wait_ge(vea_done, it + 2)
                        pool.tensor_tensor(rs_a[:], ve_a[:], half[:].to_broadcast([P, NB]), ALU.pow).then_inc(rsa_done, 1)
                    if s == 15 and live(it, 1):
                        if (n_due := uses(use1, it, 14)) is not None:
                            pool.wait_ge(x1_done, n_due)
                        if (n_due := uses(use2, it, 11)) is not None:
                            pool.wait_ge(x2_free, n_due)
                        pool.nop(nofuse=True)
                        for dst, src in ((ctxc_hi, ctxn_hi), (ctxc_lo, ctxn_lo)):
                            pool.tensor_copy(dst[:], src[:]).then_inc(ctxc_done, 1)
                    for k in range(6):
                        m_gap(it, s, k, lambda it, j: None, combine_m)

            iterations(pool, body)


_INS = ("x", "ctx_768", "L0_xattn_Wq", "L0_xattn_Wk", "L0_xattn_Wv", "L0_xattn_Wo", "L0_xattn_bo", "L0_ffn_ln1_scale",
        "L0_ffn_ln1_shift", "L0_ffn_wq", "L0_ffn_wk", "L0_ffn_wv", "L0_ffn_wo", "L0_ffn_bo", "L0_ffn_ln2_scale",
        "L0_ffn_ln2_shift", "L0_ffn_gate_w", "L0_ffn_w1", "L0_ffn_w2", "L0_ffn_w3")


def kernel(**inputs):
    import numpy as np
    import concourse.bacc as bacc
    from concourse.bass_utils import run_bass_kernel_spmd

    nc = bacc.Bacc("TRN2", target_bir_lowering=False, num_devices=1)
    arrays, args = {}, []
    for name in _INS:
        a = np.ascontiguousarray(inputs[name])
        arrays[f"in_{name}"] = a
        args.append(nc.dram_tensor(f"in_{name}", a.shape, mybir.dt.from_np(a.dtype), kind="ExternalInput").ap())
    shape = inputs["x"].shape
    out = nc.dram_tensor("out_0", shape, F32, kind="ExternalOutput").ap()
    build(nc, shape[0] // NB, *args, out)
    r = run_bass_kernel_spmd(nc, [arrays], core_ids=[0])
    return r.results[0]["out_0"]
```
